# Optimizing a Trainium2 kernel written in Bass

```python
import numpy as np
import jax
import jax.numpy as jnp

def _softmax(x, axis=-1):
    return jax.nn.softmax(x, axis=axis)

def _gelu(x):
    return jax.nn.gelu(x, approximate=True)

def _silu(x):
    return jax.nn.silu(x)

def _sigmoid(x):
    return jax.nn.sigmoid(x)

def _layernorm(x, axis=-1, eps=1e-05):
    m = jnp.mean(x, axis=axis, keepdims=True)
    v = jnp.var(x, axis=axis, keepdims=True)
    return (x - m) / jnp.sqrt(v + eps)

def _scatter_add(tgt, idx, src, axis=0):
    return tgt.at[idx].add(src)

def _segment_sum(src, seg, n):
    return jax.ops.segment_sum(src, seg, n)
kernel_name = 'mk_early_fusion_d2_tok_img768_r4_ddf3ce'

def setup_inputs(seed: int=0):
    np.random.seed(seed)
    _w = jnp.asarray

    def _rec_inputs():
        import jax
        import jax.numpy as jnp
        _rk = jax.random.key(seed)
        x = 7.57192e-06 + 1.00007 * jax.random.normal(jax.random.fold_in(_rk, 1), (16, 64, 64, 3), jnp.float32)
        txt = -0.0429142 + 10 * jax.random.normal(jax.random.fold_in(_rk, 2), (16, 128, 192), jnp.float32)
        return (x, txt)
    x, txt = _rec_inputs()

    def _L0_tok_setup():
        import jax, jax.numpy as jnp
        import numpy as np
        PATCH = 16
        DIM = 192
        EPS = 0.001

        def _shifts(x):
            zw = jnp.zeros_like(x[:, :, :1, :])
            right = jnp.concatenate([zw, x[:, :, :-1, :]], axis=2)
            left = jnp.concatenate([x[:, :, 1:, :], zw], axis=2)
            zh = jnp.zeros_like(x[:, :1, :, :])
            down = jnp.concatenate([zh, x[:, :-1, :, :]], axis=1)
            up = jnp.concatenate([x[:, 1:, :, :], zh], axis=1)
            return [right, left, down, up]

        def _patchify(x, p):
            b, H, W, C = x.shape
            hh, ww = (H // p, W // p)
            x = x.reshape(b, hh, p, ww, p, C)
            x = x.transpose(0, 1, 3, 2, 4, 5)
            return x.reshape(b, hh * ww, p * p * C)
        key = jax.random.key(seed)
        k1, k2 = jax.random.split(key)
        b, H, Wd, C = (64, 224, 224, 3)
        F = PATCH * PATCH * 5 * C
        x = jax.random.normal(k1, (b, H, Wd, C), dtype=jnp.float32)
        gamma = jnp.ones((F,), dtype=jnp.float32)
        beta = jnp.zeros((F,), dtype=jnp.float32)
        W = jax.random.normal(k2, (F, DIM), dtype=jnp.float32)
        bb = jnp.zeros((DIM,), dtype=jnp.float32)
        return {'x': x, 'gamma': gamma, 'beta': beta, 'W': W, 'b': bb}
    _L0_tok_all = _L0_tok_setup()
    _L0_tok_in = {k: v for k, v in _L0_tok_all.items() if k in ('gamma', 'beta', 'W', 'b')}
    del _L0_tok_all

    def _L0_attn_setup():
        import jax, jax.numpy as jnp
        import numpy as np
        import math
        N_HEAD = 12
        key = jax.random.key(seed)
        k1, k2, k3, k4, k5 = jax.random.split(key, 5)
        B, T, C = (4, 512, 192)
        s_in = 1.0 / math.sqrt(C)
        x = jax.random.normal(k1, (B, T, C), dtype=jnp.float32)
        w_attn = jax.random.normal(k2, (3 * C, C), dtype=jnp.float32) * s_in
        b_attn = jnp.zeros((3 * C,), dtype=jnp.float32)
        w_proj = jax.random.normal(k3, (C, C), dtype=jnp.float32) * s_in
        b_proj = jnp.zeros((C,), dtype=jnp.float32)
        return {'x': x, 'w_attn': w_attn, 'b_attn': b_attn, 'w_proj': w_proj, 'b_proj': b_proj}
    _L0_attn_all = _L0_attn_setup()
    _L0_attn_in = {k: v for k, v in _L0_attn_all.items() if k in ('w_attn', 'b_attn', 'w_proj', 'b_proj')}
    del _L0_attn_all

    def _L0_ffn_setup():
        import jax, jax.numpy as jnp
        import numpy as np
        B_SZ, S, D = (8, 128, 192)
        H = 12
        N_EXP = 8
        RANK = 16
        ALPHA = 32
        TOP_K = 2
        key = jax.random.key(seed)
        ks = jax.random.split(key, 9)
        x = jax.random.normal(ks[0], (B_SZ, S, D), jnp.float32)
        W_qkv = jax.random.normal(ks[1], (3 * D, D), jnp.float32) * 0.02
        b_qkv = jnp.zeros((3 * D,), jnp.float32)
        W_gate = jax.random.normal(ks[2], (N_EXP, D), jnp.float32) * 0.02
        b_gate = jnp.zeros((N_EXP,), jnp.float32)
        A = jax.random.normal(ks[3], (N_EXP, RANK, D), jnp.float32) * 0.02
        B_lora = jax.random.normal(ks[4], (N_EXP, 3 * D, RANK), jnp.float32) * 0.02
        W_proj = jax.random.normal(ks[5], (D, D), jnp.float32) * 0.02
        b_proj = jnp.zeros((D,), jnp.float32)
        return {'x': x, 'W_qkv': W_qkv, 'b_qkv': b_qkv, 'W_gate': W_gate, 'b_gate': b_gate, 'A': A, 'B_lora': B_lora, 'W_proj': W_proj, 'b_proj': b_proj}
    _L0_ffn_all = _L0_ffn_setup()
    _L0_ffn_in = {k: v for k, v in _L0_ffn_all.items() if k in ('W_qkv', 'b_qkv', 'W_gate', 'b_gate', 'A', 'B_lora', 'W_proj', 'b_proj')}
    del _L0_ffn_all

    def _L1_attn_setup():
        import jax, jax.numpy as jnp
        import numpy as np
        import math
        N_HEAD = 12
        N_EMBD = 192
        HEAD_DIM = N_EMBD // N_HEAD // 2
        DEPTH = 12
        LAMBDA_INIT = 0.8 - 0.6 * math.exp(-0.3 * DEPTH)

        def _sdpa_over_heads(q, k, v):
            scale = 1.0 / math.sqrt(q.shape[-1])
            s = jnp.einsum('bnqd,bnkd->bnqk', q, k) * scale
            a = jax.nn.softmax(s, axis=-1)
            return jnp.einsum('bnqk,bnkd->bnqd', a, v)
        key = jax.random.key(seed)
        ks = jax.random.split(key, 7)
        B, N, D = (4, 2048, N_EMBD)
        s = 0.02
        return {'x': jax.random.normal(ks[0], (B, N, D), dtype=jnp.float32), 'W_attn': jax.random.normal(ks[1], (3 * D, D), dtype=jnp.float32) * s, 'W_out': jax.random.normal(ks[2], (D, D), dtype=jnp.float32) * s, 'lambda_q1': jax.random.normal(ks[3], (HEAD_DIM,), dtype=jnp.float32) * 0.1, 'lambda_k1': jax.random.normal(ks[4], (HEAD_DIM,), dtype=jnp.float32) * 0.1, 'lambda_q2': jax.random.normal(ks[5], (HEAD_DIM,), dtype=jnp.float32) * 0.1, 'lambda_k2': jax.random.normal(ks[6], (HEAD_DIM,), dtype=jnp.float32) * 0.1}
    _L1_attn_all = _L1_attn_setup()
    _L1_attn_in = {k: v for k, v in _L1_attn_all.items() if k in ('W_attn', 'W_out', 'lambda_q1', 'lambda_k1', 'lambda_q2', 'lambda_k2')}
    del _L1_attn_all

    def _L1_ffn_setup():
        import jax, jax.numpy as jnp
        import numpy as np
        B, S, D = (2, 512, 192)
        E, K, F = (8, 2, 384)

        def _swiglu(xf, wg, wu, wd):
            return jax.nn.silu(xf @ wg.T) * (xf @ wu.T) @ wd.T
        key = jax.random.key(seed)
        ks = jax.random.split(key, 9)
        scale = 0.02
        x = jax.random.normal(ks[0], (B, S, D), dtype=jnp.float32)
        w_router = jax.random.normal(ks[1], (E, D), dtype=jnp.float32) * scale
        expert_bias = jnp.zeros((E,), dtype=jnp.float32)
        Wg = jax.random.normal(ks[2], (E, F, D), dtype=jnp.float32) * scale
        Wu = jax.random.normal(ks[3], (E, F, D), dtype=jnp.float32) * scale
        Wd = jax.random.normal(ks[4], (E, D, F), dtype=jnp.float32) * scale
        sg = jax.random.normal(ks[5], (F, D), dtype=jnp.float32) * scale
        su = jax.random.normal(ks[6], (F, D), dtype=jnp.float32) * scale
        sd = jax.random.normal(ks[7], (D, F), dtype=jnp.float32) * scale
        return {'x': x, 'w_router': w_router, 'expert_bias': expert_bias, 'Wg': Wg, 'Wu': Wu, 'Wd': Wd, 'sg': sg, 'su': su, 'sd': sd}
    _L1_ffn_all = _L1_ffn_setup()
    _L1_ffn_in = {k: v for k, v in _L1_ffn_all.items() if k in ('w_router', 'expert_bias', 'Wg', 'Wu', 'Wd', 'sg', 'su', 'sd')}
    del _L1_ffn_all
    return {'x': x, 'txt': txt, 'L0_tok_gamma': _L0_tok_in['gamma'], 'L0_tok_beta': _L0_tok_in['beta'], 'L0_tok_W': _L0_tok_in['W'], 'L0_tok_b': _L0_tok_in['b'], 'L0_attn_w_attn': _L0_attn_in['w_attn'], 'L0_attn_b_attn': _L0_attn_in['b_attn'], 'L0_attn_w_proj': _L0_attn_in['w_proj'], 'L0_attn_b_proj': _L0_attn_in['b_proj'], 'L0_ffn_W_qkv': _L0_ffn_in['W_qkv'], 'L0_ffn_b_qkv': _L0_ffn_in['b_qkv'], 'L0_ffn_W_gate': _L0_ffn_in['W_gate'], 'L0_ffn_b_gate': _L0_ffn_in['b_gate'], 'L0_ffn_A': _L0_ffn_in['A'], 'L0_ffn_B_lora': _L0_ffn_in['B_lora'], 'L0_ffn_W_proj': _L0_ffn_in['W_proj'], 'L0_ffn_b_proj': _L0_ffn_in['b_proj'], 'L1_attn_W_attn': _L1_attn_in['W_attn'], 'L1_attn_W_out': _L1_attn_in['W_out'], 'L1_attn_lambda_q1': _L1_attn_in['lambda_q1'], 'L1_attn_lambda_k1': _L1_attn_in['lambda_k1'], 'L1_attn_lambda_q2': _L1_attn_in['lambda_q2'], 'L1_attn_lambda_k2': _L1_attn_in['lambda_k2'], 'L1_ffn_w_router': _L1_ffn_in['w_router'], 'L1_ffn_expert_bias': _L1_ffn_in['expert_bias'], 'L1_ffn_Wg': _L1_ffn_in['Wg'], 'L1_ffn_Wu': _L1_ffn_in['Wu'], 'L1_ffn_Wd': _L1_ffn_in['Wd'], 'L1_ffn_sg': _L1_ffn_in['sg'], 'L1_ffn_su': _L1_ffn_in['su'], 'L1_ffn_sd': _L1_ffn_in['sd']}

def reference(x, txt, L0_tok_gamma, L0_tok_beta, L0_tok_W, L0_tok_b, L0_attn_w_attn, L0_attn_b_attn, L0_attn_w_proj, L0_attn_b_proj, L0_ffn_W_qkv, L0_ffn_b_qkv, L0_ffn_W_gate, L0_ffn_b_gate, L0_ffn_A, L0_ffn_B_lora, L0_ffn_W_proj, L0_ffn_b_proj, L1_attn_W_attn, L1_attn_W_out, L1_attn_lambda_q1, L1_attn_lambda_k1, L1_attn_lambda_q2, L1_attn_lambda_k2, L1_ffn_w_router, L1_ffn_expert_bias, L1_ffn_Wg, L1_ffn_Wu, L1_ffn_Wd, L1_ffn_sg, L1_ffn_su, L1_ffn_sd):
    import jax
    import jax.numpy as jnp

    def _L0_tok_ref(x, gamma, beta, W, b):
        import jax, jax.numpy as jnp
        import numpy as np
        PATCH = 16
        DIM = 192
        EPS = 0.001

        def _shifts(x):
            zw = jnp.zeros_like(x[:, :, :1, :])
            right = jnp.concatenate([zw, x[:, :, :-1, :]], axis=2)
            left = jnp.concatenate([x[:, :, 1:, :], zw], axis=2)
            zh = jnp.zeros_like(x[:, :1, :, :])
            down = jnp.concatenate([zh, x[:, :-1, :, :]], axis=1)
            up = jnp.concatenate([x[:, 1:, :, :], zh], axis=1)
            return [right, left, down, up]

        def _patchify(x, p):
            b, H, W, C = x.shape
            hh, ww = (H // p, W // p)
            x = x.reshape(b, hh, p, ww, p, C)
            x = x.transpose(0, 1, 3, 2, 4, 5)
            return x.reshape(b, hh * ww, p * p * C)
        x5 = jnp.concatenate([x] + _shifts(x), axis=-1)
        tokens = _patchify(x5, PATCH)
        mu = jnp.mean(tokens, axis=-1, keepdims=True)
        var = jnp.mean(jnp.square(tokens - mu), axis=-1, keepdims=True)
        ln = (tokens - mu) * jax.lax.rsqrt(var + EPS) * gamma + beta
        return jnp.einsum('bnf,fd->bnd', ln, W) + b

    def _L0_attn_ref(x, w_attn, b_attn, w_proj, b_proj):
        import jax, jax.numpy as jnp
        import numpy as np
        import math
        N_HEAD = 12
        B, T, C = x.shape
        H = N_HEAD
        D = C // H
        qkv = jnp.einsum('btc,oc->bto', x, w_attn) + b_attn
        k, q, v = jnp.split(qkv, 3, axis=-1)
        k = k.reshape(B, T, H, D).transpose(0, 2, 1, 3)
        q = q.reshape(B, T, H, D).transpose(0, 2, 1, 3)
        v = v.reshape(B, T, H, D).transpose(0, 2, 1, 3)
        scale = 1.0 / math.sqrt(D)
        scores = jnp.einsum('bhqd,bhkd->bhqk', q, k) * scale
        causal = jnp.tril(jnp.ones((T, T), dtype=bool))
        logits = jnp.where(causal, 2.0 * scores, -jnp.inf)
        attn = jax.nn.softmax(logits, axis=-1)
        y = jnp.einsum('bhqk,bhkd->bhqd', attn, v)
        y = y.transpose(0, 2, 1, 3).reshape(B, T, C)
        out = jnp.einsum('btc,oc->bto', y, w_proj) + b_proj
        return out

    def _L0_ffn_ref(x, W_qkv, b_qkv, W_gate, b_gate, A, B_lora, W_proj, b_proj):
        import jax, jax.numpy as jnp
        import numpy as np
        B_SZ, S, D = (8, 128, 192)
        H = 12
        N_EXP = 8
        RANK = 16
        ALPHA = 32
        TOP_K = 2
        b, s, d = x.shape
        n_exp, rank = (A.shape[0], A.shape[1])
        scaling = ALPHA / rank
        head_dim = d // H
        scale = head_dim ** (-0.5)
        t = b * s
        x_flat = x.reshape(t, d)
        qkv_base = x @ W_qkv.T + b_qkv
        logits = x_flat @ W_gate.T + b_gate
        router_probs = jax.nn.softmax(logits, axis=-1)
        top_k_weights, top_k_indices = jax.lax.top_k(router_probs, TOP_K)
        a_down = jnp.einsum('td,nrd->tnr', x_flat, A)
        expert_out = jnp.einsum('tnr,nor->tno', a_down, B_lora) * scaling
        dispatch = jnp.zeros((t, n_exp), x.dtype).at[jnp.arange(t)[:, None], top_k_indices].add(top_k_weights)
        sparse_out = jnp.einsum('tno,tn->to', expert_out, dispatch)
        qkv = qkv_base + sparse_out.reshape(b, s, 3 * d)
        qkv = qkv.reshape(b, s, 3, H, head_dim).transpose(2, 0, 3, 1, 4)
        q, k, v = (qkv[0], qkv[1], qkv[2])
        attn = jax.nn.softmax(jnp.einsum('bhqd,bhkd->bhqk', q, k) * scale, axis=-1)
        out = jnp.einsum('bhqk,bhkd->bhqd', attn, v)
        out = out.transpose(0, 2, 1, 3).reshape(b, s, d)
        return out @ W_proj.T + b_proj

    def _L1_attn_ref(x, W_attn, W_out, lambda_q1, lambda_k1, lambda_q2, lambda_k2):
        import jax, jax.numpy as jnp
        import numpy as np
        import math
        N_HEAD = 12
        N_EMBD = 192
        HEAD_DIM = N_EMBD // N_HEAD // 2
        DEPTH = 12
        LAMBDA_INIT = 0.8 - 0.6 * math.exp(-0.3 * DEPTH)

        def _sdpa_over_heads(q, k, v):
            scale = 1.0 / math.sqrt(q.shape[-1])
            s = jnp.einsum('bnqd,bnkd->bnqk', q, k) * scale
            a = jax.nn.softmax(s, axis=-1)
            return jnp.einsum('bnqk,bnkd->bnqd', a, v)
        B, N, D = x.shape
        H, hd = (N_HEAD, HEAD_DIM)
        qkv = x @ W_attn.T
        q, k, v = jnp.split(qkv, 3, axis=-1)
        q = q.reshape(B, N, H, 2, hd)
        k = k.reshape(B, N, H, 2, hd)
        v = v.reshape(B, N, H, 2 * hd)
        q1, q2 = (q[:, :, :, 0], q[:, :, :, 1])
        k1, k2 = (k[:, :, :, 0], k[:, :, :, 1])
        o1 = _sdpa_over_heads(q1, k1, v)
        o2 = _sdpa_over_heads(q2, k2, v)
        lam1 = jnp.exp(jnp.sum(lambda_q1 * lambda_k1))
        lam2 = jnp.exp(jnp.sum(lambda_q2 * lambda_k2))
        lam_full = lam1 - lam2 + LAMBDA_INIT
        y = (o1 - lam_full * o2) * (1.0 - LAMBDA_INIT)
        y = y.reshape(B, N, H * 2 * hd)
        return y @ W_out.T

    def _L1_ffn_ref(x, w_router, expert_bias, Wg, Wu, Wd, sg, su, sd):
        import jax, jax.numpy as jnp
        import numpy as np
        B, S, D = (2, 512, 192)
        E, K, F = (8, 2, 384)

        def _swiglu(xf, wg, wu, wd):
            return jax.nn.silu(xf @ wg.T) * (xf @ wu.T) @ wd.T
        b, s, d = x.shape
        xf = x.reshape(-1, d)
        T = xf.shape[0]
        e = w_router.shape[0]
        logits = xf @ w_router.T
        scores = jax.nn.softmax(logits, axis=-1)
        selection = scores + expert_bias[None, :]
        _, top_idx = jax.lax.top_k(selection, K)
        top_s = jnp.take_along_axis(scores, top_idx, axis=-1)
        top_s = top_s / (jnp.sum(top_s, axis=-1, keepdims=True) + 1e-09)
        comb = jnp.zeros((T, e), dtype=x.dtype).at[jnp.arange(T)[:, None], top_idx].add(top_s)

        def body(acc, p):
            wg, wu, wd, c = p
            return (acc + c[:, None] * _swiglu(xf, wg, wu, wd), None)
        routed, _ = jax.lax.scan(body, jnp.zeros_like(xf), (Wg, Wu, Wd, comb.T))
        out = routed + _swiglu(xf, sg, su, sd)
        return out.reshape(b, s, d)
    h = _L0_tok_ref(x, L0_tok_gamma, L0_tok_beta, L0_tok_W, L0_tok_b)
    h = jnp.concatenate([h, txt], axis=1)
    h = h + _L0_attn_ref(_layernorm(h, axis=-1), L0_attn_w_attn, L0_attn_b_attn, L0_attn_w_proj, L0_attn_b_proj)
    h = h + _L0_ffn_ref(_layernorm(h, axis=-1), L0_ffn_W_qkv, L0_ffn_b_qkv, L0_ffn_W_gate, L0_ffn_b_gate, L0_ffn_A, L0_ffn_B_lora, L0_ffn_W_proj, L0_ffn_b_proj)
    h = h + _L1_attn_ref(_layernorm(h, axis=-1), L1_attn_W_attn, L1_attn_W_out, L1_attn_lambda_q1, L1_attn_lambda_k1, L1_attn_lambda_q2, L1_attn_lambda_k2)
    h = h + _L1_ffn_ref(_layernorm(h, axis=-1), L1_ffn_w_router, L1_ffn_expert_bias, L1_ffn_Wg, L1_ffn_Wu, L1_ffn_Wd, L1_ffn_sg, L1_ffn_su, L1_ffn_sd)
    return h

_drawn_inputs = setup_inputs


def setup_inputs(seed=0):
    import zlib

    import numpy as np

    out = dict(_drawn_inputs(seed))
    spreads = {'L0_tok_gamma': (1.0, 0.2),
     'L0_tok_beta': (0.0, 0.1),
     'L0_tok_b': (0.0, 0.8),
     'L0_attn_b_attn': (0.0, 0.8),
     'L0_attn_b_proj': (0.0, 0.8),
     'L0_ffn_b_qkv': (0.0, 0.8),
     'L0_ffn_b_gate': (0.0, 0.8),
     'L0_ffn_b_proj': (0.0, 0.8),
     'L1_ffn_expert_bias': (0.0, 0.8)}
    factors = {'L0_attn_w_attn': 2.945,
     'L0_attn_w_proj': 2.82,
     'L0_ffn_W_qkv': 8.0,
     'L0_ffn_W_gate': 8.0,
     'L0_ffn_A': 8.0,
     'L0_ffn_B_lora': 8.0,
     'L0_ffn_W_proj': 8.0,
     'L1_attn_W_attn': 8.0,
     'L1_attn_W_out': 8.0,
     'L1_attn_lambda_q1': 8.0,
     'L1_attn_lambda_k1': 8.0,
     'L1_attn_lambda_q2': 8.0,
     'L1_attn_lambda_k2': 8.0,
     'L1_ffn_w_router': 8.0,
     'L1_ffn_Wg': 8.0,
     'L1_ffn_Wu': 8.0,
     'L1_ffn_Wd': 8.0,
     'L1_ffn_sg': 8.0,
     'L1_ffn_su': 8.0,
     'L1_ffn_sd': 8.0}
    for name, (base, spread) in spreads.items():
        noise = np.random.default_rng([zlib.crc32(name.encode()), seed]).standard_normal(out[name].shape)
        drawn = base * np.exp(spread * noise) if base else spread * noise
        out[name] = jnp.asarray(drawn.astype(out[name].dtype))
    for name, factor in factors.items():
        out[name] = (out[name] * factor).astype(out[name].dtype)
    return out
```

```python
import math
from contextlib import ExitStack

import numpy as np

import concourse.bass as bass
from concourse import mybir

F32 = mybir.dt.float32
I32 = mybir.dt.int32
BF16 = mybir.dt.bfloat16
ALU = mybir.AluOpType
ACT = mybir.ActivationFunctionType
X = mybir.AxisListType.X

B, TI, TT, D, H = 16, 16, 128, 192, 12
T = TI + TT
HD = D // H
C, R = 2, 96
HC = H // C
G = 2
NG = B // G
N = G * T
TB = T - 128
SL = 32
NE, FE, RANK = 8, 384, 16
NJ = (NE + 1) * FE // 128
JE = FE // 128
NH = 9
HP = 2 * 18 * 3
NI = B * TI
EPS, EPS_TOK = 1e-5, 1e-3
MAGIC = float(0x5F3759DF)
LAMBDA_INIT = 0.8 - 0.6 * math.exp(-0.3 * 12)
MASKED = -2.0 ** 100

PASSES = [(0, 0), (0, 1), (1, 0), (1, 1)]
QSCALE = [2 * HD ** -0.5, HD ** -0.5, (HD // 2) ** -0.5]
FIRST_PASS = [0, 2, 4]
NT, TR = 3, 96
GROUP_CHUNKS = [(0, 0), (1, 0), (1, 1), (2, 1)]

ORDER, ORDER_B = [1, 2, 4, 5], 3

PER = dict(
    txt_in=32, h_ready=8, mean_done=4, xc_done=4, sq_done=4, var_done=4, rsqrt_step=44, y_ready=4, yrep_ready=4,
    qk_done=4, q_ready=2, k_ready=2, kbd=2 * HC * 16, qbd_ready=4, v_done=4, v_ready=12,
    s_done=20, max_ready=20, exp_done=20, norm_step=16, lb_ready=4, t_done=24, pt_dve=16, pt_act=16,
    pv_done=4, o_ready=4, proj_done=3,
    mix_proj=NT, mix_copied=NT, mix_step=9 * NT, mix_sub=NT, mix_exp=NT, mix_out=NT, mix_t=NT, mix_back=NT,
    logits_done=2, gate_sub=2, gate_exp=2, gate_step=24, gate_ready=2, disp_done=1, disp_sb=1, ad_ready=3,
    handed=3, comb_done=8, comb_sb=8, ye_ready=9, gate_up=2 * NJ, tanh_done=NJ, half_done=NJ, hid_done=NJ, down_done=NJ,
    out_ready=1, out_dma=32,
)
FILL = dict(norm_mean=(1, 1, 1, 1), norm_var=(1, 1, 1, 1), gate=(0, 1, 0, 1), keys=(1, 1), scores=(1, 1),
            t0=(0, 0, 0, 0), t1=(1, 1, 1, 1), t2=(0, 0, 0, 0), t3=(1, 1, 0, 0), x0=(0, 0, 0, 0), x1=(0, 0, 0, 0),
            mix0=(1, 0, 0), mix1=(1, 0, 0), mix2=(1, 1, 1), mix3=(0, 0, 0))


def chunks_at():
    order = []
    for l in range(4):
        order += [("norm_mean", l), ("norm_var", l)] + [("gate", l)] * (l in (1, 3))
        if l < 2:
            order.append(("keys", l))
            for u in range(FIRST_PASS[l], FIRST_PASS[l + 1]):
                order += [("scores", l)] * (u == FIRST_PASS[l])
                order += [(point, u) for point in ("t0", "t1", "t2", "t3", "x0", "x1")]
        if l == 2:
            order += [(f"mix{n}", i) for i in range(NT) for n in range(4)]
    where, first = {}, 0
    for point, k in order:
        last = min(NJ, first + FILL[point][k])
        where[point, k] = range(first, last)
        first = last
    where["rest", 0] = range(first, NJ)
    return where


CHUNKS_AT = chunks_at()
DVE_CENTRED, DVE_LAMBDA = 1, 12
PE_MEAN, PE_VAR, PE_BETA0, PE_TOK = 1, 2, 3, 8


def dve_block_used(i):
    return 2 if i == 0 else 2 * i + 1


def program(nc, a, out):
    ctx = ExitStack()
    with ctx:
        def sb(name, shape, dt=F32):
            return ctx.enter_context(nc.sbuf_tensor(name, shape, dt))

        def sem(name):
            return ctx.enter_context(nc.semaphore(name))

        def full(t):
            return t[tuple(slice(None) for _ in t.shape)]

        w_qkv = [sb(f"w_qkv{l}", [R + 1, C, 3 * D]) for l in range(3)]
        w_out = [sb("w_out0", [128, 3, D]), sb("w_out1", [128, 3, D]), sb("w_out2", [R, C, D])]
        b_out = sb("b_out", [R, 3, C])
        w_gate = sb("w_gate", [R + 1, 2, C, NE])
        lora_a = sb("lora_a", [R, C, NE * RANK])
        lora_b = sb("lora_b", [NE * RANK, 3 * D])
        e_bias = sb("e_bias", [TR, NT, NE])
        lam = sb("lam", [TR, 4, HD // 2])
        ident = sb("ident", [128, 128])
        ident_bf = sb("ident_bf", [128, 128], BF16)
        mask_a = sb("mask_a", [128, T], BF16)
        mask_b = sb("mask_b", [R, T], BF16)
        head_q = sb("head_q", [R, HC])
        head_k = sb("head_k", [R, HC])
        col_i = sb("col_i", [R, TB])
        before = sb("before", [TR, NT, NE, NE])
        ones_d = sb("ones_d", [R, R])
        wgu = sb("wgu", [R, 2, C, NJ * 128])
        wdn = sb("wdn", [128, NJ, D])
        coef = sb("coef", [TR, 2 * H])
        img = sb("img", [R, C, NI])

        hin = sb("hin", [R, G, C, TT])
        h = sb("h", [R, C, N])
        xc = sb("xc", [R, C, N])
        y = sb("y", [R + 1, C, N])
        yrep = sb("yrep", [R + 1, C, G, TB, HC])
        var = sb("var", [R, N])
        rs = sb("rs", [R, N])
        rt = sb("rt", [R, N])
        q = sb("q", [R, C, N])
        k = sb("k", [R, C, N])
        qbd = sb("qbd", [R, 2, C, HC, TB])
        va = sb("va", [128, G, H, SL])
        vb = sb("vb", [R, G, C, 8, SL])
        nmax = sb("nmax", [128, 2, H])
        nmax_b = sb("nmax_b", [R, 2, C])
        sums = sb("sums", [128, 2, H])
        sums_b = sb("sums_b", [R, 2, C])
        inv = sb("inv", [128, H])
        inv_b = sb("inv_b", [R, C])
        pb = sb("pb", [R, 2, C, T])
        lb = sb("lb", [R, C, TB, HC])
        inv_x = sb("inv_x", [128, H, SL])
        rbc = sb("rbc", [128, 3, T])
        ptk = sb("ptk", [R, C, T])
        o = sb("o", [128, 3, N])
        mix_m = sb("mix_m", [TR, 2 * H])
        ge = sb("ge", [TR, NT, NE])
        gp = sb("gp", [TR, NT, NE])
        gs = sb("gs", [TR, NT, NE])
        gm = sb("gm", [TR, NT])
        cmp1 = sb("cmp1", [TR, NT, NE, NE])
        cmp2 = sb("cmp2", [TR, NT, NE, NE])
        comb = sb("comb", [TR, NT, NE])
        disp_x = sb("disp_x", [TR, NT, NE, RANK])
        disp_s = sb("disp_s", [128, N])
        ad = sb("ad", [128, N])
        adrep = sb("adrep", [128, G, TB, HC])
        obuf = sb("obuf", [R, C, N])
        sq = o[0:R, 0:C, :]

        work = sb("work", [128, 12096])

        def part(rows, first, pattern=None, **sizes):
            n = math.prod(sizes.values())
            v = work[0:rows, first:first + n]
            names = list(sizes)
            return v.rearrange(f"p ({' '.join(names)}) -> p {' '.join(names)}", **sizes) if len(names) > 1 else v

        win = part(HP, 0, k=NH, n=NI)
        win_sq = part(HP, 2304, k=NH, n=NI)
        wtok = part(HP, 4608, s=2, k=NH, d=D)
        weff = part(HP, 8064, k=NH, d=D)
        wtmp = part(HP, 9792, k=NH, d=D)
        kbd = part(R, 0, c=C, j=HC, n=N)
        comb_bc = part(R, 3456, e=NE, n=N)
        ye = part(R, 5760, s=2, c=C, n=N)
        prod = part(TR, 6912, n=2304)
        ot = part(TR, 9216, t=NT, d=D)
        mix = part(TR, 9792, s=2, a=H, b=H)
        qkvt = part(TR, 10368, t=NT, n=3, d=D)
        pa = part(128, 6912, s=2, c=C, t=T, j=HC)
        pt = part(128, 10368, h=H, t=T)
        hid = sb("hid", [128, 3, N])
        half = sb("half", [R, 1])
        yf = sb("yf", [R, C, N])
        hf = sb("hf", [R, C, N])
        combf = sb("combf", [TR, NT, NE])
        gtok = sb("gtok", [HP, 2, 5, NH])
        mult = sb("mult", [HP, NH])
        btok = sb("btok", [R, C])
        c0 = sb("c0", [R, C])

        ps = ctx.enter_context(nc.psum_tensor("ps", [128, 8, 512], F32))

        s = {name: sem(name) for name in PER}
        ld_tok, ld_w = sem("ld_tok"), [sem(f"ld_wtok{i}") for i in range(5)]
        ld_small, ld_ffn, ready, stored = sem("ld_small"), sem("ld_ffn"), sem("ready"), sem("stored")
        t_pe, t_dve, t_act = sem("t_pe"), sem("t_dve"), sem("t_act")

        small = [(w_qkv[l], f"w_qkv{l}") for l in range(3)] + [(w_out[l], f"w_out{l}") for l in range(3)]
        small += [(b_out, "b_out"), (w_gate, "w_gate"), (lora_a, "lora_a"), (lora_b, "lora_b"), (e_bias, "e_bias"),
                  (lam, "lam"), (ident, "ident"), (disp_s, "masks"),
                  (head_q, "head_q"), (head_k, "head_k"), (col_i, "col_i"), (before, "before")]
        tok = [(win, "win"), (full(mult), "mult"), (full(gtok), "gtok"), (full(btok), "btok")]

        def due(g, name, n):
            return g * PER[name] + n

        def banks(j, alone):
            return (0, 1) if alone and j % 2 else (4, 5)

        block = ctx.enter_context(nc.Block())

        @block.sync
        def _(sp):
            for t, n in tok:
                sp.dma_start(t, a[n]).then_inc(ld_tok, 16)
            for i in range(5):
                if i >= 2:
                    sp.wait_ge(t_dve, dve_block_used(i - 2))
                    sp.wait_ge(t_pe, PE_BETA0 + i - 2)
                sp.dma_start(wtok[:, i % 2], a["wtok"][i]).then_inc(ld_w[i], 16)
            for t, n in small:
                sp.dma_start(full(t), a[n]).then_inc(ld_small, 16)
            sp.dma_start(full(wgu), a["wgu"]).then_inc(ld_ffn, 16)
            sp.dma_start(full(wdn), a["wdn"]).then_inc(ld_ffn, 16)
            sp.wait_ge(ready, 1)

            def keys(g):
                for l in range(2):
                    sp.wait_ge(s["k_ready"], due(g, "k_ready", l + 1))
                    for j in range(HC):
                        rows = slice(HD * j, HD * (j + 1))
                        sp.dma_start(kbd[rows, :, j, :], k[rows, :, :]).then_inc(s["kbd"], 16)

            def store(g):
                sp.wait_ge(s["out_ready"], due(g, "out_ready", 1))
                for b in range(G):
                    sp.dma_start(out[bass.ds(g * G + b, 1)].rearrange("o r c n -> (o r) c n"),
                                 obuf[:, :, b * T:(b + 1) * T]).then_inc(s["out_dma"], 16)
                sp.wait_ge(s["out_dma"], due(g, "out_dma", PER["out_dma"]))
                sp.sem_inc(stored, 1)

            keys(0)
            with sp.Fori(1, NG) as g:
                keys(g)
                store(g - 1)
            store(NG - 1)

        @block.gpsimd
        def _(pool):
            nc.gpsimd.memset(full(va), 0.0)
            nc.gpsimd.memset(full(vb), 0.0)
            nc.gpsimd.memset(rbc[:, :, 128:T], 1.0)
            nc.gpsimd.memset(full(y), 1.0)
            nc.gpsimd.memset(full(ones_d), 1.0 / D)
            nc.gpsimd.memset(full(half), 0.5)
            pool.wait_ge(t_pe, PE_TOK)
            nc.gpsimd.memset(kbd, 0.0).then_inc(ready, 1)
            pool.wait_ge(ld_small, 16 * len(small))

            def load_text(g):
                for b in range(G):
                    pool.dma_start(hin[:, b], a["txt"][bass.ds(g * G + b, 1)].rearrange("o r c n -> (o r) c n"))\
                        .then_inc(s["txt_in"], 16)

            def turn(g, gf):

                def expert_input(e):
                    if e >= 2:
                        pool.wait_ge(s["gate_up"], due(gf, "gate_up", 2 * JE * (e - 1)))
                    if e == NE:
                        pool.wait_ge(s["handed"], due(gf, "handed", 3))
                        for c in range(C):
                            ins = nc.gpsimd.tensor_tensor(ye[:, e % 2, c], yf[:, c], half[:, :].to_broadcast([R, N]),
                                                          ALU.mult)
                    else:
                        pool.wait_ge(s["comb_sb"], due(gf, "comb_sb", e + 1))
                        for c in range(C):
                            ins = nc.gpsimd.tensor_tensor(ye[:, e % 2, c], yf[:, c], comb_bc[:, e], ALU.mult)
                    ins.then_inc(s["ye_ready"], 1)

                def chunk(j):
                    if j % JE == 0:
                        expert_input(j // JE + 1) if j // JE < NE else None

                if gf is not None:
                    expert_input(0)

                def here(point, k):
                    return CHUNKS_AT[point, k] if gf is not None else ()

                if g is None:
                    for j in range(NJ):
                        chunk(j)
                    return
                def queries_b(u):
                    l, b = PASSES[u]
                    pool.wait_ge(s["q_ready"], due(g, "q_ready", l + 1))
                    if u >= 2:
                        pool.wait_ge(s["s_done"], due(g, "s_done", 5 * (u - 1)))
                    for c in range(C):
                        ins = nc.gpsimd.tensor_tensor(
                            qbd[:, u % 2, c], q[:, c, b * T + 128:(b + 1) * T].unsqueeze(1).to_broadcast([R, HC, TB]),
                            head_q[:, :].unsqueeze(2).to_broadcast([R, HC, TB]), ALU.mult)
                    ins.then_inc(s["qbd_ready"], 1)

                def probs_b(u):
                    pool.wait_ge(s["norm_step"], due(g, "norm_step", 4 * u + 3))
                    for c in range(C):
                        ins = nc.gpsimd.tensor_tensor(
                            lb[:, c], pb[:, u % 2, c, 128:T].unsqueeze(2).to_broadcast([R, TB, HC]),
                            head_q[:, :].unsqueeze(1).to_broadcast([R, TB, HC]), ALU.mult)
                    ins.then_inc(s["lb_ready"], 1)

                for l in range(2):
                    for j in here("norm_mean", l):
                        chunk(j)
                    for j in here("norm_var", l):
                        chunk(j)
                    if l == 1:
                        for j in here("gate", 1):
                            chunk(j)
                    for j in here("keys", l):
                        chunk(j)
                    first, last = FIRST_PASS[l], FIRST_PASS[l + 1]
                    queries_b(first)
                    if l == 0:
                        pool.wait_ge(s["h_ready"], due(g, "h_ready", 2))
                        load_text(g + 1)
                    for u in range(first, last):
                        if u == first:
                            for j in here("scores", l):
                                chunk(j)
                        for j in here("t0", u):
                            chunk(j)
                        for j in here("t1", u):
                            chunk(j)
                        for j in here("t2", u):
                            chunk(j)
                        if u + 1 < last:
                            queries_b(u + 1)
                        for j in here("t3", u):
                            chunk(j)
                        for j in here("x0", u):
                            chunk(j)
                        probs_b(u)
                        for j in here("x1", u):
                            chunk(j)
                for l in (2, 3):
                    for point in ("norm_mean", "norm_var"):
                        for j in here(point, l):
                            chunk(j)
                    for i in range(NT if l == 2 else 0):
                        for n in range(4):
                            for j in here(f"mix{n}", i):
                                chunk(j)
                for j in here("gate", 3):
                    chunk(j)
                for j in here("rest", 0):
                    chunk(j)

            load_text(0)
            turn(0, None)
            with pool.Fori(1, NG) as g:
                turn(g, g - 1)
            turn(None, NG - 1)

        @block.scalar
        def _(act):
            fn = nc.scalar.activation
            act.wait_ge(t_dve, DVE_CENTRED)
            fn(win_sq, win, ACT.Square).then_inc(t_act, 1)
            act.wait_ge(t_dve, DVE_LAMBDA)
            fn(gm[:, 0:2], gm[:, 0:2], ACT.Exp).then_inc(t_act, 1)

            def turn(g, gf):
                alone = g is None

                def spread_weights():
                    for e in range(NE):
                        act.wait_ge(s["comb_done"], due(gf, "comb_done", e + 1))
                        nc.scalar.copy(comb_bc[:, e], ps[0:R, 4 + e % 4, 0:N]).then_inc(s["comb_sb"], 1)

                def chunk(j):
                    act.wait_ge(s["gate_up"], due(gf, "gate_up", 2 * j + 1))
                    if j >= 3:
                        act.wait_ge(s["down_done"], due(gf, "down_done", j - 2))
                    fn(hid[:, j % 3], ps[:, banks(j, alone)[0], 0:N], ACT.Tanh, scale=0.5)\
                        .then_inc(s["tanh_done"], 1)


                def here(point, k):
                    return CHUNKS_AT[point, k] if gf is not None else ()

                if alone:
                    spread_weights()
                    for j in range(NJ):
                        chunk(j)
                    return

                def square(l):
                    act.wait_ge(s["xc_done"], due(g, "xc_done", l + 1))
                    fn(sq, full(xc), ACT.Square).then_inc(s["sq_done"], 1)
                    if l == 0 and gf is not None:
                        spread_weights()
                    for j in here("norm_mean", l):
                        chunk(j)
                    for j in here("norm_var", l):
                        chunk(j)

                def gate_exp(n):
                    act.wait_ge(s["gate_sub"], due(g, "gate_sub", n + 1))
                    fn(full(ge), full(ge), ACT.Exp).then_inc(s["gate_exp"], 1)

                def exp_a(u, i):
                    act.wait_ge(s["max_ready"], due(g, "max_ready", 5 * u + ORDER[i]))
                    if i == 0 and u >= 2:
                        act.wait_ge(s["t_done"], due(g, "t_done", 6 * (u - 1)))
                    for hh in range(3 * i, 3 * i + 3):
                        ins = fn(pa[:, u % 2, hh // HC, :, hh % HC], ps[:, i % 2, (hh % 3) * T:(hh % 3 + 1) * T],
                                 ACT.Exp, bias=nmax[:, u % 2, hh:hh + 1], accum_out=sums[:, u % 2, hh:hh + 1])
                    ins.then_inc(s["exp_done"], 1)

                def exp_b(u):
                    act.wait_ge(s["max_ready"], due(g, "max_ready", 5 * u + ORDER_B))
                    for c in range(C):
                        ins = fn(pb[:, u % 2, c, :], ps[0:R, 3, c * T:(c + 1) * T], ACT.Exp,
                                 bias=nmax_b[:, u % 2, c:c + 1], accum_out=sums_b[:, u % 2, c:c + 1])
                    ins.then_inc(s["exp_done"], 1)

                def transposed(u, i):
                    act.wait_ge(s["t_done"], due(g, "t_done", 6 * u + i + 1))
                    nc.scalar.copy(pt[:, 3 * i:3 * i + 3, 0:128], ps[:, 2, 0:384].rearrange("p (h n) -> p h n", h=3))\
                        .then_inc(s["pt_act"], 1)

                for l in range(2):
                    square(l)
                    if l == 1:
                        gate_exp(0)
                        for j in here("gate", 1):
                            chunk(j)
                        act.wait_ge(s["disp_done"], due(g, "disp_done", 1))
                        nc.scalar.copy(full(disp_s), ps[:, 3, 32:32 + N]).then_inc(s["disp_sb"], 1)
                    act.wait_ge(s["qk_done"], due(g, "qk_done", 2 * l + 1))
                    nc.scalar.mul(full(q), ps[0:R, 0:2, 0:N], QSCALE[l]).then_inc(s["q_ready"], 1)
                    for j in here("keys", l):
                        chunk(j)
                    first, last = FIRST_PASS[l], FIRST_PASS[l + 1]
                    for u in range(first, last):
                        if u == first:
                            exp_a(u, 0)
                            exp_a(u, 1)
                            exp_b(u)
                            for j in here("scores", l):
                                chunk(j)
                        exp_a(u, 2)
                        for j in here("t0", u):
                            chunk(j)
                        transposed(u, 1)
                        exp_a(u, 3)
                        for j in here("t1", u):
                            chunk(j)
                        for j in here("t2", u):
                            chunk(j)
                        transposed(u, 3)
                        if u + 1 < last:
                            exp_a(u + 1, 0)
                            exp_a(u + 1, 1)
                        for j in here("t3", u):
                            chunk(j)
                        for j in here("x0", u):
                            chunk(j)
                        act.wait_ge(s["t_done"], due(g, "t_done", 6 * u + 6))
                        nc.scalar.copy(ptk[:, :, 128:T], ps[0:R, 2, 384:416].rearrange("p (c n) -> p c n", c=C))\
                            .then_inc(s["pt_act"], 1)
                        nc.scalar.copy(rbc[:, :, 0:128], ps[:, 2, 0:384].rearrange("p (g n) -> p g n", g=3))\
                            .then_inc(s["pt_act"], 1)
                        for j in here("x1", u):
                            chunk(j)
                        if u + 1 < last:
                            exp_b(u + 1)
                square(2)
                for i in range(NT):
                    act.wait_ge(s["mix_proj"], due(g, "mix_proj", i + 1))
                    b0 = 2 * (i % 2)
                    nc.scalar.mul(qkvt[:, i, 0, :], ps[0:TR, b0, 0:D], QSCALE[2])
                    nc.scalar.copy(qkvt[:, i, 1, :], ps[0:TR, b0, D:2 * D])
                    nc.scalar.copy(qkvt[:, i, 2, :], ps[0:TR, b0 + 1, 0:D]).then_inc(s["mix_copied"], 1)
                for i in range(NT):
                    for j in here("mix0", i):
                        chunk(j)
                    act.wait_ge(s["mix_sub"], due(g, "mix_sub", i + 1))
                    fn(mix, mix, ACT.Exp).then_inc(s["mix_exp"], 1)
                    for j in here("mix1", i):
                        chunk(j)
                    for j in here("mix2", i):
                        chunk(j)
                    for j in here("mix3", i):
                        chunk(j)
                    act.wait_ge(s["mix_t"], due(g, "mix_t", i + 1))
                    nc.scalar.copy(o[0:R, 0:C, i * TR:(i + 1) * TR],
                                   ps[0:R, 2 + i % 2, 0:C * TR].rearrange("p (c n) -> p c n", c=C))\
                        .then_inc(s["mix_back"], 1)
                square(3)
                gate_exp(1)
                for j in here("gate", 3):
                    chunk(j)
                for j in here("rest", 0):
                    chunk(j)

            turn(0, None)
            with act.Fori(1, NG) as g:
                turn(g, g - 1)
            turn(None, NG - 1)

        @block.vector
        def _(dve):
            tt, ts, stt = nc.vector.tensor_tensor, nc.vector.tensor_scalar, nc.vector.scalar_tensor_tensor
            cp, red, rec = nc.vector.tensor_copy, nc.vector.tensor_reduce, nc.vector.reciprocal
            count = [0]

            def link(ins):
                count[0] += 1
                ins.then_inc(t_dve, 1)
                dve.wait_ge(t_dve, count[0])

            def rsqrt(src, eps, v, r, t, mark):
                mark(ts(v, src, eps, None, ALU.add))
                mark(ts(r.bitcast(I32), v.bitcast(I32), -0.5, MAGIC, ALU.mult, ALU.add))
                for _ in range(3):
                    mark(stt(t, r, -0.5, r, ALU.mult, ALU.mult))
                    mark(tt(t, t, v, ALU.mult))
                    mark(stt(r, t, 1.5, r, ALU.add, ALU.mult))

            dve.wait_ge(ld_tok, 16 * len(tok))
            dve.wait_ge(t_pe, PE_MEAN)
            link(tt(win, win, ps[0:HP, 0, 0:NI].unsqueeze(1).to_broadcast([HP, NH, NI]), ALU.subtract))
            assert count[0] == DVE_CENTRED
            for i in range(5):
                dve.wait_ge(ld_w[i], 16)
                gamma = gtok[:, 0, i, :].unsqueeze(2).to_broadcast([HP, NH, D])
                link(tt(weff if i == 0 else wtmp, wtok[:, i % 2], gamma, ALU.mult))
                assert count[0] == dve_block_used(i)
                if i:
                    link(tt(weff, weff, wtmp, ALU.add))
            dve.wait_ge(ld_small, 16 * len(small))
            link(tt(cmp1[:, 0, 0:2, :], lam[:, 0:4:2, :], lam[:, 1:4:2, :], ALU.mult))
            link(red(gm[:, 0:2], cmp1[:, 0, 0:2, :], X, ALU.add))
            assert count[0] == DVE_LAMBDA
            dve.wait_ge(t_act, 2)
            link(tt(gm[:, 2:3], gm[:, 0:1], gm[:, 1:2], ALU.subtract))
            link(ts(coef[:, H:2 * H], gm[:, 2:3].to_broadcast([TR, H]), LAMBDA_INIT, -(1.0 - LAMBDA_INIT),
                    ALU.add, ALU.mult))
            link(nc.vector.memset(coef[:, 0:H], 1.0 - LAMBDA_INIT))
            link(cp(full(ident_bf), full(ident)))
            link(cp(full(mask_a), disp_s[:, 0:T]))
            link(cp(full(mask_b), disp_s[0:R, T:2 * T]))
            dve.wait_ge(t_pe, PE_VAR)
            rsqrt(ps[0:R, 1, 0:NI], EPS_TOK, var[:, 0:NI], rs[:, 0:NI], rt[:, 0:NI], link)
            dve.wait_ge(t_pe, PE_BETA0 + 4)
            link(tt(c0[:, :].unsqueeze(2), ps[0:R, 2:4, 0:1], btok[:, :].unsqueeze(2), ALU.add))
            dve.wait_ge(t_pe, PE_TOK)
            link(tt(full(img), ps[0:R, 4:6, 0:NI], rs[:, 0:NI].unsqueeze(1).to_broadcast([R, C, NI]), ALU.mult))
            for c in range(C):
                link(ts(img[:, c, :], img[:, c, :], c0[:, c:c + 1], None, ALU.add))
            dve.wait_ge(ready, 1)


            def turn(g, gf):
                alone = g is None
                steps = {"rsqrt_step": 0, "norm_step": 0, "gate_step": 0, "mix_step": 0}

                def stepper(name):
                    def mark(ins):
                        steps[name] += 1
                        ins.then_inc(s[name], 1)
                        dve.wait_ge(s[name], due(g, name, steps[name]))
                    return mark

                def hand_over():
                    cp(full(yf), y[0:R]).then_inc(s["handed"], 1)
                    cp(full(hf), full(h)).then_inc(s["handed"], 1)
                    cp(full(combf), full(comb)).then_inc(s["handed"], 1)
                    dve.wait_ge(s["handed"], due(gf, "handed", 3))

                def chunk(j):
                    gate, up = banks(j, alone)
                    dve.wait_ge(s["tanh_done"], due(gf, "tanh_done", j + 1))
                    stt(hid[:, j % 3], hid[:, j % 3], 1.0, ps[:, gate, 0:N], ALU.add, ALU.mult)\
                        .then_inc(s["half_done"], 1)
                    dve.wait_ge(s["half_done"], due(gf, "half_done", j + 1))
                    dve.wait_ge(s["gate_up"], due(gf, "gate_up", 2 * j + 2))
                    tt(hid[:, j % 3], hid[:, j % 3], ps[:, up, 0:N], ALU.mult).then_inc(s["hid_done"], 1)

                def finish():
                    dve.wait_ge(s["down_done"], due(gf, "down_done", NJ))
                    if alone:
                        dve.wait_ge(s["out_dma"], due(gf, "out_dma", 0))
                    tt(full(obuf), ps[0:R, 6:8, 0:N], full(hf), ALU.add).then_inc(s["out_ready"], 1)
                    dve.wait_ge(s["out_ready"], due(gf, "out_ready", 1))


                def here(point, k):
                    return CHUNKS_AT[point, k] if gf is not None else ()

                if gf is not None:
                    dve.wait_ge(s["gate_ready"], due(gf, "gate_ready", 2))
                    hand_over()
                if alone:
                    for j in range(NJ):
                        chunk(j)
                    finish()
                    return

                def layernorm(l):
                    dve.wait_ge(s["h_ready"], due(g, "h_ready", 2 * l + 2))
                    dve.wait_ge(s["mean_done"], due(g, "mean_done", l + 1))
                    tt(full(xc), full(h), ps[0:R, 3, 0:N].unsqueeze(1).to_broadcast([R, C, N]), ALU.subtract)\
                        .then_inc(s["xc_done"], 1)
                    for j in here("norm_mean", l):
                        chunk(j)
                    dve.wait_ge(s["var_done"], due(g, "var_done", l + 1))
                    rsqrt(ps[0:R, 2, 0:N], EPS, full(var), full(rs), full(rt), stepper("rsqrt_step"))
                    dve.wait_ge(s["xc_done"], due(g, "xc_done", l + 1))
                    tt(y[0:R], full(xc), rs[:, :].unsqueeze(1).to_broadcast([R, C, N]), ALU.mult)\
                        .then_inc(s["y_ready"], 1)
                    dve.wait_ge(s["y_ready"], due(g, "y_ready", l + 1))
                    for c in range(C if l < 2 else 0):
                        yb = y[:, c, :].rearrange("p (b n) -> p b n", b=G)[:, :, 128:T]
                        cp(yrep[:, c], yb.unsqueeze(3).to_broadcast([R + 1, G, TB, HC])).then_inc(s["yrep_ready"], 1)
                    for j in here("norm_var", l):
                        chunk(j)

                def top2(n):
                    mark = stepper("gate_step")
                    dve.wait_ge(s["logits_done"], due(g, "logits_done", n + 1))
                    lg = ps[0:TR, 3, 0:NT * NE].rearrange("p (t e) -> p t e", e=NE)
                    spread = gm[:, :].unsqueeze(2).to_broadcast([TR, NT, NE])
                    mark(red(full(gm), lg, X, ALU.max))
                    tt(full(ge), lg, spread, ALU.subtract).then_inc(s["gate_sub"], 1)
                    dve.wait_ge(s["gate_exp"], due(g, "gate_exp", n + 1))
                    mark(red(full(gm), full(ge), X, ALU.add))
                    mark(rec(full(gm), full(gm)))
                    mark(tt(full(gp), full(ge), spread, ALU.mult))
                    if n == 1:
                        mark(tt(full(gs), full(gp), full(e_bias), ALU.add))
                    sel = gp if n == 0 else gs
                    other = sel[:, :, :].unsqueeze(2).to_broadcast([TR, NT, NE, NE])
                    own = sel[:, :, :].unsqueeze(3).to_broadcast([TR, NT, NE, NE])
                    mark(tt(full(cmp1), other, own, ALU.is_gt))
                    mark(tt(full(cmp2), other, own, ALU.is_equal))
                    mark(tt(full(cmp2), full(cmp2), full(before), ALU.mult))
                    mark(tt(full(cmp1), full(cmp1), full(cmp2), ALU.add))
                    mark(red(full(gs), full(cmp1), X, ALU.add))
                    mark(stt(full(gs), full(gs), 2.0, full(gp), ALU.is_lt, ALU.mult))
                    return mark

                def maxima_a(u, i):
                    dve.wait_ge(s["s_done"], due(g, "s_done", 5 * u + ORDER[i]))
                    red(nmax[:, u % 2, 3 * i:3 * i + 3], ps[:, i % 2, 0:3 * T].rearrange("p (j n) -> p j n", j=3), X,
                        ALU.max, negate=True).then_inc(s["max_ready"], 1)

                def maxima_b(u):
                    dve.wait_ge(s["s_done"], due(g, "s_done", 5 * u + ORDER_B))
                    red(nmax_b[:, u % 2, :], ps[0:R, 3, 0:C * T].rearrange("p (c n) -> p c n", c=C), X, ALU.max,
                        negate=True).then_inc(s["max_ready"], 1)

                def normalise(u):
                    mark = stepper("norm_step")
                    dve.wait_ge(s["exp_done"], due(g, "exp_done", 5 * u + 5))
                    mark(rec(full(inv), sums[:, u % 2, :]))
                    mark(rec(full(inv_b), sums_b[:, u % 2, :]))
                    for c in range(C):
                        p = pb[:, u % 2, c, :]
                        ins = ts(p, p, inv_b[:, c:c + 1], None, ALU.mult)
                    mark(ins)
                    mark(cp(full(inv_x), inv[:, :].unsqueeze(2).to_broadcast([128, H, SL])))

                def transposed_a(u, i):
                    dve.wait_ge(s["t_done"], due(g, "t_done", 6 * u + i + 1))
                    cp(pt[:, 3 * i:3 * i + 3, 0:128], ps[:, 2, 0:384].rearrange("p (h n) -> p h n", h=3))\
                        .then_inc(s["pt_dve"], 1)

                def transposed_b(u):
                    dve.wait_ge(s["t_done"], due(g, "t_done", 6 * u + 5))
                    cp(pt[:, :, 128:T], ps[:, 2, 0:H * TB].rearrange("p (h i) -> p h i", h=H)).then_inc(s["pt_dve"], 1)
                    cp(ptk[:, :, 0:128], ps[0:R, 2, 192:448].rearrange("p (c n) -> p c n", c=C))\
                        .then_inc(s["pt_dve"], 1)

                def output(u):
                    _, b = PASSES[u]
                    dve.wait_ge(s["pv_done"], due(g, "pv_done", u + 1))
                    dve.wait_ge(s["pt_act"], due(g, "pt_act", 4 * u + 4))
                    tt(o[:, :, b * T:(b + 1) * T], ps[:, 3, 0:3 * T].rearrange("p (g n) -> p g n", g=3), full(rbc),
                       ALU.mult).then_inc(s["o_ready"], 1)

                def residual(l):
                    dve.wait_ge(s["proj_done"], due(g, "proj_done", l + 1))
                    for c in range(C):
                        stt(h[:, c, :], ps[0:R, c, 0:N], b_out[:, l, c:c + 1], h[:, c, :], ALU.add, ALU.add)\
                            .then_inc(s["h_ready"], 1)

                def mix_heads(i):
                    mark = stepper("mix_step")
                    dve.wait_ge(s["mix_copied"], due(g, "mix_copied", i + 1))
                    if i:
                        dve.wait_ge(s["mix_out"], due(g, "mix_out", i))
                    qh, kh, vh = (qkvt[:, i, n, :].rearrange("p (h d) -> p h d", h=H) for n in range(3))
                    half = H * H * HD // 2
                    for n in range(2):
                        d = slice(n * (HD // 2), (n + 1) * (HD // 2))
                        sh = [TR, H, H, HD // 2]
                        ins = tt(prod[:, n * half:(n + 1) * half].rearrange("p (a b d) -> p a b d", a=H, b=H),
                                 qh[:, :, d].unsqueeze(2).to_broadcast(sh), kh[:, :, d].unsqueeze(1).to_broadcast(sh),
                                 ALU.mult)
                    mark(ins)
                    for j in here("mix0", i):
                        chunk(j)
                    rows = mix.rearrange("p n a b -> p (n a) b")
                    spread = mix_m[:, :].unsqueeze(2).to_broadcast([TR, 2 * H, H])
                    mark(red(mix.rearrange("p n a b -> p (n a b)"),
                             prod.rearrange("p (a d) -> p a d", d=HD // 2), X, ALU.add))
                    mark(red(full(mix_m), rows, X, ALU.max))
                    tt(rows, rows, spread, ALU.subtract).then_inc(s["mix_sub"], 1)
                    for j in here("mix1", i):
                        chunk(j)
                    dve.wait_ge(s["mix_exp"], due(g, "mix_exp", i + 1))
                    mark(red(full(mix_m), rows, X, ALU.add))
                    mark(rec(full(mix_m), full(mix_m)))
                    mark(tt(full(mix_m), full(mix_m), full(coef), ALU.mult))
                    mark(tt(rows, rows, spread, ALU.mult))
                    mark(tt(mix[:, 0], mix[:, 0], mix[:, 1], ALU.add))
                    sh = [TR, H, HD, H]
                    mark(tt(prod.rearrange("p (a d b) -> p a d b", a=H, d=HD), mix[:, 0].unsqueeze(2).to_broadcast(sh),
                            vh.rearrange("p h d -> p d h").unsqueeze(1).to_broadcast(sh), ALU.mult))
                    for j in here("mix2", i):
                        chunk(j)
                    red(ot[:, i, :], prod.rearrange("p (a b) -> p a b", b=H), X, ALU.add).then_inc(s["mix_out"], 1)
                    for j in here("mix3", i):
                        chunk(j)

                dve.wait_ge(s["txt_in"], due(g, "txt_in", 32))
                hv = h[:, :, :].rearrange("p c (b n) -> p c b n", b=G)
                cp(hv[:, :, :, TI:T], hin[:, :, :, :].rearrange("p b c n -> p c b n")).then_inc(s["h_ready"], 1)
                cp(hv[:, :, :, 0:TI], img[:, :, bass.ds(g * (G * TI), G * TI)].rearrange("p c (b n) -> p c b n", b=G))\
                    .then_inc(s["h_ready"], 1)
                for l in range(2):
                    layernorm(l)
                    if l == 1:
                        mark = top2(0)
                        for j in here("gate", 1):
                            chunk(j)
                        ts(full(disp_x), gs[:, :, :].unsqueeze(3).to_broadcast([TR, NT, NE, RANK]), 2.0, None,
                           ALU.mult).then_inc(s["gate_ready"], 1)
                        dve.wait_ge(s["disp_sb"], due(g, "disp_sb", 1))
                        tt(full(ad), full(disp_s), ps[:, 2, 0:N], ALU.mult).then_inc(s["ad_ready"], 1)
                        dve.wait_ge(s["ad_ready"], due(g, "ad_ready", 1))
                        for b in range(G):
                            cp(adrep[:, b], ad[:, b * T + 128:(b + 1) * T].unsqueeze(2).to_broadcast([128, TB, HC]))\
                                .then_inc(s["ad_ready"], 1)
                    dve.wait_ge(s["qk_done"], due(g, "qk_done", 2 * l + 2))
                    cp(full(k), ps[0:R, 2:4, 0:N]).then_inc(s["k_ready"], 1)
                    for b in range(G):
                        dve.wait_ge(s["v_done"], due(g, "v_done", 2 * l + b + 1))
                        cp(va[:, b, :, 0:HD], ps[:, 2 + b, 0:D].rearrange("p (h d) -> p h d", h=H))\
                            .then_inc(s["v_ready"], 1)
                        for c in range(C):
                            tt(vb[:, b, c, 2 * c:2 * c + HC, 0:HD],
                               ps[0:R, 2 + b, D + c * R:D + (c + 1) * R].rearrange("p (h d) -> p h d", h=HC),
                               head_k[:, :].unsqueeze(2).to_broadcast([R, HC, HD]), ALU.mult).then_inc(s["v_ready"], 1)
                    for j in here("keys", l):
                        chunk(j)
                    first, last = FIRST_PASS[l], FIRST_PASS[l + 1]
                    for u in range(first, last):
                        if u == first:
                            maxima_a(u, 0)
                            maxima_a(u, 1)
                            maxima_b(u)
                            for j in here("scores", l):
                                chunk(j)
                        transposed_a(u, 0)
                        maxima_a(u, 2)
                        for j in here("t0", u):
                            chunk(j)
                        maxima_a(u, 3)
                        for j in here("t1", u):
                            chunk(j)
                        transposed_a(u, 2)
                        normalise(u)
                        for j in here("t2", u):
                            chunk(j)
                        if u + 1 < last:
                            maxima_a(u + 1, 0)
                            maxima_a(u + 1, 1)
                        for j in here("t3", u):
                            chunk(j)
                        transposed_b(u)
                        for j in here("x0", u):
                            chunk(j)
                        for j in here("x1", u):
                            chunk(j)
                        output(u)
                        if u + 1 < last:
                            maxima_b(u + 1)
                    residual(l)
                layernorm(2)
                for i in range(NT):
                    mix_heads(i)
                residual(2)
                layernorm(3)
                mark = top2(1)
                mark(red(full(gm), full(gs), X, ALU.add))
                mark(ts(full(gm), full(gm), 1e-9, 2.0, ALU.add, ALU.mult))
                mark(rec(full(gm), full(gm)))
                tt(full(comb), full(gs), gm[:, :].unsqueeze(2).to_broadcast([TR, NT, NE]), ALU.mult)\
                    .then_inc(s["gate_ready"], 1)

                for j in here("gate", 3):
                    chunk(j)
                for j in here("rest", 0):
                    chunk(j)
                if gf is not None:
                    finish()
                assert steps == {x: PER[x] for x in steps}, steps

            turn(0, None)
            with dve.Fori(1, NG) as g:
                turn(g, g - 1)
            turn(None, NG - 1)

        @block.tensor
        def _(pe):
            mm, tr = nc.tensor.matmul, nc.tensor.transpose
            pe.wait_ge(ld_tok, 16 * len(tok))
            for i in range(NH):
                ins = mm(ps[0:HP, 0, 0:NI], mult[:, i:i + 1].to_broadcast([HP, HP]), win[:, i], start=i == 0,
                         stop=i == NH - 1)
            ins.then_inc(t_pe, 1)
            pe.wait_ge(t_act, 1)
            for i in range(NH):
                ins = mm(ps[0:HP, 1, 0:NI], mult[:, i:i + 1].to_broadcast([HP, HP]), win_sq[:, i], start=i == 0,
                         stop=i == NH - 1)
            ins.then_inc(t_pe, 1)
            for i in range(5):
                pe.wait_ge(ld_w[i], 16)
                for kk in range(NH):
                    for c in range(C):
                        ins = mm(ps[0:R, 2 + c, 0:1], wtok[:, i % 2, kk, c * R:(c + 1) * R], gtok[:, 1, i, kk:kk + 1],
                                 start=i == kk == 0, stop=i == 4 and kk == NH - 1)
                ins.then_inc(t_pe, 1)
            pe.wait_ge(t_dve, dve_block_used(4) + 1)
            for c in range(C):
                for kk in range(NH):
                    ins = mm(ps[0:R, 4 + c, 0:NI], weff[:, kk, c * R:(c + 1) * R], win[:, kk], start=kk == 0,
                             stop=kk == NH - 1)
            ins.then_inc(t_pe, 1)
            pe.wait_ge(ready, 1)
            pe.wait_ge(ld_small, 16 * len(small))

            def turn(g, gf):
                alone = g is None

                def expert_weights():
                    pe.wait_ge(s["handed"], due(gf, "handed", 3))
                    for e in range(NE):
                        if e >= 4:
                            pe.wait_ge(s["comb_sb"], due(gf, "comb_sb", e - 3))
                        for i in range(NT):
                            ins = tr(ps[0:R, 4 + e % 4, i * TR:(i + 1) * TR],
                                     combf[:, i, e:e + 1].to_broadcast([TR, R]), ident[0:TR, 0:TR])
                        ins.then_inc(s["comb_done"], 1)
                    pe.wait_ge(s["comb_sb"], due(gf, "comb_sb", NE))

                def hidden(j):
                    e = j // JE
                    former = j - 1 if alone else j
                    if former > 0:
                        pe.wait_ge(s["hid_done"], due(gf, "hid_done", former))
                    pe.wait_ge(s["ye_ready"], due(gf, "ye_ready", e + 1))
                    for n in range(2):
                        for c in range(C):
                            ins = mm(ps[:, banks(j, alone)[n], 0:N], wgu[:, n, c, j * 128:(j + 1) * 128],
                                     yf[:, c, :] if n == 0 else ye[:, e % 2, c, :], start=c == 0, stop=c == C - 1)
                        ins.then_inc(s["gate_up"], 1)

                def down(j):
                    pe.wait_ge(s["hid_done"], due(gf, "hid_done", j + 1))
                    for c in range(C):
                        ins = mm(ps[0:R, 6 + c, 0:N], wdn[:, j, c * R:(c + 1) * R], hid[:, j % 3], start=j == 0,
                                 stop=j == NJ - 1)
                    ins.then_inc(s["down_done"], 1)

                def chunk(j):
                    hidden(j)
                    if j:
                        down(j - 1)

                def finish():
                    down(NJ - 1)
                    pe.wait_ge(s["out_ready"], due(gf, "out_ready", 1))


                def here(point, k):
                    return CHUNKS_AT[point, k] if gf is not None else ()

                if alone:
                    expert_weights()
                    for j in range(NJ):
                        chunk(j)
                    finish()
                    return

                def layernorm(l):
                    pe.wait_ge(s["h_ready"], due(g, "h_ready", 2 * l + 2))
                    for c in range(C):
                        ins = mm(ps[0:R, 3, 0:N], full(ones_d), h[:, c, :], start=c == 0, stop=c == C - 1)
                    ins.then_inc(s["mean_done"], 1)
                    if l == 0 and gf is not None:
                        expert_weights()
                    for j in here("norm_mean", l):
                        chunk(j)
                    pe.wait_ge(s["sq_done"], due(g, "sq_done", l + 1))
                    for c in range(C):
                        ins = mm(ps[0:R, 2, 0:N], full(ones_d), sq[:, c, :], start=c == 0, stop=c == C - 1)
                    ins.then_inc(s["var_done"], 1)
                    for j in here("norm_var", l):
                        chunk(j)
                    pe.wait_ge(s["y_ready"], due(g, "y_ready", l + 1))

                def rows(c):
                    return R + 1 if c == 0 else R

                def logits(n):
                    for i in range(NT):
                        for c in range(C):
                            r = rows(c)
                            ins = mm(ps[0:TR, 3, i * NE:(i + 1) * NE], y[0:r, c, i * TR:(i + 1) * TR],
                                     w_gate[0:r, n, c, :], start=c == 0, stop=c == C - 1)
                    ins.then_inc(s["logits_done"], 1)

                def lora_down():
                    for c in range(C):
                        mm(ps[:, 2, 0:N], lora_a[:, c, :], y[0:R, c, :], start=c == 0, stop=c == C - 1)
                    for j in here("gate", 1):
                        chunk(j)
                    pe.wait_ge(s["gate_ready"], due(g, "gate_ready", 1))
                    for i in range(NT):
                        ins = tr(ps[:, 3, 32 + i * TR:32 + (i + 1) * TR],
                                 disp_x[:, i, :, :].rearrange("p e r -> p (e r)"), ident[0:TR, 0:TR])
                    ins.then_inc(s["disp_done"], 1)
                    pe.wait_ge(s["ad_ready"], due(g, "ad_ready", 3))

                def projections(l):
                    lora = l == 1
                    for n in range(2):
                        for c in range(C):
                            cols = slice(n * D + c * R, n * D + (c + 1) * R)
                            for i in range(C):
                                r = rows(i)
                                ins = mm(ps[0:R, 2 * n + c, 0:N], w_qkv[l][0:r, i, cols], y[0:r, i, :], start=i == 0,
                                         stop=i == C - 1 and not lora)
                            if lora:
                                ins = mm(ps[0:R, 2 * n + c, 0:N], lora_b[:, cols], full(ad), start=False, stop=True)
                        ins.then_inc(s["qk_done"], 1)
                    pe.wait_ge(s["yrep_ready"], due(g, "yrep_ready", 2 * l + 2))
                    pe.wait_ge(s["k_ready"], due(g, "k_ready", l + 1))
                    for b in range(G):
                        for m, lhs, lhs_ad, col in (
                                (128, lambda i, r: y[0:r, i, b * T:b * T + 128], ad[:, b * T:b * T + 128], 0),
                                (R, lambda i, r: yrep[0:r, i, b].rearrange("p n h -> p (n h)"),
                                 adrep[:, b].rearrange("p n h -> p (n h)"), D)):
                            dst = ps[0:m, 2 + b, col:col + D]
                            for i in range(C):
                                r = rows(i)
                                ins = mm(dst, lhs(i, r), w_qkv[l][0:r, i, 2 * D:3 * D], start=i == 0,
                                         stop=i == C - 1 and not lora)
                            if lora:
                                ins = mm(dst, lhs_ad, lora_b[:, 2 * D:3 * D], start=False, stop=True)
                        ins.then_inc(s["v_done"], 1)

                def scores_a(u, i):
                    l, b = PASSES[u]
                    before_ = 5 * u + ORDER[i - 2] if i >= 2 else 5 * (u - 1) + ORDER[i + 2]
                    if i >= 2 or u > FIRST_PASS[l]:
                        pe.wait_ge(s["exp_done"], due(g, "exp_done", before_))
                    c, j = i // 2, 3 * (i % 2)
                    dst = ps[:, i % 2, 0:3 * T]
                    ins = mm(dst, q[:, c, b * T:b * T + 128], kbd[:, c, j:j + 3, b * T:(b + 1) * T],
                             start=True, stop=l > 0)
                    if l == 0:
                        ins = mm(dst, full(ident_bf), mask_a[:, :].unsqueeze(1).to_broadcast([128, 3, T]),
                                 start=False, stop=True)
                    ins.then_inc(s["s_done"], 1)

                def scores_b(u):
                    l, b = PASSES[u]
                    pe.wait_ge(s["qbd_ready"], due(g, "qbd_ready", u + 1))
                    if u > FIRST_PASS[l]:
                        pe.wait_ge(s["o_ready"], due(g, "o_ready", u))
                    for c in range(C):
                        dst = ps[0:R, 3, c * T:(c + 1) * T]
                        ins = mm(dst, qbd[:, u % 2, c].rearrange("p h i -> p (h i)"), k[:, c, b * T:(b + 1) * T],
                                 start=True, stop=l > 0)
                        if l == 0:
                            ins = mm(dst, ident_bf[0:R, 0:R], full(mask_b), start=False, stop=True)
                    ins.then_inc(s["s_done"], 1)

                def transposes_a(u, i):
                    if i == 0:
                        if u:
                            pe.wait_ge(s["pt_act"], due(g, "pt_act", 4 * u))
                    elif i % 2:
                        pe.wait_ge(s["pt_dve"], due(g, "pt_dve", 4 * u + (i + 1) // 2))
                    else:
                        pe.wait_ge(s["pt_act"], due(g, "pt_act", 4 * u + 1))
                    pe.wait_ge(s["exp_done"], due(g, "exp_done", 5 * u + ORDER[i]))
                    for j in range(3):
                        hh = 3 * i + j
                        ins = tr(ps[:, 2, j * 128:(j + 1) * 128], pa[:, u % 2, hh // HC, 0:128, hh % HC], full(ident))
                    ins.then_inc(s["t_done"], 1)

                def transposes_b(u):
                    pe.wait_ge(s["pt_act"], due(g, "pt_act", 4 * u + 2))
                    pe.wait_ge(s["norm_step"], due(g, "norm_step", 4 * u + 3))
                    for c in range(C):
                        tr(ps[:, 2, c * R:(c + 1) * R], pb[:, u % 2, c, 0:128], ident[0:R, 0:R])
                    for c in range(C):
                        ins = tr(ps[0:R, 2, 192 + c * 128:320 + c * 128],
                                 pa[:, u % 2, c, 128:T, :].rearrange("p n h -> p (n h)"), full(ident))
                    ins.then_inc(s["t_done"], 1)

                def transposes_x(u):
                    pe.wait_ge(s["pt_dve"], due(g, "pt_dve", 4 * u + 4))
                    pe.wait_ge(s["norm_step"], due(g, "norm_step", 4 * u + 4))
                    for gg in range(3):
                        tr(ps[:, 2, gg * 128:(gg + 1) * 128],
                           inv_x[:, 4 * gg:4 * gg + 4, :].rearrange("p h r -> p (h r)"), full(ident))
                    pe.wait_ge(s["lb_ready"], due(g, "lb_ready", u + 1))
                    for c in range(C):
                        ins = mm(ps[0:R, 2, 384 + c * TB:384 + (c + 1) * TB], lb[:, c].rearrange("p n h -> p (n h)"),
                                 full(col_i), start=True, stop=True)
                    ins.then_inc(s["t_done"], 1)

                def values(u):
                    l, b = PASSES[u]
                    pe.wait_ge(s["exp_done"], due(g, "exp_done", 5 * u + 5))
                    pe.wait_ge(s["pt_act"], due(g, "pt_act", 4 * u + 3))
                    for gg in range(3):
                        cols = slice(gg * T, (gg + 1) * T)
                        for j in range(4):
                            mm(ps[SL * j:SL * (j + 1), 3, cols], va[:, b, 4 * gg + j, :], pt[:, 4 * gg + j, :],
                               start=True, stop=False)
                        chunks = [c for g_, c in GROUP_CHUNKS if g_ == gg]
                        for c in chunks:
                            first = 4 * gg - 4 * c
                            ins = mm(ps[:, 3, cols], vb[:, b, c, first:first + 4, :].rearrange("p h r -> p (h r)"),
                                     ptk[:, c, :], start=False, stop=c == chunks[-1])
                    ins.then_inc(s["pv_done"], 1)

                for l in range(2):
                    layernorm(l)
                    if l == 1:
                        logits(0)
                        lora_down()
                    projections(l)
                    for j in here("keys", l):
                        chunk(j)
                    first, last = FIRST_PASS[l], FIRST_PASS[l + 1]
                    pe.wait_ge(s["q_ready"], due(g, "q_ready", l + 1))
                    pe.wait_ge(s["kbd"], due(g, "kbd", (l + 1) * HC * 16))
                    for u in range(first, last):
                        if u == first:
                            scores_a(u, 0)
                            scores_a(u, 1)
                            pe.wait_ge(s["v_ready"], due(g, "v_ready", 6 * (l + 1)))
                            scores_b(u)
                            for j in here("scores", l):
                                chunk(j)
                        transposes_a(u, 0)
                        scores_a(u, 2)
                        for j in here("t0", u):
                            chunk(j)
                        transposes_a(u, 1)
                        scores_a(u, 3)
                        for j in here("t1", u):
                            chunk(j)
                        transposes_a(u, 2)
                        for j in here("t2", u):
                            chunk(j)
                        transposes_a(u, 3)
                        if u + 1 < last:
                            scores_a(u + 1, 0)
                            scores_a(u + 1, 1)
                        for j in here("t3", u):
                            chunk(j)
                        transposes_b(u)
                        for j in here("x0", u):
                            chunk(j)
                        transposes_x(u)
                        for j in here("x1", u):
                            chunk(j)
                        values(u)
                        if u + 1 < last:
                            scores_b(u + 1)
                    pe.wait_ge(s["o_ready"], due(g, "o_ready", last))
                    for c in range(C):
                        for gg in range(3):
                            ins = mm(ps[0:R, c, 0:N], w_out[l][:, gg, c * R:(c + 1) * R], o[:, gg, :],
                                     start=gg == 0, stop=gg == 2)
                    ins.then_inc(s["proj_done"], 1)

                layernorm(2)
                for i in range(NT):
                    if i == 2:
                        pe.wait_ge(s["mix_copied"], due(g, "mix_copied", 1))
                    b0 = 2 * (i % 2)
                    for bank, cols in ((b0, slice(0, 2 * D)), (b0 + 1, slice(2 * D, 3 * D))):
                        for c in range(C):
                            r = rows(c)
                            ins = mm(ps[0:TR, bank, 0:cols.stop - cols.start], y[0:r, c, i * TR:(i + 1) * TR],
                                     w_qkv[2][0:r, c, cols], start=c == 0, stop=c == C - 1)
                    ins.then_inc(s["mix_proj"], 1)
                for i in range(NT):
                    for n in range(4):
                        for j in here(f"mix{n}", i):
                            chunk(j)
                    pe.wait_ge(s["mix_out"], due(g, "mix_out", i + 1))
                    if i == 2:
                        pe.wait_ge(s["mix_back"], due(g, "mix_back", 1))
                    for c in range(C):
                        ins = tr(ps[0:R, 2 + i % 2, c * TR:(c + 1) * TR], ot[:, i, c * R:(c + 1) * R],
                                 ident[0:TR, 0:TR])
                    ins.then_inc(s["mix_t"], 1)
                pe.wait_ge(s["mix_back"], due(g, "mix_back", NT))
                for c in range(C):
                    for i in range(C):
                        ins = mm(ps[0:R, c, 0:N], w_out[2][:, i, c * R:(c + 1) * R], o[0:R, i, :], start=i == 0,
                                 stop=i == C - 1)
                ins.then_inc(s["proj_done"], 1)

                layernorm(3)
                logits(1)
                for j in here("gate", 3):
                    chunk(j)
                for j in here("rest", 0):
                    chunk(j)
                if gf is not None:
                    finish()

            turn(0, None)
            pe.wait_ge(ld_ffn, 32)
            with pe.Fori(1, NG) as g:
                turn(g, g - 1)
            turn(None, NG - 1)


SHIFTS = [(0, 0), (0, -1), (0, 1), (-1, 0), (1, 0)]


def chunked(w):
    return w.reshape(C, R, -1).transpose(1, 0, 2)


def with_bias(w, bias):
    out = np.zeros((R + 1, C, w.shape[1]), w.dtype)
    out[:R] = chunked(w)
    if bias is not None:
        out[R, 0] = bias
    return out


def padded_rows(w):
    out = np.zeros((4, SL, 3, D), w.dtype)
    out[:, :HD] = w.reshape(3, 4, HD, D).transpose(1, 2, 0, 3)
    return out.reshape(128, 3, D)


def layout(i):
    f = {}
    x = i["x"]
    xp = np.zeros((B, 66, 66, 3), x.dtype)
    xp[:, 1:65, 1:65] = x
    win = np.stack([xp[:, 16 * r:16 * r + 18, 16 * c:16 * c + 18] for r in range(4) for c in range(4)], 1)
    f["win"] = win.reshape(NI, NH, HP).transpose(2, 1, 0)
    per_feature = {"wtok": (i["L0_tok_W"], D), "g": (i["L0_tok_gamma"], 1), "be": (i["L0_tok_beta"], 1)}
    for name, (v, n) in per_feature.items():
        v = v.reshape(16, 16, 5, 3, n)
        placed = np.zeros((5, 18, 18, 3, n), v.dtype)
        for sh, (di, dj) in enumerate(SHIFTS):
            placed[sh, 1 + di:17 + di, 1 + dj:17 + dj] = v[:, :, sh]
        f[name] = placed.reshape(5, NH, HP, n).transpose(0, 2, 1, 3)
    f["gtok"] = np.stack([f.pop("g")[..., 0], f.pop("be")[..., 0]], 0).transpose(2, 0, 1, 3)
    occurs = np.zeros((18, 18, 3), np.float32)
    for di, dj in SHIFTS:
        occurs[1 + di:17 + di, 1 + dj:17 + dj] += np.float32(1.0 / (16 * 16 * 15))
    f["mult"] = occurs.reshape(NH, HP).T
    f["btok"] = i["L0_tok_b"].reshape(C, R).T
    txt = np.zeros((B + G, D, TT), i["txt"].dtype)
    txt[:B] = i["txt"].transpose(0, 2, 1)
    f["txt"] = txt.reshape(B + G, C, R, TT).transpose(0, 2, 1, 3)
    wa, ba = i["L0_attn_w_attn"].T, i["L0_attn_b_attn"]
    kqv = lambda v: np.concatenate([v[..., D:2 * D], v[..., 0:D], v[..., 2 * D:]], -1)
    f["w_qkv0"] = with_bias(kqv(wa), kqv(ba))
    f["w_qkv1"] = with_bias(i["L0_ffn_W_qkv"].T, i["L0_ffn_b_qkv"])
    f["w_qkv2"] = with_bias(i["L1_attn_W_attn"].T, None)
    f["w_out0"] = padded_rows(i["L0_attn_w_proj"].T)
    f["w_out1"] = padded_rows(i["L0_ffn_W_proj"].T)
    f["w_out2"] = chunked(i["L1_attn_W_out"].T)
    b_out = np.zeros((3, D), np.float32)
    b_out[0], b_out[1] = i["L0_attn_b_proj"], i["L0_ffn_b_proj"]
    f["b_out"] = b_out.reshape(3, C, R).transpose(2, 0, 1)
    f["lam"] = np.broadcast_to(np.stack([i[f"L1_attn_lambda_{n}"] for n in ("q1", "k1", "q2", "k2")]),
                               (TR, 4, HD // 2))
    f["w_gate"] = np.stack([with_bias(i["L0_ffn_W_gate"].T, i["L0_ffn_b_gate"]),
                            with_bias(i["L1_ffn_w_router"].T, None)], 1)
    f["lora_a"] = chunked(i["L0_ffn_A"].reshape(NE * RANK, D).T)
    f["lora_b"] = i["L0_ffn_B_lora"].transpose(0, 2, 1).reshape(NE * RANK, 3 * D)
    f["e_bias"] = np.broadcast_to(i["L1_ffn_expert_bias"], (TR, NT, NE))
    wide = lambda e, sh: chunked(np.concatenate([e.reshape(NE * FE, D), sh], 0).T)
    f["wgu"] = np.stack([wide(i["L1_ffn_Wg"], i["L1_ffn_sg"]), wide(i["L1_ffn_Wu"], i["L1_ffn_su"])], 1)
    wd = np.concatenate([i["L1_ffn_Wd"].transpose(0, 2, 1).reshape(NE * FE, D), i["L1_ffn_sd"].T], 0)
    f["wdn"] = wd.reshape(NJ, 128, D).transpose(1, 0, 2)
    f["ident"] = np.eye(128, dtype=np.float32)
    causal = np.where(np.arange(T)[None, :] > np.arange(T)[:, None], MASKED, 0.0).astype(np.float32)
    masks = np.zeros((128, 2, T), np.float32)
    masks[:, 0] = causal[:128]
    masks[:R, 1] = np.tile(causal[128:], (HC, 1))
    f["masks"] = masks.reshape(128, 2 * T)
    rows = np.arange(R)
    f["head_q"] = np.equal(rows[:, None] // HD, np.arange(HC)[None, :]).astype(np.float32)
    f["head_k"] = np.equal(rows[:, None] % HC, np.arange(HC)[None, :]).astype(np.float32)
    f["col_i"] = np.equal(rows[:, None] % TB, np.arange(TB)[None, :]).astype(np.float32)
    f["before"] = np.broadcast_to(np.tril(np.ones((NE, NE), np.float32), -1), (TR, NT, NE, NE))
    return {n: np.ascontiguousarray(v) for n, v in f.items()}


def kernel(**inputs):
    import concourse.bacc as bacc
    from concourse.bass_utils import run_bass_kernel_spmd

    nc = bacc.Bacc("TRN2", target_bir_lowering=False, num_devices=1)
    arrays, aps = {}, {}
    for name, v in layout({n: np.asarray(v) for n, v in inputs.items()}).items():
        arrays[f"in_{name}"] = v
        aps[name] = nc.dram_tensor(f"in_{name}", v.shape, mybir.dt.from_np(v.dtype), kind="ExternalInput").ap()
    out = nc.dram_tensor("out", (B, R, C, T), F32, kind="ExternalOutput").ap()
    program(nc, aps, out)
    got = run_bass_kernel_spmd(nc, [arrays], core_ids=[0]).results[0]["out"]
    return got.transpose(0, 3, 2, 1).reshape(B, T, D)
```

```python
import math
from contextlib import ExitStack

import numpy as np

import concourse.bass as bass
from concourse import mybir

F32 = mybir.dt.float32
I32 = mybir.dt.int32
BF16 = mybir.dt.bfloat16
ALU = mybir.AluOpType
ACT = mybir.ActivationFunctionType
X = mybir.AxisListType.X

B, TI, TT, D, H = 16, 16, 128, 192, 12
T = TI + TT
HD = D // H
C, R = 2, 96
HC = H // C
G = 2
NG = B // G
N = G * T
TB = T - 128
SL = 32
NE, FE, RANK = 8, 384, 16
NJ = (NE + 1) * FE // 128
JE = FE // 128
NH = 9
HP = 2 * 18 * 3
NI = B * TI
EPS, EPS_TOK = 1e-5, 1e-3
MAGIC = float(0x5F3759DF)
LAMBDA_INIT = 0.8 - 0.6 * math.exp(-0.3 * 12)
MASKED = -2.0 ** 100

PASSES = [(0, 0), (0, 1), (1, 0), (1, 1)]
QSCALE = [2 * HD ** -0.5, HD ** -0.5, (HD // 2) ** -0.5]
FIRST_PASS = [0, 2, 4]
NT, TR = 3, 96
GROUP_CHUNKS = [(0, 0), (1, 0), (1, 1), (2, 1)]

ORDER, ORDER_B = [1, 2, 4, 5], 3

PER = dict(
    txt_in=32, h_ready=8, mean_done=4, xc_done=4, sq_done=4, var_done=4, rsqrt_step=44, spread_done=4, y_ready=4, yrep_ready=4,
    qk_done=4, q_ready=2, k_ready=2, kbd=2 * HC * 16, qbd_ready=4, v_done=4, v_ready=12,
    s_done=20, max_ready=20, exp_done=20, norm_step=16, lb_ready=4, t_done=24, pt_dve=16, pt_act=16,
    pv_done=4, o_ready=4, proj_done=3,
    mix_proj=NT, mix_copied=NT, mix_step=8 * NT + 1, mix_prod=NT - 1, mix_sub=NT, mix_exp=NT, mix_out=NT, mix_t=NT, mix_back=NT,
    logits_done=2, gate_sub=2, gate_exp=2, gate_step=24, gate_ready=2, disp_done=1, disp_sb=1, ad_ready=3,
    handed=3, comb_done=8, comb_sb=8, ye_ready=9, gate_up=2 * NJ, tanh_done=NJ, half_done=NJ, hid_done=NJ, down_done=NJ,
    out_ready=1, out_dma=32,
)
UNITS = 3 * NJ
FILL = dict(norm_mean=(0, 3, 3, 2), norm_var=(3, 3, 3, 3), norm_y=(0, 0, 0, 0), gate=(0, 5, 0, 0), kv=(3, 1),
            keys=(5, 3), scores=(1, 1), t0=(0, 0, 1, 0), t1=(3, 2, 2, 2), t2=(1, 0, 0, 1), t3=(1, 1, 0, 4),
            x0=(0, 2, 0, 0), x1=(2, 0, 0, 0), x2=(0, 0, 0, 1), mix0=(2, 0, 2), mix1=(0, 4, 3), mix2=(1, 2, 3),
            mix3=(2, 0, 2))


def units_at():
    order = []
    for l in range(4):
        order += [("norm_mean", l), ("norm_var", l), ("norm_y", l)] + [("gate", l)] * (l in (1, 3))
        if l < 2:
            order += [("kv", l), ("keys", l)]
            for u in range(FIRST_PASS[l], FIRST_PASS[l + 1]):
                order += [("scores", l)] * (u == FIRST_PASS[l])
                order += [(point, u) for point in ("t0", "t1", "t2", "t3", "x0", "x1", "x2")]
        if l == 2:
            order += [(f"mix{n}", i) for i in range(NT) for n in range(4)]
    where, first = {}, 0
    for point, k in order:
        last = min(UNITS, first + FILL[point][k])
        where[point, k] = range(first, last)
        first = last
    where["rest", 0] = range(first, UNITS)
    return where


UNITS_AT = units_at()
DVE_CENTRED, DVE_LAMBDA = 1, 12
PE_MEAN, PE_VAR, PE_BETA, PE_TOK = 1, 4, (2, 3, 5, 6, 7), 8


def dve_block_used(i):
    return 2 if i == 0 else 2 * i + 1


def program(nc, a, out):
    ctx = ExitStack()
    with ctx:
        def sb(name, shape, dt=F32):
            return ctx.enter_context(nc.sbuf_tensor(name, shape, dt))

        def sem(name):
            return ctx.enter_context(nc.semaphore(name))

        def full(t):
            return t[tuple(slice(None) for _ in t.shape)]

        w_qkv = [sb(f"w_qkv{l}", [R + 1, C, 3 * D]) for l in range(3)]
        w_out = [sb("w_out0", [128, 3, D]), sb("w_out1", [128, 3, D]), sb("w_out2", [R, C, D])]
        b_out = sb("b_out", [R, 3, C])
        w_gate = sb("w_gate", [R + 1, 2, C, NE])
        lora_a = sb("lora_a", [R, C, NE * RANK])
        lora_b = sb("lora_b", [NE * RANK, 3 * D])
        e_bias = sb("e_bias", [TR, NT, NE])
        lam = sb("lam", [TR, 4, HD // 2])
        ident = sb("ident", [128, 128])
        ident_bf = sb("ident_bf", [128, 128], BF16)
        mask_a = sb("mask_a", [128, T], BF16)
        mask_b = sb("mask_b", [R, T], BF16)
        head_q = sb("head_q", [R, HC])
        head_k = sb("head_k", [R, HC])
        col_i = sb("col_i", [R, TB])
        before = sb("before", [TR, NT, NE, NE])
        ones_d = sb("ones_d", [R, R])
        wgu = sb("wgu", [R, 2, C, NJ * 128])
        wdn = sb("wdn", [128, NJ, D])
        coef = sb("coef", [TR, 2 * H])
        img = sb("img", [R, C, NI])

        hin = sb("hin", [R, G, C, TT])
        h = sb("h", [R, C, N])
        xc = sb("xc", [R, C, N])
        y = sb("y", [R + 1, C, N])
        yrep = sb("yrep", [R + 1, C, G, TB, HC])
        var = sb("var", [TR, NT])
        rs = sb("rs", [TR, NT])
        rt = sb("rt", [TR, NT])
        qk = sb("qk", [R, H * H * HD])
        q, k = (qk[:, n * C * N:(n + 1) * C * N].rearrange("p (c n) -> p c n", c=C) for n in range(2))
        qbd = sb("qbd", [R, 2, C, HC, TB])
        va = sb("va", [128, G, H, SL])
        vb = sb("vb", [R, G, C, 8, SL])
        nmax = sb("nmax", [128, 2, H])
        nmax_b = sb("nmax_b", [R, 2, C])
        sums = sb("sums", [128, 2, H])
        sums_b = sb("sums_b", [R, 2, C])
        inv = sb("inv", [128, H])
        inv_b = sb("inv_b", [R, C])
        pb = sb("pb", [R, 2, C, T])
        lb = sb("lb", [R, C, TB, HC])
        inv_x = sb("inv_x", [128, H, SL])
        rbc = sb("rbc", [128, 3, T])
        ptk = sb("ptk", [R, C, T])
        o = sb("o", [128, 3, N])
        mix_m = sb("mix_m", [TR, 2 * H])
        ge = sb("ge", [TR, NT, NE])
        gp = sb("gp", [TR, NT, NE])
        gs = sb("gs", [TR, NT, NE])
        gm = sb("gm", [TR, NT])
        cmp1 = sb("cmp1", [TR, NT, NE, NE])
        cmp2 = sb("cmp2", [TR, NT, NE, NE])
        comb = sb("comb", [TR, NT, NE])
        disp_x = sb("disp_x", [TR, NT, NE, RANK])
        disp_s = sb("disp_s", [128, N])
        ad = sb("ad", [128, N])
        adrep = sb("adrep", [128, G, TB, HC])
        obuf = sb("obuf", [R, C, N])
        sq = o[0:R, 0:C, :]

        work = sb("work", [128, 12096])

        def part(rows, first, pattern=None, **sizes):
            n = math.prod(sizes.values())
            v = work[0:rows, first:first + n]
            names = list(sizes)
            return v.rearrange(f"p ({' '.join(names)}) -> p {' '.join(names)}", **sizes) if len(names) > 1 else v

        win = part(HP, 0, k=NH, n=NI)
        win_sq = part(HP, 2304, k=NH, n=NI)
        wtok = part(HP, 4608, s=2, k=NH, d=D)
        weff = part(HP, 8064, k=NH, d=D)
        wtmp = part(HP, 9792, k=NH, d=D)
        kbd = part(R, 0, c=C, j=HC, n=N)
        comb_bc = part(R, 3456, e=NE, n=N)
        ye = part(R, 5760, s=2, c=C, n=N)
        prod = [part(TR, 6912, n=2304), qk[:, :]]
        ot = part(TR, 9216, t=NT, d=D)
        mix = part(TR, 9792, s=2, a=H, b=H)
        qkvt = part(TR, 10368, t=NT, n=3, d=D)
        pa = part(128, 6912, s=2, c=C, t=T, j=HC)
        pt = part(128, 10368, h=H, t=T)
        hid = sb("hid", [128, 3, N])
        half = sb("half", [R, 1])
        yf = sb("yf", [R, C, N])
        hf = sb("hf", [R, C, N])
        combf = sb("combf", [TR, NT, NE])
        gtok = sb("gtok", [HP, 2, 5, NH])
        mult = sb("mult", [HP, NH])
        btok = sb("btok", [R, C])
        c0 = sb("c0", [R, C])

        ps = ctx.enter_context(nc.psum_tensor("ps", [128, 8, 512], F32))

        s = {name: sem(name) for name in PER}
        ld_tok, ld_w = sem("ld_tok"), [sem(f"ld_wtok{i}") for i in range(5)]
        ld_small, ld_ffn, ready, stored = sem("ld_small"), sem("ld_ffn"), sem("ready"), sem("stored")
        constants_set = sem("constants_set")
        t_pe, t_dve, t_act = sem("t_pe"), sem("t_dve"), sem("t_act")

        small = [(w_qkv[l], f"w_qkv{l}") for l in range(3)] + [(w_out[l], f"w_out{l}") for l in range(3)]
        small += [(b_out, "b_out"), (w_gate, "w_gate"), (lora_a, "lora_a"), (lora_b, "lora_b"), (e_bias, "e_bias"),
                  (lam, "lam"), (ident, "ident"), (disp_s, "masks"),
                  (head_q, "head_q"), (head_k, "head_k"), (col_i, "col_i"), (before, "before")]
        tok = [(win, "win"), (full(mult), "mult"), (full(gtok), "gtok"), (full(btok), "btok")]

        def due(g, name, n):
            return g * PER[name] + n

        def banks(j, alone):
            return (0, 1) if alone and j % 2 else (4, 5)

        def all_pairs(multiply, i):
            qh, kh = (qkvt[:, i, n, :].rearrange("p (h d) -> p h d", h=H) for n in range(2))
            half_d = HD // 2
            size = H * H * half_d
            for n in range(2):
                d = slice(n * half_d, (n + 1) * half_d)
                shape = [TR, H, H, half_d]
                ins = multiply(prod[i % 2][:, n * size:(n + 1) * size].rearrange("p (a b d) -> p a b d", a=H, b=H),
                               qh[:, :, d].unsqueeze(2).to_broadcast(shape),
                               kh[:, :, d].unsqueeze(1).to_broadcast(shape), ALU.mult)
            return ins

        block = ctx.enter_context(nc.Block())

        @block.sync
        def _(sp):
            for t, n in tok:
                sp.dma_start(t, a[n]).then_inc(ld_tok, 16)
            for i in range(5):
                if i >= 2:
                    sp.wait_ge(t_dve, dve_block_used(i - 2))
                    sp.wait_ge(t_pe, PE_BETA[i - 2])
                sp.dma_start(wtok[:, i % 2], a["wtok"][i]).then_inc(ld_w[i], 16)
            for t, n in small:
                sp.dma_start(full(t), a[n]).then_inc(ld_small, 16)
            sp.dma_start(full(wgu), a["wgu"]).then_inc(ld_ffn, 16)
            sp.dma_start(full(wdn), a["wdn"]).then_inc(ld_ffn, 16)
            sp.wait_ge(ready, 1)

            def keys(g):
                for l in range(2):
                    sp.wait_ge(s["k_ready"], due(g, "k_ready", l + 1))
                    for j in range(HC):
                        rows = slice(HD * j, HD * (j + 1))
                        sp.dma_start(kbd[rows, :, j, :], k[rows, :, :]).then_inc(s["kbd"], 16)

            def store(g):
                sp.wait_ge(s["out_ready"], due(g, "out_ready", 2))
                for b in range(G):
                    sp.dma_start(out[bass.ds(g * G + b, 1)].rearrange("o r c n -> (o r) c n"),
                                 obuf[:, :, b * T:(b + 1) * T]).then_inc(s["out_dma"], 16)
                sp.wait_ge(s["out_dma"], due(g, "out_dma", PER["out_dma"]))
                sp.sem_inc(stored, 1)

            keys(0)
            with sp.Fori(1, NG) as g:
                keys(g)
                store(g - 1)
            store(NG - 1)

        @block.gpsimd
        def _(pool):
            def load_text(g):
                for b in range(G):
                    pool.dma_start(hin[:, b], a["txt"][bass.ds(g * G + b, 1)].rearrange("o r c n -> (o r) c n"))\
                        .then_inc(s["txt_in"], 16)

            nc.gpsimd.memset(full(va), 0.0)
            nc.gpsimd.memset(full(vb), 0.0)
            nc.gpsimd.memset(rbc[:, :, 128:T], 1.0)
            nc.gpsimd.memset(full(y), 1.0)
            nc.gpsimd.memset(full(ones_d), 1.0 / D)
            nc.gpsimd.memset(full(half), 0.5).then_inc(constants_set, 1)
            load_text(0)
            pool.wait_ge(t_pe, PE_TOK)
            nc.gpsimd.memset(kbd, 0.0).then_inc(ready, 1)
            pool.wait_ge(ld_small, 16 * len(small))

            def turn(g, gf):

                def expert_input(e):
                    if e >= 2:
                        pool.wait_ge(s["gate_up"], due(gf, "gate_up", 2 * JE * (e - 1)))
                    if e == NE:
                        pool.wait_ge(s["handed"], due(gf, "handed", 3))
                        for c in range(C):
                            ins = nc.gpsimd.tensor_tensor(ye[:, e % 2, c], yf[:, c], half[:, :].to_broadcast([R, N]),
                                                          ALU.mult)
                    else:
                        pool.wait_ge(s["comb_sb"], due(gf, "comb_sb", e + 1))
                        for c in range(C):
                            ins = nc.gpsimd.tensor_tensor(ye[:, e % 2, c], yf[:, c], comb_bc[:, e], ALU.mult)
                    ins.then_inc(s["ye_ready"], 1)

                def unit(n):
                    if n % (3 * JE) == 0 and n // (3 * JE) < NE:
                        expert_input(n // (3 * JE) + 1)

                if gf is not None:
                    expert_input(0)

                def here(point, k):
                    return UNITS_AT[point, k] if gf is not None else ()

                if g is None:
                    for n in range(UNITS):
                        unit(n)
                    return
                def queries_b(u):
                    l, b = PASSES[u]
                    pool.wait_ge(s["q_ready"], due(g, "q_ready", l + 1))
                    if u >= 2:
                        pool.wait_ge(s["s_done"], due(g, "s_done", 5 * (u - 1)))
                    for c in range(C):
                        ins = nc.gpsimd.tensor_tensor(
                            qbd[:, u % 2, c], q[:, c, b * T + 128:(b + 1) * T].unsqueeze(1).to_broadcast([R, HC, TB]),
                            head_q[:, :].unsqueeze(2).to_broadcast([R, HC, TB]), ALU.mult)
                    ins.then_inc(s["qbd_ready"], 1)

                def probs_b(u):
                    pool.wait_ge(s["norm_step"], due(g, "norm_step", 4 * u + 3))
                    for c in range(C):
                        ins = nc.gpsimd.tensor_tensor(
                            lb[:, c], pb[:, u % 2, c, 128:T].unsqueeze(2).to_broadcast([R, TB, HC]),
                            head_q[:, :].unsqueeze(1).to_broadcast([R, TB, HC]), ALU.mult)
                    ins.then_inc(s["lb_ready"], 1)

                def head_products(i):
                    pool.wait_ge(s["mix_copied"], due(g, "mix_copied", i + 1))
                    if i >= 2:
                        pool.wait_ge(s["mix_out"], due(g, "mix_out", i - 1))
                    all_pairs(nc.gpsimd.tensor_tensor, i).then_inc(s["mix_prod"], 1)

                for l in range(2):
                    for n in here("norm_mean", l):
                        unit(n)
                    for n in here("norm_var", l):
                        unit(n)
                    for n in here("norm_y", l):
                        unit(n)
                    if l == 1:
                        for n in here("gate", 1):
                            unit(n)
                    for n in here("kv", l):
                        unit(n)
                    for n in here("keys", l):
                        unit(n)
                    first, last = FIRST_PASS[l], FIRST_PASS[l + 1]
                    queries_b(first)
                    if l == 0:
                        pool.wait_ge(s["h_ready"], due(g, "h_ready", 2))
                        load_text(g + 1)
                    for u in range(first, last):
                        if u == first:
                            for n in here("scores", l):
                                unit(n)
                        for n in here("t0", u):
                            unit(n)
                        for n in here("t1", u):
                            unit(n)
                        for n in here("t2", u):
                            unit(n)
                        if u + 1 < last:
                            queries_b(u + 1)
                        for n in here("t3", u):
                            unit(n)
                        for n in here("x0", u):
                            unit(n)
                        probs_b(u)
                        for n in here("x1", u):
                            unit(n)
                        for n in here("x2", u):
                            unit(n)
                for l in (2, 3):
                    for point in ("norm_mean", "norm_var", "norm_y"):
                        for n in here(point, l):
                            unit(n)
                    if l == 2:
                        head_products(1)
                    for i in range(NT if l == 2 else 0):
                        if i == 1:
                            head_products(2)
                        for m in range(4):
                            for n in here(f"mix{m}", i):
                                unit(n)
                for n in here("gate", 3):
                    unit(n)
                for n in here("rest", 0):
                    unit(n)

            turn(0, None)
            with pool.Fori(1, NG) as g:
                turn(g, g - 1)
            turn(None, NG - 1)

        @block.scalar
        def _(act):
            fn = nc.scalar.activation
            act.wait_ge(t_dve, DVE_CENTRED)
            fn(win_sq, win, ACT.Square).then_inc(t_act, 1)
            act.wait_ge(t_dve, DVE_LAMBDA)
            fn(gm[:, 0:2], gm[:, 0:2], ACT.Exp).then_inc(t_act, 1)

            def turn(g, gf):
                alone = g is None

                def spread_weights():
                    for e in range(NE):
                        act.wait_ge(s["comb_done"], due(gf, "comb_done", e + 1))
                        nc.scalar.copy(comb_bc[:, e], ps[0:R, 4 + e % 4, 0:N]).then_inc(s["comb_sb"], 1)

                def unit(n):
                    j = n // 3
                    if n % 3:
                        return
                    act.wait_ge(s["gate_up"], due(gf, "gate_up", 2 * j + 1))
                    if j >= 3:
                        act.wait_ge(s["down_done"], due(gf, "down_done", j - 2))
                    fn(hid[:, j % 3], ps[:, banks(j, alone)[0], 0:N], ACT.Tanh, scale=0.5)\
                        .then_inc(s["tanh_done"], 1)

                def here(point, k):
                    return UNITS_AT[point, k] if gf is not None else ()

                if alone:
                    spread_weights()
                    for n in range(UNITS):
                        unit(n)
                    return

                def square(l):
                    act.wait_ge(s["xc_done"], due(g, "xc_done", l + 1))
                    fn(sq, full(xc), ACT.Square).then_inc(s["sq_done"], 1)
                    if l == 0 and gf is not None:
                        spread_weights()
                    for n in here("norm_mean", l):
                        unit(n)
                    for n in here("norm_var", l):
                        unit(n)
                    for n in here("norm_y", l):
                        unit(n)

                def gate_exp(n):
                    act.wait_ge(s["gate_sub"], due(g, "gate_sub", n + 1))
                    fn(full(ge), full(ge), ACT.Exp).then_inc(s["gate_exp"], 1)

                def exp_a(u, i):
                    act.wait_ge(s["max_ready"], due(g, "max_ready", 5 * u + ORDER[i]))
                    if i == 0 and u >= 2:
                        act.wait_ge(s["t_done"], due(g, "t_done", 6 * (u - 1)))
                    for hh in range(3 * i, 3 * i + 3):
                        ins = fn(pa[:, u % 2, hh // HC, :, hh % HC], ps[:, i % 2, (hh % 3) * T:(hh % 3 + 1) * T],
                                 ACT.Exp, bias=nmax[:, u % 2, hh:hh + 1], accum_out=sums[:, u % 2, hh:hh + 1])
                    ins.then_inc(s["exp_done"], 1)

                def exp_b(u):
                    act.wait_ge(s["max_ready"], due(g, "max_ready", 5 * u + ORDER_B))
                    for c in range(C):
                        ins = fn(pb[:, u % 2, c, :], ps[0:R, 3, c * T:(c + 1) * T], ACT.Exp,
                                 bias=nmax_b[:, u % 2, c:c + 1], accum_out=sums_b[:, u % 2, c:c + 1])
                    ins.then_inc(s["exp_done"], 1)

                def transposed(u, i):
                    act.wait_ge(s["t_done"], due(g, "t_done", 6 * u + i + 1))
                    nc.scalar.copy(pt[:, 3 * i:3 * i + 3, 0:128], ps[:, 2, 0:384].rearrange("p (h n) -> p h n", h=3))\
                        .then_inc(s["pt_act"], 1)

                for l in range(2):
                    square(l)
                    if l == 1:
                        gate_exp(0)
                        for n in here("gate", 1):
                            unit(n)
                        act.wait_ge(s["disp_done"], due(g, "disp_done", 1))
                        nc.scalar.copy(full(disp_s), ps[:, 3, 32:32 + N]).then_inc(s["disp_sb"], 1)
                    act.wait_ge(s["qk_done"], due(g, "qk_done", 2 * l + 1))
                    nc.scalar.mul(q, ps[0:R, 0:2, 0:N], QSCALE[l]).then_inc(s["q_ready"], 1)
                    for n in here("kv", l):
                        unit(n)
                    for n in here("keys", l):
                        unit(n)
                    first, last = FIRST_PASS[l], FIRST_PASS[l + 1]
                    for u in range(first, last):
                        if u == first:
                            exp_a(u, 0)
                            exp_a(u, 1)
                            exp_b(u)
                            for n in here("scores", l):
                                unit(n)
                        exp_a(u, 2)
                        for n in here("t0", u):
                            unit(n)
                        transposed(u, 1)
                        exp_a(u, 3)
                        for n in here("t1", u):
                            unit(n)
                        for n in here("t2", u):
                            unit(n)
                        transposed(u, 3)
                        if u + 1 < last:
                            exp_a(u + 1, 0)
                            exp_a(u + 1, 1)
                        for n in here("t3", u):
                            unit(n)
                        for n in here("x0", u):
                            unit(n)
                        act.wait_ge(s["t_done"], due(g, "t_done", 6 * u + 6))
                        nc.scalar.copy(ptk[:, :, 128:T], ps[0:R, 2, 384:416].rearrange("p (c n) -> p c n", c=C))\
                            .then_inc(s["pt_act"], 1)
                        nc.scalar.copy(rbc[:, :, 0:128], ps[:, 2, 0:384].rearrange("p (g n) -> p g n", g=3))\
                            .then_inc(s["pt_act"], 1)
                        for n in here("x1", u):
                            unit(n)
                        for n in here("x2", u):
                            unit(n)
                        if u + 1 < last:
                            exp_b(u + 1)
                square(2)
                for i in range(NT):
                    act.wait_ge(s["mix_proj"], due(g, "mix_proj", i + 1))
                    b0 = 2 * (i % 2)
                    nc.scalar.mul(qkvt[:, i, 0, :], ps[0:TR, b0, 0:D], QSCALE[2])
                    nc.scalar.copy(qkvt[:, i, 1, :], ps[0:TR, b0, D:2 * D])
                    nc.scalar.copy(qkvt[:, i, 2, :], ps[0:TR, b0 + 1, 0:D]).then_inc(s["mix_copied"], 1)
                for i in range(NT):
                    for n in here("mix0", i):
                        unit(n)
                    act.wait_ge(s["mix_sub"], due(g, "mix_sub", i + 1))
                    fn(mix, mix, ACT.Exp).then_inc(s["mix_exp"], 1)
                    for n in here("mix1", i):
                        unit(n)
                    for n in here("mix2", i):
                        unit(n)
                    for n in here("mix3", i):
                        unit(n)
                    act.wait_ge(s["mix_t"], due(g, "mix_t", i + 1))
                    nc.scalar.copy(o[0:R, 0:C, i * TR:(i + 1) * TR],
                                   ps[0:R, 2 + i % 2, 0:C * TR].rearrange("p (c n) -> p c n", c=C))\
                        .then_inc(s["mix_back"], 1)
                square(3)
                gate_exp(1)
                for n in here("gate", 3):
                    unit(n)
                for n in here("rest", 0):
                    unit(n)

            turn(0, None)
            with act.Fori(1, NG) as g:
                turn(g, g - 1)
            turn(None, NG - 1)

        @block.vector
        def _(dve):
            tt, ts, stt = nc.vector.tensor_tensor, nc.vector.tensor_scalar, nc.vector.scalar_tensor_tensor
            cp, red, rec = nc.vector.tensor_copy, nc.vector.tensor_reduce, nc.vector.reciprocal
            count = [0]

            def link(ins):
                count[0] += 1
                ins.then_inc(t_dve, 1)
                dve.wait_ge(t_dve, count[0])

            def rsqrt(src, eps, v, r, t, mark):
                mark(ts(v, src, eps, None, ALU.add))
                mark(ts(r.bitcast(I32), v.bitcast(I32), -0.5, MAGIC, ALU.mult, ALU.add))
                for _ in range(3):
                    mark(stt(t, r, -0.5, r, ALU.mult, ALU.mult))
                    mark(tt(t, t, v, ALU.mult))
                    mark(stt(r, t, 1.5, r, ALU.add, ALU.mult))

            dve.wait_ge(ld_tok, 16 * len(tok))
            dve.wait_ge(t_pe, PE_MEAN)
            link(tt(win, win, ps[0:HP, 0, 0:NI].unsqueeze(1).to_broadcast([HP, NH, NI]), ALU.subtract))
            assert count[0] == DVE_CENTRED
            for i in range(5):
                dve.wait_ge(ld_w[i], 16)
                gamma = gtok[:, 0, i, :].unsqueeze(2).to_broadcast([HP, NH, D])
                link(tt(weff if i == 0 else wtmp, wtok[:, i % 2], gamma, ALU.mult))
                assert count[0] == dve_block_used(i)
                if i:
                    link(tt(weff, weff, wtmp, ALU.add))
            dve.wait_ge(ld_small, 16 * len(small))
            link(tt(cmp1[:, 0, 0:2, :], lam[:, 0:4:2, :], lam[:, 1:4:2, :], ALU.mult))
            link(red(gm[:, 0:2], cmp1[:, 0, 0:2, :], X, ALU.add))
            assert count[0] == DVE_LAMBDA
            dve.wait_ge(t_act, 2)
            link(tt(gm[:, 2:3], gm[:, 0:1], gm[:, 1:2], ALU.subtract))
            link(ts(coef[:, H:2 * H], gm[:, 2:3].to_broadcast([TR, H]), LAMBDA_INIT, -(1.0 - LAMBDA_INIT),
                    ALU.add, ALU.mult))
            link(nc.vector.memset(coef[:, 0:H], 1.0 - LAMBDA_INIT))
            link(cp(full(ident_bf), full(ident)))
            link(cp(full(mask_a), disp_s[:, 0:T]))
            link(cp(full(mask_b), disp_s[0:R, T:2 * T]))
            dve.wait_ge(t_pe, PE_VAR)
            rsqrt(ps[0:R, 1, 0:NI], EPS_TOK, q[:, 0, 0:NI], q[:, 1, 0:NI], k[:, 0, 0:NI], link)
            dve.wait_ge(t_pe, PE_BETA[4])
            link(tt(c0[:, :].unsqueeze(2), ps[0:R, 2:4, 0:1], btok[:, :].unsqueeze(2), ALU.add))
            dve.wait_ge(t_pe, PE_TOK)
            link(tt(full(img), ps[0:R, 4:6, 0:NI], q[:, 1, 0:NI].unsqueeze(1).to_broadcast([R, C, NI]), ALU.mult))
            for c in range(C):
                link(ts(img[:, c, :], img[:, c, :], c0[:, c:c + 1], None, ALU.add))
            dve.wait_ge(constants_set, 1)
            dve.sem_inc(s["out_ready"], 1)


            def turn(g, gf):
                alone = g is None
                steps = {"rsqrt_step": 0, "norm_step": 0, "gate_step": 0, "mix_step": 0}

                def stepper(name):
                    def mark(ins):
                        steps[name] += 1
                        ins.then_inc(s[name], 1)
                        dve.wait_ge(s[name], due(g, name, steps[name]))
                    return mark

                def hand_over():
                    cp(full(yf), y[0:R]).then_inc(s["handed"], 1)
                    cp(full(hf), full(h)).then_inc(s["handed"], 1)
                    cp(full(combf), full(comb)).then_inc(s["handed"], 1)
                    dve.wait_ge(s["handed"], due(gf, "handed", 3))

                def unit(n):
                    j = n // 3
                    if n % 3 < 2:
                        return
                    gate, up = banks(j, alone)
                    dve.wait_ge(s["tanh_done"], due(gf, "tanh_done", j + 1))
                    stt(hid[:, j % 3], hid[:, j % 3], 1.0, ps[:, gate, 0:N], ALU.add, ALU.mult)\
                        .then_inc(s["half_done"], 1)
                    dve.wait_ge(s["half_done"], due(gf, "half_done", j + 1))
                    dve.wait_ge(s["gate_up"], due(gf, "gate_up", 2 * j + 2))
                    tt(hid[:, j % 3], hid[:, j % 3], ps[:, up, 0:N], ALU.mult).then_inc(s["hid_done"], 1)

                def finish():
                    dve.wait_ge(s["down_done"], due(gf, "down_done", NJ))
                    if alone:
                        dve.wait_ge(s["out_dma"], due(gf, "out_dma", 0))
                    tt(full(obuf), ps[0:R, 6:8, 0:N], full(hf), ALU.add).then_inc(s["out_ready"], 1)
                    dve.wait_ge(s["out_ready"], due(gf, "out_ready", 2))

                def here(point, k):
                    return UNITS_AT[point, k] if gf is not None else ()

                if gf is not None:
                    dve.wait_ge(s["gate_ready"], due(gf, "gate_ready", 2))
                    hand_over()
                if alone:
                    for n in range(UNITS):
                        unit(n)
                    finish()
                    return

                def layernorm(l):
                    dve.wait_ge(s["h_ready"], due(g, "h_ready", 2 * l + 2))
                    dve.wait_ge(s["mean_done"], due(g, "mean_done", l + 1))
                    tt(full(xc), full(h), ps[0:R, 3, 0:N].unsqueeze(1).to_broadcast([R, C, N]), ALU.subtract)\
                        .then_inc(s["xc_done"], 1)
                    for n in here("norm_mean", l):
                        unit(n)
                    dve.wait_ge(s["var_done"], due(g, "var_done", l + 1))
                    rsqrt(ps[0:TR, 2, 0:NT], EPS, full(var), full(rs), full(rt), stepper("rsqrt_step"))
                    dve.wait_ge(s["spread_done"], due(g, "spread_done", l + 1))
                    dve.wait_ge(s["xc_done"], due(g, "xc_done", l + 1))
                    tt(y[0:R], full(xc), ps[0:R, 2, R:R + N].unsqueeze(1).to_broadcast([R, C, N]), ALU.mult)\
                        .then_inc(s["y_ready"], 1)
                    dve.wait_ge(s["y_ready"], due(g, "y_ready", l + 1))
                    for c in range(C if l < 2 else 0):
                        yb = y[:, c, :].rearrange("p (b n) -> p b n", b=G)[:, :, 128:T]
                        cp(yrep[:, c], yb.unsqueeze(3).to_broadcast([R + 1, G, TB, HC])).then_inc(s["yrep_ready"], 1)
                    for n in here("norm_var", l):
                        unit(n)
                    for n in here("norm_y", l):
                        unit(n)

                def top2(n):
                    mark = stepper("gate_step")
                    dve.wait_ge(s["logits_done"], due(g, "logits_done", n + 1))
                    lg = ps[0:TR, 3, 0:NT * NE].rearrange("p (t e) -> p t e", e=NE)
                    spread = gm[:, :].unsqueeze(2).to_broadcast([TR, NT, NE])
                    mark(red(full(gm), lg, X, ALU.max))
                    tt(full(ge), lg, spread, ALU.subtract).then_inc(s["gate_sub"], 1)
                    dve.wait_ge(s["gate_exp"], due(g, "gate_exp", n + 1))
                    mark(red(full(gm), full(ge), X, ALU.add))
                    mark(rec(full(gm), full(gm)))
                    mark(tt(full(gp), full(ge), spread, ALU.mult))
                    if n == 1:
                        mark(tt(full(gs), full(gp), full(e_bias), ALU.add))
                    sel = gp if n == 0 else gs
                    other = sel[:, :, :].unsqueeze(2).to_broadcast([TR, NT, NE, NE])
                    own = sel[:, :, :].unsqueeze(3).to_broadcast([TR, NT, NE, NE])
                    mark(tt(full(cmp1), other, own, ALU.is_gt))
                    mark(tt(full(cmp2), other, own, ALU.is_equal))
                    mark(tt(full(cmp2), full(cmp2), full(before), ALU.mult))
                    mark(tt(full(cmp1), full(cmp1), full(cmp2), ALU.add))
                    mark(red(full(gs), full(cmp1), X, ALU.add))
                    mark(stt(full(gs), full(gs), 2.0, full(gp), ALU.is_lt, ALU.mult))
                    return mark

                def maxima_a(u, i):
                    dve.wait_ge(s["s_done"], due(g, "s_done", 5 * u + ORDER[i]))
                    red(nmax[:, u % 2, 3 * i:3 * i + 3], ps[:, i % 2, 0:3 * T].rearrange("p (j n) -> p j n", j=3), X,
                        ALU.max, negate=True).then_inc(s["max_ready"], 1)

                def maxima_b(u):
                    dve.wait_ge(s["s_done"], due(g, "s_done", 5 * u + ORDER_B))
                    red(nmax_b[:, u % 2, :], ps[0:R, 3, 0:C * T].rearrange("p (c n) -> p c n", c=C), X, ALU.max,
                        negate=True).then_inc(s["max_ready"], 1)

                def normalise(u):
                    mark = stepper("norm_step")
                    dve.wait_ge(s["exp_done"], due(g, "exp_done", 5 * u + 5))
                    mark(rec(full(inv), sums[:, u % 2, :]))
                    mark(rec(full(inv_b), sums_b[:, u % 2, :]))
                    for c in range(C):
                        p = pb[:, u % 2, c, :]
                        ins = ts(p, p, inv_b[:, c:c + 1], None, ALU.mult)
                    mark(ins)
                    mark(cp(full(inv_x), inv[:, :].unsqueeze(2).to_broadcast([128, H, SL])))

                def transposed_a(u, i):
                    dve.wait_ge(s["t_done"], due(g, "t_done", 6 * u + i + 1))
                    cp(pt[:, 3 * i:3 * i + 3, 0:128], ps[:, 2, 0:384].rearrange("p (h n) -> p h n", h=3))\
                        .then_inc(s["pt_dve"], 1)

                def transposed_b(u):
                    dve.wait_ge(s["t_done"], due(g, "t_done", 6 * u + 5))
                    cp(pt[:, :, 128:T], ps[:, 2, 0:H * TB].rearrange("p (h i) -> p h i", h=H)).then_inc(s["pt_dve"], 1)
                    cp(ptk[:, :, 0:128], ps[0:R, 2, 192:448].rearrange("p (c n) -> p c n", c=C))\
                        .then_inc(s["pt_dve"], 1)

                def output(u):
                    _, b = PASSES[u]
                    dve.wait_ge(s["pv_done"], due(g, "pv_done", u + 1))
                    dve.wait_ge(s["pt_act"], due(g, "pt_act", 4 * u + 4))
                    tt(o[:, :, b * T:(b + 1) * T], ps[:, 3, 0:3 * T].rearrange("p (g n) -> p g n", g=3), full(rbc),
                       ALU.mult).then_inc(s["o_ready"], 1)

                def residual(l):
                    dve.wait_ge(s["proj_done"], due(g, "proj_done", l + 1))
                    for c in range(C):
                        stt(h[:, c, :], ps[0:R, c, 0:N], b_out[:, l, c:c + 1], h[:, c, :], ALU.add, ALU.add)\
                            .then_inc(s["h_ready"], 1)

                def mix_heads(i):
                    mark = stepper("mix_step")
                    dve.wait_ge(s["mix_copied"], due(g, "mix_copied", i + 1))
                    vh = qkvt[:, i, 2, :].rearrange("p (h d) -> p h d", h=H)
                    if i == 0:
                        mark(all_pairs(tt, i))
                    else:
                        dve.wait_ge(s["mix_prod"], due(g, "mix_prod", i))
                    for n in here("mix0", i):
                        unit(n)
                    rows = mix.rearrange("p n a b -> p (n a) b")
                    spread = mix_m[:, :].unsqueeze(2).to_broadcast([TR, 2 * H, H])
                    mark(red(mix.rearrange("p n a b -> p (n a b)"),
                             prod[i % 2].rearrange("p (a d) -> p a d", d=HD // 2), X, ALU.add))
                    mark(red(full(mix_m), rows, X, ALU.max))
                    tt(rows, rows, spread, ALU.subtract).then_inc(s["mix_sub"], 1)
                    for n in here("mix1", i):
                        unit(n)
                    dve.wait_ge(s["mix_exp"], due(g, "mix_exp", i + 1))
                    mark(red(full(mix_m), rows, X, ALU.add))
                    mark(rec(full(mix_m), full(mix_m)))
                    mark(tt(full(mix_m), full(mix_m), full(coef), ALU.mult))
                    mark(tt(rows, rows, spread, ALU.mult))
                    mark(tt(mix[:, 0], mix[:, 0], mix[:, 1], ALU.add))
                    sh = [TR, H, HD, H]
                    mark(tt(prod[i % 2].rearrange("p (a d b) -> p a d b", a=H, d=HD), mix[:, 0].unsqueeze(2).to_broadcast(sh),
                            vh.rearrange("p h d -> p d h").unsqueeze(1).to_broadcast(sh), ALU.mult))
                    for n in here("mix2", i):
                        unit(n)
                    red(ot[:, i, :], prod[i % 2].rearrange("p (a b) -> p a b", b=H), X, ALU.add).then_inc(s["mix_out"], 1)
                    for n in here("mix3", i):
                        unit(n)

                dve.wait_ge(s["txt_in"], due(g, "txt_in", 32))
                hv = h[:, :, :].rearrange("p c (b n) -> p c b n", b=G)
                cp(hv[:, :, :, TI:T], hin[:, :, :, :].rearrange("p b c n -> p c b n")).then_inc(s["h_ready"], 1)
                cp(hv[:, :, :, 0:TI], img[:, :, bass.ds(g * (G * TI), G * TI)].rearrange("p c (b n) -> p c b n", b=G))\
                    .then_inc(s["h_ready"], 1)
                for l in range(2):
                    layernorm(l)
                    if l == 1:
                        mark = top2(0)
                        for n in here("gate", 1):
                            unit(n)
                        ts(full(disp_x), gs[:, :, :].unsqueeze(3).to_broadcast([TR, NT, NE, RANK]), 2.0, None,
                           ALU.mult).then_inc(s["gate_ready"], 1)
                        dve.wait_ge(s["disp_sb"], due(g, "disp_sb", 1))
                        tt(full(ad), full(disp_s), ps[:, 2, 0:N], ALU.mult).then_inc(s["ad_ready"], 1)
                        dve.wait_ge(s["ad_ready"], due(g, "ad_ready", 1))
                        for b in range(G):
                            cp(adrep[:, b], ad[:, b * T + 128:(b + 1) * T].unsqueeze(2).to_broadcast([128, TB, HC]))\
                                .then_inc(s["ad_ready"], 1)
                    dve.wait_ge(s["qk_done"], due(g, "qk_done", 2 * l + 2))
                    cp(k, ps[0:R, 2:4, 0:N]).then_inc(s["k_ready"], 1)
                    for n in here("kv", l):
                        unit(n)
                    for b in range(G):
                        dve.wait_ge(s["v_done"], due(g, "v_done", 2 * l + b + 1))
                        cp(va[:, b, :, 0:HD], ps[:, 2 + b, 0:D].rearrange("p (h d) -> p h d", h=H))\
                            .then_inc(s["v_ready"], 1)
                        for c in range(C):
                            tt(vb[:, b, c, 2 * c:2 * c + HC, 0:HD],
                               ps[0:R, 2 + b, D + c * R:D + (c + 1) * R].rearrange("p (h d) -> p h d", h=HC),
                               head_k[:, :].unsqueeze(2).to_broadcast([R, HC, HD]), ALU.mult).then_inc(s["v_ready"], 1)
                    for n in here("keys", l):
                        unit(n)
                    first, last = FIRST_PASS[l], FIRST_PASS[l + 1]
                    for u in range(first, last):
                        if u == first:
                            maxima_a(u, 0)
                            maxima_a(u, 1)
                            maxima_b(u)
                            for n in here("scores", l):
                                unit(n)
                        transposed_a(u, 0)
                        maxima_a(u, 2)
                        for n in here("t0", u):
                            unit(n)
                        maxima_a(u, 3)
                        for n in here("t1", u):
                            unit(n)
                        transposed_a(u, 2)
                        normalise(u)
                        for n in here("t2", u):
                            unit(n)
                        if u + 1 < last:
                            maxima_a(u + 1, 0)
                            maxima_a(u + 1, 1)
                        for n in here("t3", u):
                            unit(n)
                        transposed_b(u)
                        for n in here("x0", u):
                            unit(n)
                        for n in here("x1", u):
                            unit(n)
                        output(u)
                        for n in here("x2", u):
                            unit(n)
                        if u + 1 < last:
                            maxima_b(u + 1)
                    residual(l)
                layernorm(2)
                for i in range(NT):
                    mix_heads(i)
                residual(2)
                layernorm(3)
                mark = top2(1)
                mark(red(full(gm), full(gs), X, ALU.add))
                mark(ts(full(gm), full(gm), 1e-9, 2.0, ALU.add, ALU.mult))
                mark(rec(full(gm), full(gm)))
                tt(full(comb), full(gs), gm[:, :].unsqueeze(2).to_broadcast([TR, NT, NE]), ALU.mult)\
                    .then_inc(s["gate_ready"], 1)

                for n in here("gate", 3):
                    unit(n)
                for n in here("rest", 0):
                    unit(n)
                if gf is not None:
                    finish()
                assert steps == {x: PER[x] for x in steps}, steps

            turn(0, None)
            with dve.Fori(1, NG) as g:
                turn(g, g - 1)
            turn(None, NG - 1)

        @block.tensor
        def _(pe):
            mm, tr = nc.tensor.matmul, nc.tensor.transpose
            pe.wait_ge(ld_tok, 16 * len(tok))
            for i in range(NH):
                ins = mm(ps[0:HP, 0, 0:NI], mult[:, i:i + 1].to_broadcast([HP, HP]), win[:, i], start=i == 0,
                         stop=i == NH - 1)
            ins.then_inc(t_pe, 1)
            for i in range(5):
                if i == 2:
                    pe.wait_ge(t_act, 1)
                    for kk in range(NH):
                        ins = mm(ps[0:HP, 1, 0:NI], mult[:, kk:kk + 1].to_broadcast([HP, HP]), win_sq[:, kk],
                                 start=kk == 0, stop=kk == NH - 1)
                    ins.then_inc(t_pe, 1)
                pe.wait_ge(ld_w[i], 16)
                for kk in range(NH):
                    for c in range(C):
                        ins = mm(ps[0:R, 2 + c, 0:1], wtok[:, i % 2, kk, c * R:(c + 1) * R], gtok[:, 1, i, kk:kk + 1],
                                 start=i == kk == 0, stop=i == 4 and kk == NH - 1)
                ins.then_inc(t_pe, 1)
            pe.wait_ge(t_dve, dve_block_used(4) + 1)
            for c in range(C):
                for kk in range(NH):
                    ins = mm(ps[0:R, 4 + c, 0:NI], weff[:, kk, c * R:(c + 1) * R], win[:, kk], start=kk == 0,
                             stop=kk == NH - 1)
            ins.then_inc(t_pe, 1)
            pe.wait_ge(constants_set, 1)
            pe.wait_ge(ld_small, 16 * len(small))

            def turn(g, gf):
                alone = g is None

                def expert_weights():
                    pe.wait_ge(s["handed"], due(gf, "handed", 3))
                    for e in range(NE):
                        if e >= 4:
                            pe.wait_ge(s["comb_sb"], due(gf, "comb_sb", e - 3))
                        for i in range(NT):
                            ins = tr(ps[0:R, 4 + e % 4, i * TR:(i + 1) * TR],
                                     combf[:, i, e:e + 1].to_broadcast([TR, R]), ident[0:TR, 0:TR])
                        ins.then_inc(s["comb_done"], 1)
                    pe.wait_ge(s["comb_sb"], due(gf, "comb_sb", NE))

                def hidden(j, n):
                    e = j // JE
                    former = j - 1 if alone else j
                    if n == 0 and former > 0:
                        pe.wait_ge(s["hid_done"], due(gf, "hid_done", former))
                    if n == 1 and j % JE == 0:
                        pe.wait_ge(s["ye_ready"], due(gf, "ye_ready", e + 1))
                    for c in range(C):
                        ins = mm(ps[:, banks(j, alone)[n], 0:N], wgu[:, n, c, j * 128:(j + 1) * 128],
                                 yf[:, c, :] if n == 0 else ye[:, e % 2, c, :], start=c == 0, stop=c == C - 1)
                    ins.then_inc(s["gate_up"], 1)

                def down(j):
                    pe.wait_ge(s["hid_done"], due(gf, "hid_done", j + 1))
                    if j == 0:
                        pe.wait_ge(s["out_ready"], due(gf, "out_ready", 1))
                    for c in range(C):
                        ins = mm(ps[0:R, 6 + c, 0:N], wdn[:, j, c * R:(c + 1) * R], hid[:, j % 3], start=j == 0,
                                 stop=j == NJ - 1)
                    ins.then_inc(s["down_done"], 1)

                def unit(n):
                    if n % 3 < 2:
                        hidden(n // 3, n % 3)
                    elif n > 2:
                        down(n // 3 - 1)

                def finish():
                    down(NJ - 1)

                def here(point, k):
                    return UNITS_AT[point, k] if gf is not None else ()

                if alone:
                    expert_weights()
                    for n in range(UNITS):
                        unit(n)
                    finish()
                    return

                def layernorm(l):
                    pe.wait_ge(s["h_ready"], due(g, "h_ready", 2 * l + 2))
                    for c in range(C):
                        ins = mm(ps[0:R, 3, 0:N], full(ones_d), h[:, c, :], start=c == 0, stop=c == C - 1)
                    ins.then_inc(s["mean_done"], 1)
                    if l == 0 and gf is not None:
                        expert_weights()
                    for n in here("norm_mean", l):
                        unit(n)
                    pe.wait_ge(s["sq_done"], due(g, "sq_done", l + 1))
                    for i in range(NT):
                        for c in range(C):
                            ins = mm(ps[0:TR, 2, i:i + 1], sq[:, c, i * TR:(i + 1) * TR], ones_d[:, 0:1],
                                     start=c == 0, stop=c == C - 1)
                    ins.then_inc(s["var_done"], 1)
                    for n in here("norm_var", l):
                        unit(n)
                    pe.wait_ge(s["rsqrt_step"], due(g, "rsqrt_step", 11 * (l + 1)))
                    for i in range(NT):
                        ins = tr(ps[0:R, 2, R + i * TR:R + (i + 1) * TR], rs[:, i:i + 1].to_broadcast([TR, R]),
                                 ident[0:TR, 0:TR])
                    ins.then_inc(s["spread_done"], 1)
                    for n in here("norm_y", l):
                        unit(n)
                    pe.wait_ge(s["y_ready"], due(g, "y_ready", l + 1))

                def rows(c):
                    return R + 1 if c == 0 else R

                def logits(n):
                    for i in range(NT):
                        for c in range(C):
                            r = rows(c)
                            ins = mm(ps[0:TR, 3, i * NE:(i + 1) * NE], y[0:r, c, i * TR:(i + 1) * TR],
                                     w_gate[0:r, n, c, :], start=c == 0, stop=c == C - 1)
                    ins.then_inc(s["logits_done"], 1)

                def lora_down():
                    for c in range(C):
                        mm(ps[:, 2, 0:N], lora_a[:, c, :], y[0:R, c, :], start=c == 0, stop=c == C - 1)
                    for n in here("gate", 1):
                        unit(n)
                    pe.wait_ge(s["gate_ready"], due(g, "gate_ready", 1))
                    for i in range(NT):
                        ins = tr(ps[:, 3, 32 + i * TR:32 + (i + 1) * TR],
                                 disp_x[:, i, :, :].rearrange("p e r -> p (e r)"), ident[0:TR, 0:TR])
                    ins.then_inc(s["disp_done"], 1)
                    pe.wait_ge(s["ad_ready"], due(g, "ad_ready", 3))

                def projections(l):
                    lora = l == 1
                    for n in range(2):
                        for c in range(C):
                            cols = slice(n * D + c * R, n * D + (c + 1) * R)
                            for i in range(C):
                                r = rows(i)
                                ins = mm(ps[0:R, 2 * n + c, 0:N], w_qkv[l][0:r, i, cols], y[0:r, i, :], start=i == 0,
                                         stop=i == C - 1 and not lora)
                            if lora:
                                ins = mm(ps[0:R, 2 * n + c, 0:N], lora_b[:, cols], full(ad), start=False, stop=True)
                        ins.then_inc(s["qk_done"], 1)
                    for n in here("kv", l):
                        unit(n)
                    pe.wait_ge(s["yrep_ready"], due(g, "yrep_ready", 2 * l + 2))
                    pe.wait_ge(s["k_ready"], due(g, "k_ready", l + 1))
                    for b in range(G):
                        for m, lhs, lhs_ad, col in (
                                (128, lambda i, r: y[0:r, i, b * T:b * T + 128], ad[:, b * T:b * T + 128], 0),
                                (R, lambda i, r: yrep[0:r, i, b].rearrange("p n h -> p (n h)"),
                                 adrep[:, b].rearrange("p n h -> p (n h)"), D)):
                            dst = ps[0:m, 2 + b, col:col + D]
                            for i in range(C):
                                r = rows(i)
                                ins = mm(dst, lhs(i, r), w_qkv[l][0:r, i, 2 * D:3 * D], start=i == 0,
                                         stop=i == C - 1 and not lora)
                            if lora:
                                ins = mm(dst, lhs_ad, lora_b[:, 2 * D:3 * D], start=False, stop=True)
                        ins.then_inc(s["v_done"], 1)

                def scores_a(u, i):
                    l, b = PASSES[u]
                    before_ = 5 * u + ORDER[i - 2] if i >= 2 else 5 * (u - 1) + ORDER[i + 2]
                    if i >= 2 or u > FIRST_PASS[l]:
                        pe.wait_ge(s["exp_done"], due(g, "exp_done", before_))
                    c, j = i // 2, 3 * (i % 2)
                    dst = ps[:, i % 2, 0:3 * T]
                    ins = mm(dst, q[:, c, b * T:b * T + 128], kbd[:, c, j:j + 3, b * T:(b + 1) * T],
                             start=True, stop=l > 0)
                    if l == 0:
                        ins = mm(dst, full(ident_bf), mask_a[:, :].unsqueeze(1).to_broadcast([128, 3, T]),
                                 start=False, stop=True)
                    ins.then_inc(s["s_done"], 1)

                def scores_b(u):
                    l, b = PASSES[u]
                    pe.wait_ge(s["qbd_ready"], due(g, "qbd_ready", u + 1))
                    if u > FIRST_PASS[l]:
                        pe.wait_ge(s["o_ready"], due(g, "o_ready", u))
                    for c in range(C):
                        dst = ps[0:R, 3, c * T:(c + 1) * T]
                        ins = mm(dst, qbd[:, u % 2, c].rearrange("p h i -> p (h i)"), k[:, c, b * T:(b + 1) * T],
                                 start=True, stop=l > 0)
                        if l == 0:
                            ins = mm(dst, ident_bf[0:R, 0:R], full(mask_b), start=False, stop=True)
                    ins.then_inc(s["s_done"], 1)

                def transposes_a(u, i):
                    if i == 0:
                        if u:
                            pe.wait_ge(s["pt_act"], due(g, "pt_act", 4 * u))
                    elif i % 2:
                        pe.wait_ge(s["pt_dve"], due(g, "pt_dve", 4 * u + (i + 1) // 2))
                    else:
                        pe.wait_ge(s["pt_act"], due(g, "pt_act", 4 * u + 1))
                    pe.wait_ge(s["exp_done"], due(g, "exp_done", 5 * u + ORDER[i]))
                    for j in range(3):
                        hh = 3 * i + j
                        ins = tr(ps[:, 2, j * 128:(j + 1) * 128], pa[:, u % 2, hh // HC, 0:128, hh % HC], full(ident))
                    ins.then_inc(s["t_done"], 1)

                def transposes_b(u):
                    pe.wait_ge(s["pt_act"], due(g, "pt_act", 4 * u + 2))
                    pe.wait_ge(s["norm_step"], due(g, "norm_step", 4 * u + 3))
                    for c in range(C):
                        tr(ps[:, 2, c * R:(c + 1) * R], pb[:, u % 2, c, 0:128], ident[0:R, 0:R])
                    for c in range(C):
                        ins = tr(ps[0:R, 2, 192 + c * 128:320 + c * 128],
                                 pa[:, u % 2, c, 128:T, :].rearrange("p n h -> p (n h)"), full(ident))
                    ins.then_inc(s["t_done"], 1)

                def transposes_x(u):
                    pe.wait_ge(s["pt_dve"], due(g, "pt_dve", 4 * u + 4))
                    pe.wait_ge(s["norm_step"], due(g, "norm_step", 4 * u + 4))
                    for gg in range(3):
                        tr(ps[:, 2, gg * 128:(gg + 1) * 128],
                           inv_x[:, 4 * gg:4 * gg + 4, :].rearrange("p h r -> p (h r)"), full(ident))
                    pe.wait_ge(s["lb_ready"], due(g, "lb_ready", u + 1))
                    for c in range(C):
                        ins = mm(ps[0:R, 2, 384 + c * TB:384 + (c + 1) * TB], lb[:, c].rearrange("p n h -> p (n h)"),
                                 full(col_i), start=True, stop=True)
                    ins.then_inc(s["t_done"], 1)

                def values(u):
                    l, b = PASSES[u]
                    pe.wait_ge(s["exp_done"], due(g, "exp_done", 5 * u + 5))
                    pe.wait_ge(s["pt_act"], due(g, "pt_act", 4 * u + 3))
                    for gg in range(3):
                        cols = slice(gg * T, (gg + 1) * T)
                        for j in range(4):
                            mm(ps[SL * j:SL * (j + 1), 3, cols], va[:, b, 4 * gg + j, :], pt[:, 4 * gg + j, :],
                               start=True, stop=False)
                        chunks = [c for g_, c in GROUP_CHUNKS if g_ == gg]
                        for c in chunks:
                            first = 4 * gg - 4 * c
                            ins = mm(ps[:, 3, cols], vb[:, b, c, first:first + 4, :].rearrange("p h r -> p (h r)"),
                                     ptk[:, c, :], start=False, stop=c == chunks[-1])
                    ins.then_inc(s["pv_done"], 1)

                for l in range(2):
                    layernorm(l)
                    if l == 1:
                        logits(0)
                        lora_down()
                    projections(l)
                    for n in here("keys", l):
                        unit(n)
                    first, last = FIRST_PASS[l], FIRST_PASS[l + 1]
                    pe.wait_ge(s["q_ready"], due(g, "q_ready", l + 1))
                    pe.wait_ge(s["kbd"], due(g, "kbd", (l + 1) * HC * 16))
                    for u in range(first, last):
                        if u == first:
                            scores_a(u, 0)
                            scores_a(u, 1)
                            pe.wait_ge(s["v_ready"], due(g, "v_ready", 6 * (l + 1)))
                            scores_b(u)
                            for n in here("scores", l):
                                unit(n)
                        transposes_a(u, 0)
                        scores_a(u, 2)
                        for n in here("t0", u):
                            unit(n)
                        transposes_a(u, 1)
                        scores_a(u, 3)
                        for n in here("t1", u):
                            unit(n)
                        transposes_a(u, 2)
                        for n in here("t2", u):
                            unit(n)
                        transposes_a(u, 3)
                        if u + 1 < last:
                            scores_a(u + 1, 0)
                            scores_a(u + 1, 1)
                        for n in here("t3", u):
                            unit(n)
                        transposes_b(u)
                        for n in here("x0", u):
                            unit(n)
                        transposes_x(u)
                        for n in here("x1", u):
                            unit(n)
                        values(u)
                        for n in here("x2", u):
                            unit(n)
                        if u + 1 < last:
                            scores_b(u + 1)
                    pe.wait_ge(s["o_ready"], due(g, "o_ready", last))
                    for c in range(C):
                        for gg in range(3):
                            ins = mm(ps[0:R, c, 0:N], w_out[l][:, gg, c * R:(c + 1) * R], o[:, gg, :],
                                     start=gg == 0, stop=gg == 2)
                    ins.then_inc(s["proj_done"], 1)

                layernorm(2)
                for i in range(NT):
                    if i == 2:
                        pe.wait_ge(s["mix_copied"], due(g, "mix_copied", 1))
                    b0 = 2 * (i % 2)
                    for bank, cols in ((b0, slice(0, 2 * D)), (b0 + 1, slice(2 * D, 3 * D))):
                        for c in range(C):
                            r = rows(c)
                            ins = mm(ps[0:TR, bank, 0:cols.stop - cols.start], y[0:r, c, i * TR:(i + 1) * TR],
                                     w_qkv[2][0:r, c, cols], start=c == 0, stop=c == C - 1)
                    ins.then_inc(s["mix_proj"], 1)
                for i in range(NT):
                    for m in range(4):
                        for n in here(f"mix{m}", i):
                            unit(n)
                    pe.wait_ge(s["mix_out"], due(g, "mix_out", i + 1))
                    if i == 2:
                        pe.wait_ge(s["mix_back"], due(g, "mix_back", 1))
                    for c in range(C):
                        ins = tr(ps[0:R, 2 + i % 2, c * TR:(c + 1) * TR], ot[:, i, c * R:(c + 1) * R],
                                 ident[0:TR, 0:TR])
                    ins.then_inc(s["mix_t"], 1)
                pe.wait_ge(s["mix_back"], due(g, "mix_back", NT))
                for c in range(C):
                    for i in range(C):
                        ins = mm(ps[0:R, c, 0:N], w_out[2][:, i, c * R:(c + 1) * R], o[0:R, i, :], start=i == 0,
                                 stop=i == C - 1)
                ins.then_inc(s["proj_done"], 1)

                layernorm(3)
                logits(1)
                for n in here("gate", 3):
                    unit(n)
                for n in here("rest", 0):
                    unit(n)
                if gf is not None:
                    finish()

            turn(0, None)
            pe.wait_ge(ld_ffn, 32)
            with pe.Fori(1, NG) as g:
                turn(g, g - 1)
            turn(None, NG - 1)


SHIFTS = [(0, 0), (0, -1), (0, 1), (-1, 0), (1, 0)]


def chunked(w):
    return w.reshape(C, R, -1).transpose(1, 0, 2)


def with_bias(w, bias):
    out = np.zeros((R + 1, C, w.shape[1]), w.dtype)
    out[:R] = chunked(w)
    if bias is not None:
        out[R, 0] = bias
    return out


def padded_rows(w):
    out = np.zeros((4, SL, 3, D), w.dtype)
    out[:, :HD] = w.reshape(3, 4, HD, D).transpose(1, 2, 0, 3)
    return out.reshape(128, 3, D)


def layout(i):
    f = {}
    x = i["x"]
    xp = np.zeros((B, 66, 66, 3), x.dtype)
    xp[:, 1:65, 1:65] = x
    win = np.stack([xp[:, 16 * r:16 * r + 18, 16 * c:16 * c + 18] for r in range(4) for c in range(4)], 1)
    f["win"] = win.reshape(NI, NH, HP).transpose(2, 1, 0)
    per_feature = {"wtok": (i["L0_tok_W"], D), "g": (i["L0_tok_gamma"], 1), "be": (i["L0_tok_beta"], 1)}
    for name, (v, n) in per_feature.items():
        v = v.reshape(16, 16, 5, 3, n)
        placed = np.zeros((5, 18, 18, 3, n), v.dtype)
        for sh, (di, dj) in enumerate(SHIFTS):
            placed[sh, 1 + di:17 + di, 1 + dj:17 + dj] = v[:, :, sh]
        f[name] = placed.reshape(5, NH, HP, n).transpose(0, 2, 1, 3)
    f["gtok"] = np.stack([f.pop("g")[..., 0], f.pop("be")[..., 0]], 0).transpose(2, 0, 1, 3)
    occurs = np.zeros((18, 18, 3), np.float32)
    for di, dj in SHIFTS:
        occurs[1 + di:17 + di, 1 + dj:17 + dj] += np.float32(1.0 / (16 * 16 * 15))
    f["mult"] = occurs.reshape(NH, HP).T
    f["btok"] = i["L0_tok_b"].reshape(C, R).T
    txt = np.zeros((B + G, D, TT), i["txt"].dtype)
    txt[:B] = i["txt"].transpose(0, 2, 1)
    f["txt"] = txt.reshape(B + G, C, R, TT).transpose(0, 2, 1, 3)
    wa, ba = i["L0_attn_w_attn"].T, i["L0_attn_b_attn"]
    kqv = lambda v: np.concatenate([v[..., D:2 * D], v[..., 0:D], v[..., 2 * D:]], -1)
    f["w_qkv0"] = with_bias(kqv(wa), kqv(ba))
    f["w_qkv1"] = with_bias(i["L0_ffn_W_qkv"].T, i["L0_ffn_b_qkv"])
    f["w_qkv2"] = with_bias(i["L1_attn_W_attn"].T, None)
    f["w_out0"] = padded_rows(i["L0_attn_w_proj"].T)
    f["w_out1"] = padded_rows(i["L0_ffn_W_proj"].T)
    f["w_out2"] = chunked(i["L1_attn_W_out"].T)
    b_out = np.zeros((3, D), np.float32)
    b_out[0], b_out[1] = i["L0_attn_b_proj"], i["L0_ffn_b_proj"]
    f["b_out"] = b_out.reshape(3, C, R).transpose(2, 0, 1)
    f["lam"] = np.broadcast_to(np.stack([i[f"L1_attn_lambda_{n}"] for n in ("q1", "k1", "q2", "k2")]),
                               (TR, 4, HD // 2))
    f["w_gate"] = np.stack([with_bias(i["L0_ffn_W_gate"].T, i["L0_ffn_b_gate"]),
                            with_bias(i["L1_ffn_w_router"].T, None)], 1)
    f["lora_a"] = chunked(i["L0_ffn_A"].reshape(NE * RANK, D).T)
    f["lora_b"] = i["L0_ffn_B_lora"].transpose(0, 2, 1).reshape(NE * RANK, 3 * D)
    f["e_bias"] = np.broadcast_to(i["L1_ffn_expert_bias"], (TR, NT, NE))
    wide = lambda e, sh: chunked(np.concatenate([e.reshape(NE * FE, D), sh], 0).T)
    f["wgu"] = np.stack([wide(i["L1_ffn_Wg"], i["L1_ffn_sg"]), wide(i["L1_ffn_Wu"], i["L1_ffn_su"])], 1)
    wd = np.concatenate([i["L1_ffn_Wd"].transpose(0, 2, 1).reshape(NE * FE, D), i["L1_ffn_sd"].T], 0)
    f["wdn"] = wd.reshape(NJ, 128, D).transpose(1, 0, 2)
    f["ident"] = np.eye(128, dtype=np.float32)
    causal = np.where(np.arange(T)[None, :] > np.arange(T)[:, None], MASKED, 0.0).astype(np.float32)
    masks = np.zeros((128, 2, T), np.float32)
    masks[:, 0] = causal[:128]
    masks[:R, 1] = np.tile(causal[128:], (HC, 1))
    f["masks"] = masks.reshape(128, 2 * T)
    rows = np.arange(R)
    f["head_q"] = np.equal(rows[:, None] // HD, np.arange(HC)[None, :]).astype(np.float32)
    f["head_k"] = np.equal(rows[:, None] % HC, np.arange(HC)[None, :]).astype(np.float32)
    f["col_i"] = np.equal(rows[:, None] % TB, np.arange(TB)[None, :]).astype(np.float32)
    f["before"] = np.broadcast_to(np.tril(np.ones((NE, NE), np.float32), -1), (TR, NT, NE, NE))
    return {n: np.ascontiguousarray(v) for n, v in f.items()}


def kernel(**inputs):
    import concourse.bacc as bacc
    from concourse.bass_utils import run_bass_kernel_spmd

    nc = bacc.Bacc("TRN2", target_bir_lowering=False, num_devices=1)
    arrays, aps = {}, {}
    for name, v in layout({n: np.asarray(v) for n, v in inputs.items()}).items():
        arrays[f"in_{name}"] = v
        aps[name] = nc.dram_tensor(f"in_{name}", v.shape, mybir.dt.from_np(v.dtype), kind="ExternalInput").ap()
    out = nc.dram_tensor("out", (B, R, C, T), F32, kind="ExternalOutput").ap()
    program(nc, aps, out)
    got = run_bass_kernel_spmd(nc, [arrays], core_ids=[0]).results[0]["out"]
    return got.transpose(0, 3, 2, 1).reshape(B, T, D)
```

```python
import math
from contextlib import ExitStack

import numpy as np

import concourse.bass as bass
from concourse import mybir

F32 = mybir.dt.float32
I32 = mybir.dt.int32
BF16 = mybir.dt.bfloat16
ALU = mybir.AluOpType
ACT = mybir.ActivationFunctionType
X = mybir.AxisListType.X

B, TI, TT, D, H = 16, 16, 128, 192, 12
T = TI + TT
HD = D // H
C, R = 2, 96
HC = H // C
G = 2
NG = B // G
N = G * T
TB = T - 128
SL = 32
NE, FE, RANK = 8, 384, 16
NJ = (NE + 1) * FE // 128
JE = FE // 128
NH = 9
HP = 2 * 18 * 3
NI = B * TI
EPS, EPS_TOK = 1e-5, 1e-3
MAGIC = float(0x5F3759DF)
LAMBDA_INIT = 0.8 - 0.6 * math.exp(-0.3 * 12)
MASKED = -2.0 ** 100

PASSES = [(0, 0), (0, 1), (1, 0), (1, 1)]
QSCALE = [2 * HD ** -0.5, HD ** -0.5, (HD // 2) ** -0.5]
FIRST_PASS = [0, 2, 4]
NT, TR = 3, 96
GROUP_CHUNKS = [(0, 0), (1, 0), (1, 1), (2, 1)]

ORDER, ORDER_B = [1, 2, 4, 5], 3

PER = dict(
    txt_in=32, h_ready=8, mean_done=4, xc_done=4, sq_done=4, var_done=4, rsqrt_step=44, spread_done=4, y_ready=4,
    yrep_ready=4,
    qk_done=4, q_ready=2, k_ready=2, kbd=2 * HC * 16, qbd_ready=4, v_done=4, v_ready=12,
    s_done=20, max_ready=20, exp_done=20, norm_step=16, lb_ready=4, t_done=24, pt_dve=16, pt_act=16,
    pv_done=4, o_ready=4, proj_done=3,
    mix_proj=NT, mix_copied=NT, mix_step=7 * NT, mix_prod=1,
    mix_sub=NT, mix_exp=NT, mix_probs=NT, mix_av=2, mix_out=NT, mix_t=NT, mix_back=NT,
    logits_done=2, gate_sub=2, gate_exp=2, gate_step=24, gate_ready=1, disp_done=1, disp_sb=1, ad_ready=3,
    handed=3, comb_done=8, comb_sb=8, ye_ready=9, gate_up=2 * NJ, tanh_done=NJ, half_done=NJ, hid_done=NJ, down_done=NJ,
    out_ready=1, out_dma=32,
)
UNITS = 3 * NJ + 1
FILL = dict(proj=(1, 0, 0), norm_mean=(5, 2, 2, 1), norm_var=(1, 4, 2, 3), norm_y=(2, 2, 1, 4), start=(3,), gate=(5,),
            kv=(1, 1), keys=(3, 2), scores=(0, 1), t0=(0, 0, 0, 0), t1=(1, 1, 2, 1), t2=(1, 0, 0, 1), t3=(1, 1, 1, 1),
            x0=(1, 1, 1, 0), x1=(0, 0, 0, 1), x2=(1, 1, 1, 1), mix=(0, 0, 5, 0, 3, 1, 3, 1, 0, 0, 0, 2, 3, 2))


def units_at():
    order = [("start", 0)]
    for l in range(4):
        order += [("norm_mean", l), ("norm_var", l), ("norm_y", l)] + [("gate", 0)] * (l == 1)
        if l < 2:
            order += [("kv", l), ("keys", l)]
            for u in range(FIRST_PASS[l], FIRST_PASS[l + 1]):
                order += [("scores", l)] * (u == FIRST_PASS[l])
                order += [(point, u) for point in ("t0", "t1", "t2", "t3", "x0", "x1", "x2")]
        if l == 2:
            order += [("mix", k) for k in range(14)]
        if l < 3:
            order.append(("proj", l))
    where, first = {}, 0
    for point, k in order:
        last = min(UNITS, first + FILL[point][k])
        where[point, k] = range(first, last)
        first = last
    where["rest", 0] = range(first, UNITS)
    return where


UNITS_AT = units_at()
DVE_CENTRED, DVE_LAMBDA = 1, 12
PE_MEAN, PE_VAR, PE_BETA, PE_TOK = 1, 4, (2, 3, 5, 6, 7), 8


def dve_block_used(i):
    return 2 if i == 0 else 2 * i + 1


def program(nc, a, out):
    ctx = ExitStack()
    with ctx:
        def sb(name, shape, dt=F32):
            return ctx.enter_context(nc.sbuf_tensor(name, shape, dt))

        def sem(name):
            return ctx.enter_context(nc.semaphore(name))

        def full(t):
            return t[tuple(slice(None) for _ in t.shape)]

        w_qkv = [sb(f"w_qkv{l}", [R + 1, C, 3 * D]) for l in range(3)]
        w_out = [sb("w_out0", [128, 3, D]), sb("w_out1", [128, 3, D]), sb("w_out2", [R, C, D])]
        b_out = sb("b_out", [R, 3, C])
        w_gate = sb("w_gate", [R + 1, 2, C, NE])
        lora_a = sb("lora_a", [R, C, NE * RANK])
        lora_b = sb("lora_b", [NE * RANK, 3 * D])
        e_bias = sb("e_bias", [TR, NT, NE])
        lam = sb("lam", [TR, 4, HD // 2])
        ident = sb("ident", [128, 128])
        ident_bf = sb("ident_bf", [128, 128], BF16)
        mask_a = sb("mask_a", [128, T], BF16)
        mask_b = sb("mask_b", [R, T], BF16)
        head_q = sb("head_q", [R, HC])
        head_k = sb("head_k", [R, HC])
        col_i = sb("col_i", [R, TB])
        before = sb("before", [TR, NT, NE, NE])
        ones_d = sb("ones_d", [R, R])
        wgu = sb("wgu", [R, 2, C, NJ * 128])
        wdn = sb("wdn", [128, NJ, D])
        coef = sb("coef", [TR, 2 * H])
        img = sb("img", [R, C, NI])

        hin = sb("hin", [R, G, C, TT])
        h = sb("h", [R, C, N])
        xc = sb("xc", [R, C, N])
        y = sb("y", [R + 1, C, N])
        yrep = sb("yrep", [R + 1, C, G, TB, HC])
        var = sb("var", [TR, NT])
        rs = sb("rs", [TR, NT])
        rt = sb("rt", [TR, NT])
        qk = sb("qk", [R, H * H * HD])
        q, k = (qk[:, n * C * N:(n + 1) * C * N].rearrange("p (c n) -> p c n", c=C) for n in range(2))
        qbd = sb("qbd", [R, 2, C, HC, TB])
        va = sb("va", [128, G, H, SL])
        vb = sb("vb", [R, G, C, 8, SL])
        nmax = sb("nmax", [128, 2, H])
        nmax_b = sb("nmax_b", [R, 2, C])
        sums = sb("sums", [128, 2, H])
        sums_b = sb("sums_b", [R, 2, C])
        inv = sb("inv", [128, H])
        inv_b = sb("inv_b", [R, C])
        pb = sb("pb", [R, 2, C, T])
        lb = sb("lb", [R, C, TB, HC])
        inv_x = sb("inv_x", [128, H, SL])
        rbc = sb("rbc", [128, 3, T])
        ptk = sb("ptk", [R, C, T])
        o = sb("o", [128, 3, N])
        mix_m = sb("mix_m", [TR, 2, 2 * H])
        ge = sb("ge", [TR, NT, NE])
        gp = sb("gp", [TR, NT, NE])
        gs = sb("gs", [TR, NT, NE])
        gm = sb("gm", [TR, NT])
        cmp1 = sb("cmp1", [TR, NT, NE, NE])
        cmp2 = sb("cmp2", [TR, NT, NE, NE])
        disp_x = sb("disp_x", [TR, NT, NE, RANK])
        disp_s = sb("disp_s", [128, N])
        ad = sb("ad", [128, N])
        adrep = sb("adrep", [128, G, TB, HC])
        obuf = sb("obuf", [R, C, N])
        sq = o[0:R, 0:C, :]

        work = sb("work", [128, 12096])

        def part(rows, first, pattern=None, **sizes):
            n = math.prod(sizes.values())
            v = work[0:rows, first:first + n]
            names = list(sizes)
            return v.rearrange(f"p ({' '.join(names)}) -> p {' '.join(names)}", **sizes) if len(names) > 1 else v

        win = part(HP, 0, k=NH, n=NI)
        win_sq = part(HP, 2304, k=NH, n=NI)
        wtok = part(HP, 4608, s=2, k=NH, d=D)
        weff = part(HP, 8064, k=NH, d=D)
        wtmp = part(HP, 9792, k=NH, d=D)
        kbd = part(R, 0, c=C, j=HC, n=N)
        comb_bc = part(R, 3456, e=NE, n=N)
        ye = part(R, 5760, s=2, c=C, n=N)
        prod = [part(TR, 6912, n=2304), qk[:, :]]
        ot = part(TR, 9216, t=NT, d=D)
        mix = part(TR, 9792, k=2, s=2, a=H, b=H)
        qkvt = part(TR, 10368, t=NT, n=3, d=D)
        pa = part(128, 6912, s=2, c=C, t=T, j=HC)
        pt = part(128, 10368, h=H, t=T)
        hid = sb("hid", [128, 3, N])
        half = sb("half", [R, 1])
        yf = sb("yf", [R, C, N])
        hf = sb("hf", [R, C, N])
        combf = sb("combf", [TR, NT, NE])
        gtok = sb("gtok", [HP, 2, 5, NH])
        mult = sb("mult", [HP, NH])
        btok = sb("btok", [R, C])
        c0 = sb("c0", [R, C])

        ps = ctx.enter_context(nc.psum_tensor("ps", [128, 8, 512], F32))

        s = {name: sem(name) for name in PER}
        ld_tok, ld_w = sem("ld_tok"), [sem(f"ld_wtok{i}") for i in range(5)]
        ld_small, ld_ffn, ready, stored = sem("ld_small"), sem("ld_ffn"), sem("ready"), sem("stored")
        constants_set = sem("constants_set")
        t_pe, t_dve, t_act = sem("t_pe"), sem("t_dve"), sem("t_act")

        small = [(w_qkv[l], f"w_qkv{l}") for l in range(3)] + [(w_out[l], f"w_out{l}") for l in range(3)]
        small += [(b_out, "b_out"), (w_gate, "w_gate"), (lora_a, "lora_a"), (lora_b, "lora_b"), (e_bias, "e_bias"),
                  (lam, "lam"), (ident, "ident"), (disp_s, "masks"),
                  (head_q, "head_q"), (head_k, "head_k"), (col_i, "col_i"), (before, "before")]
        tok = [(win, "win"), (full(mult), "mult"), (full(gtok), "gtok"), (full(btok), "btok")]

        def due(g, name, n):
            return g * PER[name] + n

        def banks(j, alone):
            return (0, 1) if alone and j % 2 else (4, 5)

        def all_pairs(multiply, i, halves=(0, 1)):
            qh, kh = (qkvt[:, i, n, :].rearrange("p (h d) -> p h d", h=H) for n in range(2))
            half_d = HD // 2
            size = H * H * half_d
            for n in halves:
                d = slice(n * half_d, (n + 1) * half_d)
                shape = [TR, H, H, half_d]
                ins = multiply(prod[i % 2][:, n * size:(n + 1) * size].rearrange("p (a b d) -> p a b d", a=H, b=H),
                               qh[:, :, d].unsqueeze(2).to_broadcast(shape),
                               kh[:, :, d].unsqueeze(1).to_broadcast(shape), ALU.mult)
            return ins

        def all_values(multiply, i):
            vh = qkvt[:, i, 2, :].rearrange("p (h d) -> p h d", h=H)
            shape = [TR, H, HD, H]
            return multiply(prod[i % 2].rearrange("p (a d b) -> p a d b", a=H, d=HD),
                            mix[:, i % 2, 0].unsqueeze(2).to_broadcast(shape),
                            vh.rearrange("p h d -> p d h").unsqueeze(1).to_broadcast(shape), ALU.mult)

        block = ctx.enter_context(nc.Block())

        @block.sync
        def _(sp):
            for t, n in tok:
                sp.dma_start(t, a[n]).then_inc(ld_tok, 16)
            for i in range(5):
                if i >= 2:
                    sp.wait_ge(t_dve, dve_block_used(i - 2))
                    sp.wait_ge(t_pe, PE_BETA[i - 2])
                sp.dma_start(wtok[:, i % 2], a["wtok"][i]).then_inc(ld_w[i], 16)
            for t, n in small:
                sp.dma_start(full(t), a[n]).then_inc(ld_small, 16)
            sp.dma_start(full(wgu), a["wgu"]).then_inc(ld_ffn, 16)
            sp.dma_start(full(wdn), a["wdn"]).then_inc(ld_ffn, 16)
            sp.wait_ge(ready, 1)

            def keys(g):
                for l in range(2):
                    sp.wait_ge(s["k_ready"], due(g, "k_ready", l + 1))
                    for j in range(HC):
                        rows = slice(HD * j, HD * (j + 1))
                        sp.dma_start(kbd[rows, :, j, :], k[rows, :, :]).then_inc(s["kbd"], 16)

            def store(g):
                sp.wait_ge(s["out_ready"], due(g, "out_ready", 2))
                for b in range(G):
                    sp.dma_start(out[bass.ds(g * G + b, 1)].rearrange("o r c n -> (o r) c n"),
                                 obuf[:, :, b * T:(b + 1) * T]).then_inc(s["out_dma"], 16)
                sp.wait_ge(s["out_dma"], due(g, "out_dma", PER["out_dma"]))
                sp.sem_inc(stored, 1)

            keys(0)
            with sp.Fori(1, NG) as g:
                keys(g)
                store(g - 1)
            store(NG - 1)

        @block.gpsimd
        def _(pool):
            def load_text(g):
                for b in range(G):
                    pool.dma_start(hin[:, b], a["txt"][bass.ds(g * G + b, 1)].rearrange("o r c n -> (o r) c n"))\
                        .then_inc(s["txt_in"], 16)

            nc.gpsimd.memset(full(va), 0.0)
            nc.gpsimd.memset(full(vb), 0.0)
            nc.gpsimd.memset(rbc[:, :, 128:T], 1.0)
            nc.gpsimd.memset(full(y), 1.0)
            nc.gpsimd.memset(full(ones_d), 1.0 / D)
            nc.gpsimd.memset(full(half), 0.5).then_inc(constants_set, 1)
            load_text(0)
            pool.wait_ge(t_pe, PE_TOK)
            nc.gpsimd.memset(kbd, 0.0).then_inc(ready, 1)
            pool.wait_ge(ld_small, 16 * len(small))

            def turn(g, gf):

                def expert_input(e):
                    if e >= 2:
                        pool.wait_ge(s["gate_up"], due(gf, "gate_up", 2 * JE * (e - 1)))
                    if e == 0:
                        pool.wait_ge(s["handed"], due(gf, "handed", 1))
                        for c in range(C):
                            ins = nc.gpsimd.tensor_tensor(ye[:, e % 2, c], yf[:, c], half[:, :].to_broadcast([R, N]),
                                                          ALU.mult)
                    else:
                        pool.wait_ge(s["comb_sb"], due(gf, "comb_sb", e))
                        for c in range(C):
                            ins = nc.gpsimd.tensor_tensor(ye[:, e % 2, c], yf[:, c], comb_bc[:, e - 1], ALU.mult)
                    ins.then_inc(s["ye_ready"], 1)

                def unit(n):
                    if n % (3 * JE) == 0 and n // (3 * JE) < NE:
                        expert_input(n // (3 * JE) + 1)

                if gf is not None:
                    expert_input(0)

                def here(point, k):
                    return UNITS_AT[point, k] if gf is not None else ()

                if g is None:
                    for n in range(UNITS):
                        unit(n)
                    return
                for n in here("start", 0):
                    unit(n)
                def queries_b(u):
                    l, b = PASSES[u]
                    pool.wait_ge(s["q_ready"], due(g, "q_ready", l + 1))
                    if u >= 2:
                        pool.wait_ge(s["s_done"], due(g, "s_done", 5 * (u - 1)))
                    for c in range(C):
                        ins = nc.gpsimd.tensor_tensor(
                            qbd[:, u % 2, c], q[:, c, b * T + 128:(b + 1) * T].unsqueeze(1).to_broadcast([R, HC, TB]),
                            head_q[:, :].unsqueeze(2).to_broadcast([R, HC, TB]), ALU.mult)
                    ins.then_inc(s["qbd_ready"], 1)

                def probs_b(u):
                    pool.wait_ge(s["norm_step"], due(g, "norm_step", 4 * u + 3))
                    for c in range(C):
                        ins = nc.gpsimd.tensor_tensor(
                            lb[:, c], pb[:, u % 2, c, 128:T].unsqueeze(2).to_broadcast([R, TB, HC]),
                            head_q[:, :].unsqueeze(1).to_broadcast([R, TB, HC]), ALU.mult)
                    ins.then_inc(s["lb_ready"], 1)

                def head_products():
                    pool.wait_ge(s["mix_copied"], due(g, "mix_copied", 2))
                    all_pairs(nc.gpsimd.tensor_tensor, 1).then_inc(s["mix_prod"], 1)

                def head_values(i):
                    pool.wait_ge(s["mix_probs"], due(g, "mix_probs", i + 1))
                    all_values(nc.gpsimd.tensor_tensor, i).then_inc(s["mix_av"], 1)

                for l in range(2):
                    for n in here("norm_mean", l):
                        unit(n)
                    for n in here("norm_var", l):
                        unit(n)
                    for n in here("norm_y", l):
                        unit(n)
                    if l == 1:
                        for n in here("gate", 0):
                            unit(n)
                    for n in here("kv", l):
                        unit(n)
                    for n in here("keys", l):
                        unit(n)
                    first, last = FIRST_PASS[l], FIRST_PASS[l + 1]
                    queries_b(first)
                    if l == 0:
                        pool.wait_ge(s["h_ready"], due(g, "h_ready", 2))
                        load_text(g + 1)
                    for u in range(first, last):
                        if u == first:
                            for n in here("scores", l):
                                unit(n)
                        for n in here("t0", u):
                            unit(n)
                        for n in here("t1", u):
                            unit(n)
                        for n in here("t2", u):
                            unit(n)
                        if u + 1 < last:
                            queries_b(u + 1)
                        for n in here("t3", u):
                            unit(n)
                        for n in here("x0", u):
                            unit(n)
                        probs_b(u)
                        for n in here("x1", u):
                            unit(n)
                        for n in here("x2", u):
                            unit(n)
                    for n in here("proj", l):
                        unit(n)
                for l in (2, 3):
                    for point in ("norm_mean", "norm_var", "norm_y"):
                        for n in here(point, l):
                            unit(n)
                    if l == 2:
                        head_products()
                        for m in range(5):
                            for n in here("mix", m):
                                unit(n)
                        head_values(0)
                        for n in here("mix", 5):
                            unit(n)
                        head_values(1)
                        for m in range(6, 14):
                            for n in here("mix", m):
                                unit(n)
                        for n in here("proj", 2):
                            unit(n)
                for n in here("rest", 0):
                    unit(n)

            turn(0, None)
            with pool.Fori(1, NG) as g:
                turn(g, g - 1)
            turn(None, NG - 1)

        @block.scalar
        def _(act):
            fn = nc.scalar.activation
            act.wait_ge(t_dve, DVE_CENTRED)
            fn(win_sq, win, ACT.Square).then_inc(t_act, 1)
            act.wait_ge(t_dve, DVE_LAMBDA)
            fn(gm[:, 0:2], gm[:, 0:2], ACT.Exp).then_inc(t_act, 1)

            def turn(g, gf):
                alone = g is None

                def spread_weights(experts):
                    for e in experts:
                        act.wait_ge(s["comb_done"], due(gf, "comb_done", e + 1))
                        nc.scalar.copy(comb_bc[:, e], ps[0:R, e % 2, 0:N]).then_inc(s["comb_sb"], 1)

                def unit(n):
                    j = n // 3
                    if n % 3 != 1:
                        return
                    act.wait_ge(s["gate_up"], due(gf, "gate_up", 2 * j + 1))
                    if j >= 3:
                        act.wait_ge(s["down_done"], due(gf, "down_done", j - 2))
                    fn(hid[:, j % 3], ps[:, banks(j, alone)[0], 0:N], ACT.Tanh, scale=0.5)\
                        .then_inc(s["tanh_done"], 1)

                def here(point, k):
                    return UNITS_AT[point, k] if gf is not None else ()

                if alone:
                    spread_weights(range(NE))
                    for n in range(UNITS):
                        unit(n)
                    return
                for n in here("start", 0):
                    unit(n)

                def square(l):
                    act.wait_ge(s["xc_done"], due(g, "xc_done", l + 1))
                    fn(sq, full(xc), ACT.Square).then_inc(s["sq_done"], 1)
                    spread = l == 0 and gf is not None
                    if spread:
                        spread_weights((0, 1))
                    for n in here("norm_mean", l):
                        unit(n)
                    if spread:
                        spread_weights((2, 3, 4, 5))
                    for n in here("norm_var", l):
                        unit(n)
                    if spread:
                        spread_weights((6, 7))
                    for n in here("norm_y", l):
                        unit(n)

                def gate_exp(n):
                    act.wait_ge(s["gate_sub"], due(g, "gate_sub", n + 1))
                    fn(full(ge), full(ge), ACT.Exp).then_inc(s["gate_exp"], 1)

                def exp_a(u, i):
                    act.wait_ge(s["max_ready"], due(g, "max_ready", 5 * u + ORDER[i]))
                    if i == 0 and u >= 2:
                        act.wait_ge(s["t_done"], due(g, "t_done", 6 * (u - 1)))
                    for hh in range(3 * i, 3 * i + 3):
                        ins = fn(pa[:, u % 2, hh // HC, :, hh % HC], ps[:, i % 2, (hh % 3) * T:(hh % 3 + 1) * T],
                                 ACT.Exp, bias=nmax[:, u % 2, hh:hh + 1], accum_out=sums[:, u % 2, hh:hh + 1])
                    ins.then_inc(s["exp_done"], 1)

                def exp_b(u):
                    act.wait_ge(s["max_ready"], due(g, "max_ready", 5 * u + ORDER_B))
                    for c in range(C):
                        ins = fn(pb[:, u % 2, c, :], ps[0:R, 3, c * T:(c + 1) * T], ACT.Exp,
                                 bias=nmax_b[:, u % 2, c:c + 1], accum_out=sums_b[:, u % 2, c:c + 1])
                    ins.then_inc(s["exp_done"], 1)

                def transposed(u, i):
                    act.wait_ge(s["t_done"], due(g, "t_done", 6 * u + i + 1))
                    nc.scalar.copy(pt[:, 3 * i:3 * i + 3, 0:128], ps[:, 2, 0:384].rearrange("p (h n) -> p h n", h=3))\
                        .then_inc(s["pt_act"], 1)

                for l in range(2):
                    square(l)
                    if l == 1:
                        gate_exp(0)
                        for n in here("gate", 0):
                            unit(n)
                        act.wait_ge(s["disp_done"], due(g, "disp_done", 1))
                        nc.scalar.copy(full(disp_s), ps[:, 3, 32:32 + N]).then_inc(s["disp_sb"], 1)
                    act.wait_ge(s["qk_done"], due(g, "qk_done", 2 * l + 1))
                    nc.scalar.mul(q, ps[0:R, 0:2, 0:N], QSCALE[l]).then_inc(s["q_ready"], 1)
                    for n in here("kv", l):
                        unit(n)
                    for n in here("keys", l):
                        unit(n)
                    first, last = FIRST_PASS[l], FIRST_PASS[l + 1]
                    for u in range(first, last):
                        if u == first:
                            exp_a(u, 0)
                            exp_a(u, 1)
                            exp_b(u)
                            for n in here("scores", l):
                                unit(n)
                        exp_a(u, 2)
                        for n in here("t0", u):
                            unit(n)
                        transposed(u, 1)
                        exp_a(u, 3)
                        for n in here("t1", u):
                            unit(n)
                        for n in here("t2", u):
                            unit(n)
                        transposed(u, 3)
                        if u + 1 < last:
                            exp_a(u + 1, 0)
                            exp_a(u + 1, 1)
                        for n in here("t3", u):
                            unit(n)
                        for n in here("x0", u):
                            unit(n)
                        act.wait_ge(s["t_done"], due(g, "t_done", 6 * u + 6))
                        nc.scalar.copy(ptk[:, :, 128:T], ps[0:R, 2, 384:416].rearrange("p (c n) -> p c n", c=C))\
                            .then_inc(s["pt_act"], 1)
                        nc.scalar.copy(rbc[:, :, 0:128], ps[:, 2, 0:384].rearrange("p (g n) -> p g n", g=3))\
                            .then_inc(s["pt_act"], 1)
                        for n in here("x1", u):
                            unit(n)
                        for n in here("x2", u):
                            unit(n)
                        if u + 1 < last:
                            exp_b(u + 1)
                    for n in here("proj", l):
                        unit(n)
                square(2)
                for i in range(NT):
                    act.wait_ge(s["mix_proj"], due(g, "mix_proj", i + 1))
                    b0 = 2 * (i % 2)
                    nc.scalar.mul(qkvt[:, i, 0, :], ps[0:TR, b0, 0:D], QSCALE[2])
                    nc.scalar.copy(qkvt[:, i, 1, :], ps[0:TR, b0, D:2 * D])
                    nc.scalar.copy(qkvt[:, i, 2, :], ps[0:TR, b0 + 1, 0:D]).then_inc(s["mix_copied"], 1)

                def exp_mix(i):
                    act.wait_ge(s["mix_sub"], due(g, "mix_sub", i + 1))
                    fn(mix[:, i % 2], mix[:, i % 2], ACT.Exp).then_inc(s["mix_exp"], 1)

                def mixed(i):
                    act.wait_ge(s["mix_t"], due(g, "mix_t", i + 1))
                    nc.scalar.copy(o[0:R, 0:C, i * TR:(i + 1) * TR],
                                   ps[0:R, 2 + i % 2, 0:C * TR].rearrange("p (c n) -> p c n", c=C))\
                        .then_inc(s["mix_back"], 1)

                for m in range(0, 3):
                    for n in here("mix", m):
                        unit(n)
                exp_mix(0)
                for m in range(3, 5):
                    for n in here("mix", m):
                        unit(n)
                exp_mix(1)
                for m in range(5, 9):
                    for n in here("mix", m):
                        unit(n)
                mixed(0)
                for n in here("mix", 9):
                    unit(n)
                exp_mix(2)
                for m in range(10, 13):
                    for n in here("mix", m):
                        unit(n)
                mixed(1)
                for n in here("mix", 13):
                    unit(n)
                mixed(2)
                for n in here("proj", 2):
                    unit(n)
                square(3)
                for n in here("rest", 0):
                    unit(n)
                gate_exp(1)

            turn(0, None)
            with act.Fori(1, NG) as g:
                turn(g, g - 1)
            turn(None, NG - 1)

        @block.vector
        def _(dve):
            tt, ts, stt = nc.vector.tensor_tensor, nc.vector.tensor_scalar, nc.vector.scalar_tensor_tensor
            cp, red, rec = nc.vector.tensor_copy, nc.vector.tensor_reduce, nc.vector.reciprocal
            count = [0]

            def link(ins):
                count[0] += 1
                ins.then_inc(t_dve, 1)
                dve.wait_ge(t_dve, count[0])

            def rsqrt(src, eps, v, r, t, mark):
                mark(ts(v, src, eps, None, ALU.add))
                mark(ts(r.bitcast(I32), v.bitcast(I32), -0.5, MAGIC, ALU.mult, ALU.add))
                for _ in range(3):
                    mark(stt(t, r, -0.5, r, ALU.mult, ALU.mult))
                    mark(tt(t, t, v, ALU.mult))
                    mark(stt(r, t, 1.5, r, ALU.add, ALU.mult))

            dve.wait_ge(ld_tok, 16 * len(tok))
            dve.wait_ge(t_pe, PE_MEAN)
            link(tt(win, win, ps[0:HP, 0, 0:NI].unsqueeze(1).to_broadcast([HP, NH, NI]), ALU.subtract))
            assert count[0] == DVE_CENTRED
            for i in range(5):
                dve.wait_ge(ld_w[i], 16)
                gamma = gtok[:, 0, i, :].unsqueeze(2).to_broadcast([HP, NH, D])
                link(tt(weff if i == 0 else wtmp, wtok[:, i % 2], gamma, ALU.mult))
                assert count[0] == dve_block_used(i)
                if i:
                    link(tt(weff, weff, wtmp, ALU.add))
            dve.wait_ge(ld_small, 16 * len(small))
            link(tt(cmp1[:, 0, 0:2, :], lam[:, 0:4:2, :], lam[:, 1:4:2, :], ALU.mult))
            link(red(gm[:, 0:2], cmp1[:, 0, 0:2, :], X, ALU.add))
            assert count[0] == DVE_LAMBDA
            dve.wait_ge(t_act, 2)
            link(tt(gm[:, 2:3], gm[:, 0:1], gm[:, 1:2], ALU.subtract))
            link(ts(coef[:, H:2 * H], gm[:, 2:3].to_broadcast([TR, H]), LAMBDA_INIT, -(1.0 - LAMBDA_INIT),
                    ALU.add, ALU.mult))
            link(nc.vector.memset(coef[:, 0:H], 1.0 - LAMBDA_INIT))
            link(cp(full(ident_bf), full(ident)))
            link(cp(full(mask_a), disp_s[:, 0:T]))
            link(cp(full(mask_b), disp_s[0:R, T:2 * T]))
            dve.wait_ge(t_pe, PE_VAR)
            rsqrt(ps[0:R, 1, 0:NI], EPS_TOK, q[:, 0, 0:NI], q[:, 1, 0:NI], k[:, 0, 0:NI], link)
            dve.wait_ge(t_pe, PE_BETA[4])
            link(tt(c0[:, :].unsqueeze(2), ps[0:R, 2:4, 0:1], btok[:, :].unsqueeze(2), ALU.add))
            dve.wait_ge(t_pe, PE_TOK)
            link(tt(full(img), ps[0:R, 4:6, 0:NI], q[:, 1, 0:NI].unsqueeze(1).to_broadcast([R, C, NI]), ALU.mult))
            for c in range(C):
                link(ts(img[:, c, :], img[:, c, :], c0[:, c:c + 1], None, ALU.add))
            dve.wait_ge(constants_set, 1)
            dve.sem_inc(s["out_ready"], 1)

            def turn(g, gf):
                alone = g is None
                steps = {"rsqrt_step": 0, "norm_step": 0, "gate_step": 0, "mix_step": 0}

                def stepper(name):
                    def mark(ins):
                        steps[name] += 1
                        ins.then_inc(s[name], 1)
                        dve.wait_ge(s[name], due(g, name, steps[name]))
                    return mark

                def hand_over():
                    cp(full(yf), y[0:R]).then_inc(s["handed"], 1)
                    cp(full(hf), full(h)).then_inc(s["handed"], 1)
                    dve.wait_ge(s["handed"], due(g, "handed", 2))

                def unit(n):
                    j = n // 3
                    if n % 3 < 2:
                        return
                    gate, up = banks(j, alone)
                    dve.wait_ge(s["tanh_done"], due(gf, "tanh_done", j + 1))
                    stt(hid[:, j % 3], hid[:, j % 3], 1.0, ps[:, gate, 0:N], ALU.add, ALU.mult)\
                        .then_inc(s["half_done"], 1)
                    dve.wait_ge(s["half_done"], due(gf, "half_done", j + 1))
                    dve.wait_ge(s["gate_up"], due(gf, "gate_up", 2 * j + 2))
                    tt(hid[:, j % 3], hid[:, j % 3], ps[:, up, 0:N], ALU.mult).then_inc(s["hid_done"], 1)

                def finish():
                    dve.wait_ge(s["down_done"], due(gf, "down_done", NJ))
                    if alone:
                        dve.wait_ge(s["out_dma"], due(gf, "out_dma", 0))
                    tt(full(obuf), ps[0:R, 6:8, 0:N], full(hf), ALU.add).then_inc(s["out_ready"], 1)
                    dve.wait_ge(s["out_ready"], due(gf, "out_ready", 2))

                def here(point, k):
                    return UNITS_AT[point, k] if gf is not None else ()

                if alone:
                    for n in range(UNITS):
                        unit(n)
                    finish()
                    return

                def layernorm(l):
                    dve.wait_ge(s["h_ready"], due(g, "h_ready", 2 * l + 2))
                    dve.wait_ge(s["mean_done"], due(g, "mean_done", l + 1))
                    tt(full(xc), full(h), ps[0:R, 3, 0:N].unsqueeze(1).to_broadcast([R, C, N]), ALU.subtract)\
                        .then_inc(s["xc_done"], 1)
                    for n in here("norm_mean", l):
                        unit(n)
                    dve.wait_ge(s["var_done"], due(g, "var_done", l + 1))
                    rsqrt(ps[0:TR, 2, 0:NT], EPS, full(var), full(rs), full(rt), stepper("rsqrt_step"))
                    for n in here("norm_var", l):
                        unit(n)
                    dve.wait_ge(s["spread_done"], due(g, "spread_done", l + 1))
                    dve.wait_ge(s["xc_done"], due(g, "xc_done", l + 1))
                    tt(y[0:R], full(xc), ps[0:R, 2, R:R + N].unsqueeze(1).to_broadcast([R, C, N]), ALU.mult)\
                        .then_inc(s["y_ready"], 1)
                    dve.wait_ge(s["y_ready"], due(g, "y_ready", l + 1))
                    for c in range(C if l < 2 else 0):
                        yb = y[:, c, :].rearrange("p (b n) -> p b n", b=G)[:, :, 128:T]
                        cp(yrep[:, c], yb.unsqueeze(3).to_broadcast([R + 1, G, TB, HC])).then_inc(s["yrep_ready"], 1)
                    for n in here("norm_y", l):
                        unit(n)

                def top2(n):
                    mark = stepper("gate_step")
                    dve.wait_ge(s["logits_done"], due(g, "logits_done", n + 1))
                    lg = ps[0:TR, 3, 0:NT * NE].rearrange("p (t e) -> p t e", e=NE)
                    spread = gm[:, :].unsqueeze(2).to_broadcast([TR, NT, NE])
                    mark(red(full(gm), lg, X, ALU.max))
                    tt(full(ge), lg, spread, ALU.subtract).then_inc(s["gate_sub"], 1)
                    dve.wait_ge(s["gate_exp"], due(g, "gate_exp", n + 1))
                    mark(red(full(gm), full(ge), X, ALU.add))
                    mark(rec(full(gm), full(gm)))
                    mark(tt(full(gp), full(ge), spread, ALU.mult))
                    if n == 1:
                        mark(tt(full(gs), full(gp), full(e_bias), ALU.add))
                    sel = gp if n == 0 else gs
                    other = sel[:, :, :].unsqueeze(2).to_broadcast([TR, NT, NE, NE])
                    own = sel[:, :, :].unsqueeze(3).to_broadcast([TR, NT, NE, NE])
                    mark(tt(full(cmp1), other, own, ALU.is_gt))
                    mark(tt(full(cmp2), other, own, ALU.is_equal))
                    mark(tt(full(cmp2), full(cmp2), full(before), ALU.mult))
                    mark(tt(full(cmp1), full(cmp1), full(cmp2), ALU.add))
                    mark(red(full(gs), full(cmp1), X, ALU.add))
                    mark(stt(full(gs), full(gs), 2.0, full(gp), ALU.is_lt, ALU.mult))
                    return mark

                def maxima_a(u, i):
                    dve.wait_ge(s["s_done"], due(g, "s_done", 5 * u + ORDER[i]))
                    red(nmax[:, u % 2, 3 * i:3 * i + 3], ps[:, i % 2, 0:3 * T].rearrange("p (j n) -> p j n", j=3), X,
                        ALU.max, negate=True).then_inc(s["max_ready"], 1)

                def maxima_b(u):
                    dve.wait_ge(s["s_done"], due(g, "s_done", 5 * u + ORDER_B))
                    red(nmax_b[:, u % 2, :], ps[0:R, 3, 0:C * T].rearrange("p (c n) -> p c n", c=C), X, ALU.max,
                        negate=True).then_inc(s["max_ready"], 1)

                def normalise(u):
                    mark = stepper("norm_step")
                    dve.wait_ge(s["exp_done"], due(g, "exp_done", 5 * u + 5))
                    mark(rec(full(inv), sums[:, u % 2, :]))
                    mark(rec(full(inv_b), sums_b[:, u % 2, :]))
                    for c in range(C):
                        p = pb[:, u % 2, c, :]
                        ins = ts(p, p, inv_b[:, c:c + 1], None, ALU.mult)
                    mark(ins)
                    mark(cp(full(inv_x), inv[:, :].unsqueeze(2).to_broadcast([128, H, SL])))

                def transposed_a(u, i):
                    dve.wait_ge(s["t_done"], due(g, "t_done", 6 * u + i + 1))
                    cp(pt[:, 3 * i:3 * i + 3, 0:128], ps[:, 2, 0:384].rearrange("p (h n) -> p h n", h=3))\
                        .then_inc(s["pt_dve"], 1)

                def transposed_b(u):
                    dve.wait_ge(s["t_done"], due(g, "t_done", 6 * u + 5))
                    cp(pt[:, :, 128:T], ps[:, 2, 0:H * TB].rearrange("p (h i) -> p h i", h=H)).then_inc(s["pt_dve"], 1)
                    cp(ptk[:, :, 0:128], ps[0:R, 2, 192:448].rearrange("p (c n) -> p c n", c=C))\
                        .then_inc(s["pt_dve"], 1)

                def output(u):
                    _, b = PASSES[u]
                    dve.wait_ge(s["pv_done"], due(g, "pv_done", u + 1))
                    dve.wait_ge(s["pt_act"], due(g, "pt_act", 4 * u + 4))
                    tt(o[:, :, b * T:(b + 1) * T], ps[:, 3, 0:3 * T].rearrange("p (g n) -> p g n", g=3), full(rbc),
                       ALU.mult).then_inc(s["o_ready"], 1)

                def residual(l):
                    dve.wait_ge(s["proj_done"], due(g, "proj_done", l + 1))
                    for c in range(C):
                        stt(h[:, c, :], ps[0:R, c, 0:N], b_out[:, l, c:c + 1], h[:, c, :], ALU.add, ALU.add)\
                            .then_inc(s["h_ready"], 1)

                def mix_scores(i, point):
                    rows = mix[:, i % 2].rearrange("p n a b -> p (n a) b")
                    mark_mix(red(mix[:, i % 2].rearrange("p n a b -> p (n a b)"),
                                 prod[i % 2].rearrange("p (a d) -> p a d", d=HD // 2), X, ALU.add))
                    for n in here("mix", point):
                        unit(n)
                    mark_mix(red(mix_m[:, i % 2], rows, X, ALU.max))
                    tt(rows, rows, mix_m[:, i % 2].unsqueeze(2).to_broadcast([TR, 2 * H, H]), ALU.subtract)\
                        .then_inc(s["mix_sub"], 1)

                def mix_softmax(i):
                    rows = mix[:, i % 2].rearrange("p n a b -> p (n a) b")
                    m = mix_m[:, i % 2]
                    dve.wait_ge(s["mix_exp"], due(g, "mix_exp", i + 1))
                    mark_mix(red(m, rows, X, ALU.add))
                    mark_mix(rec(m, m))
                    mark_mix(tt(m, m, full(coef), ALU.mult))
                    mark_mix(tt(rows, rows, m.unsqueeze(2).to_broadcast([TR, 2 * H, H]), ALU.mult))
                    tt(mix[:, i % 2, 0], mix[:, i % 2, 0], mix[:, i % 2, 1], ALU.add).then_inc(s["mix_probs"], 1)

                def mix_output(i):
                    red(ot[:, i, :], prod[i % 2].rearrange("p (a b) -> p a b", b=H), X, ALU.add)\
                        .then_inc(s["mix_out"], 1)

                dve.wait_ge(s["txt_in"], due(g, "txt_in", 32))
                hv = h[:, :, :].rearrange("p c (b n) -> p c b n", b=G)
                cp(hv[:, :, :, TI:T], hin[:, :, :, :].rearrange("p b c n -> p c b n")).then_inc(s["h_ready"], 1)
                cp(hv[:, :, :, 0:TI], img[:, :, bass.ds(g * (G * TI), G * TI)].rearrange("p c (b n) -> p c b n", b=G))\
                    .then_inc(s["h_ready"], 1)
                for n in here("start", 0):
                    unit(n)
                for l in range(2):
                    layernorm(l)
                    if l == 1:
                        mark = top2(0)
                        for n in here("gate", 0):
                            unit(n)
                        ts(full(disp_x), gs[:, :, :].unsqueeze(3).to_broadcast([TR, NT, NE, RANK]), 2.0, None,
                           ALU.mult).then_inc(s["gate_ready"], 1)
                        dve.wait_ge(s["disp_sb"], due(g, "disp_sb", 1))
                        tt(full(ad), full(disp_s), ps[:, 2, 0:N], ALU.mult).then_inc(s["ad_ready"], 1)
                        dve.wait_ge(s["ad_ready"], due(g, "ad_ready", 1))
                        for b in range(G):
                            cp(adrep[:, b], ad[:, b * T + 128:(b + 1) * T].unsqueeze(2).to_broadcast([128, TB, HC]))\
                                .then_inc(s["ad_ready"], 1)
                    dve.wait_ge(s["qk_done"], due(g, "qk_done", 2 * l + 2))
                    cp(k, ps[0:R, 2:4, 0:N]).then_inc(s["k_ready"], 1)
                    for n in here("kv", l):
                        unit(n)
                    for b in range(G):
                        dve.wait_ge(s["v_done"], due(g, "v_done", 2 * l + b + 1))
                        cp(va[:, b, :, 0:HD], ps[:, 2 + b, 0:D].rearrange("p (h d) -> p h d", h=H))\
                            .then_inc(s["v_ready"], 1)
                        for c in range(C):
                            tt(vb[:, b, c, 2 * c:2 * c + HC, 0:HD],
                               ps[0:R, 2 + b, D + c * R:D + (c + 1) * R].rearrange("p (h d) -> p h d", h=HC),
                               head_k[:, :].unsqueeze(2).to_broadcast([R, HC, HD]), ALU.mult).then_inc(s["v_ready"], 1)
                    for n in here("keys", l):
                        unit(n)
                    first, last = FIRST_PASS[l], FIRST_PASS[l + 1]
                    for u in range(first, last):
                        if u == first:
                            maxima_a(u, 0)
                            maxima_a(u, 1)
                            maxima_b(u)
                            for n in here("scores", l):
                                unit(n)
                        transposed_a(u, 0)
                        maxima_a(u, 2)
                        for n in here("t0", u):
                            unit(n)
                        maxima_a(u, 3)
                        for n in here("t1", u):
                            unit(n)
                        transposed_a(u, 2)
                        normalise(u)
                        for n in here("t2", u):
                            unit(n)
                        if u + 1 < last:
                            maxima_a(u + 1, 0)
                            maxima_a(u + 1, 1)
                        for n in here("t3", u):
                            unit(n)
                        transposed_b(u)
                        for n in here("x0", u):
                            unit(n)
                        for n in here("x1", u):
                            unit(n)
                        output(u)
                        for n in here("x2", u):
                            unit(n)
                        if u + 1 < last:
                            maxima_b(u + 1)
                    residual(l)
                    for n in here("proj", l):
                        unit(n)
                layernorm(2)
                mark_mix = stepper("mix_step")
                dve.wait_ge(s["mix_copied"], due(g, "mix_copied", 1))
                all_pairs(tt, 0, [0])
                for n in here("mix", 0):
                    unit(n)
                mark_mix(all_pairs(tt, 0, [1]))
                for n in here("mix", 1):
                    unit(n)
                mix_scores(0, 2)
                for n in here("mix", 3):
                    unit(n)
                dve.wait_ge(s["mix_prod"], due(g, "mix_prod", 1))
                mix_scores(1, 4)
                mix_softmax(0)
                for n in here("mix", 5):
                    unit(n)
                mix_softmax(1)
                for n in here("mix", 6):
                    unit(n)
                dve.wait_ge(s["mix_av"], due(g, "mix_av", 1))
                mix_output(0)
                for n in here("mix", 7):
                    unit(n)
                dve.wait_ge(s["mix_copied"], due(g, "mix_copied", 3))
                dve.wait_ge(s["mix_out"], due(g, "mix_out", 1))
                mark_mix(all_pairs(tt, 2))
                for n in here("mix", 8):
                    unit(n)
                mix_scores(2, 9)
                for n in here("mix", 10):
                    unit(n)
                dve.wait_ge(s["mix_av"], due(g, "mix_av", 2))
                mix_output(1)
                for n in here("mix", 11):
                    unit(n)
                mix_softmax(2)
                dve.wait_ge(s["mix_probs"], due(g, "mix_probs", 3))
                mark_mix(all_values(tt, 2))
                for n in here("mix", 12):
                    unit(n)
                mix_output(2)
                for n in here("mix", 13):
                    unit(n)
                residual(2)
                for n in here("proj", 2):
                    unit(n)
                layernorm(3)
                for n in here("rest", 0):
                    unit(n)
                if gf is not None:
                    finish()
                hand_over()
                mark = top2(1)
                mark(red(full(gm), full(gs), X, ALU.add))
                mark(ts(full(gm), full(gm), 1e-9, 2.0, ALU.add, ALU.mult))
                mark(rec(full(gm), full(gm)))
                tt(full(combf), full(gs), gm[:, :].unsqueeze(2).to_broadcast([TR, NT, NE]), ALU.mult)\
                    .then_inc(s["handed"], 1)
                assert steps == {x: PER[x] for x in steps}, steps

            turn(0, None)
            with dve.Fori(1, NG) as g:
                turn(g, g - 1)
            turn(None, NG - 1)

        @block.tensor
        def _(pe):
            mm, tr = nc.tensor.matmul, nc.tensor.transpose
            pe.wait_ge(ld_tok, 16 * len(tok))
            for i in range(NH):
                ins = mm(ps[0:HP, 0, 0:NI], mult[:, i:i + 1].to_broadcast([HP, HP]), win[:, i], start=i == 0,
                         stop=i == NH - 1)
            ins.then_inc(t_pe, 1)
            for i in range(5):
                if i == 2:
                    pe.wait_ge(t_act, 1)
                    for kk in range(NH):
                        ins = mm(ps[0:HP, 1, 0:NI], mult[:, kk:kk + 1].to_broadcast([HP, HP]), win_sq[:, kk],
                                 start=kk == 0, stop=kk == NH - 1)
                    ins.then_inc(t_pe, 1)
                pe.wait_ge(ld_w[i], 16)
                for kk in range(NH):
                    for c in range(C):
                        ins = mm(ps[0:R, 2 + c, 0:1], wtok[:, i % 2, kk, c * R:(c + 1) * R], gtok[:, 1, i, kk:kk + 1],
                                 start=i == kk == 0, stop=i == 4 and kk == NH - 1)
                ins.then_inc(t_pe, 1)
            pe.wait_ge(t_dve, dve_block_used(4) + 1)
            for c in range(C):
                for kk in range(NH):
                    ins = mm(ps[0:R, 4 + c, 0:NI], weff[:, kk, c * R:(c + 1) * R], win[:, kk], start=kk == 0,
                             stop=kk == NH - 1)
            ins.then_inc(t_pe, 1)
            pe.wait_ge(constants_set, 1)
            pe.wait_ge(ld_small, 16 * len(small))

            def turn(g, gf):
                alone = g is None

                def expert_weights(experts):
                    pe.wait_ge(s["handed"], due(gf, "handed", 3))
                    for e in experts:
                        if e >= 2:
                            pe.wait_ge(s["comb_sb"], due(gf, "comb_sb", e - 1))
                        for i in range(NT):
                            ins = tr(ps[0:R, e % 2, i * TR:(i + 1) * TR],
                                     combf[:, i, e:e + 1].to_broadcast([TR, R]), ident[0:TR, 0:TR])
                        ins.then_inc(s["comb_done"], 1)
                    if NE - 1 in experts:
                        pe.wait_ge(s["comb_sb"], due(gf, "comb_sb", NE))

                def hidden(j, n):
                    e = j // JE
                    former = j - 1 if alone else j
                    if j == n == 0:
                        pe.wait_ge(s["handed"], due(gf, "handed", 1))
                    if n == 0 and former > 0:
                        pe.wait_ge(s["hid_done"], due(gf, "hid_done", former))
                    if n == 1 and j % JE == 0:
                        pe.wait_ge(s["ye_ready"], due(gf, "ye_ready", e + 1))
                    for c in range(C):
                        ins = mm(ps[:, banks(j, alone)[n], 0:N], wgu[:, n, c, j * 128:(j + 1) * 128],
                                 yf[:, c, :] if n == 0 else ye[:, e % 2, c, :], start=c == 0, stop=c == C - 1)
                    ins.then_inc(s["gate_up"], 1)

                def down(j):
                    pe.wait_ge(s["hid_done"], due(gf, "hid_done", j + 1))
                    if j == 0:
                        pe.wait_ge(s["out_ready"], due(gf, "out_ready", 1))
                    for c in range(C):
                        ins = mm(ps[0:R, 6 + c, 0:N], wdn[:, j, c * R:(c + 1) * R], hid[:, j % 3], start=j == 0,
                                 stop=j == NJ - 1)
                    ins.then_inc(s["down_done"], 1)

                def unit(n):
                    if n == 3 * NJ:
                        down(NJ - 1)
                    elif n % 3 < 2:
                        hidden(n // 3, n % 3)
                    elif n > 2:
                        down(n // 3 - 1)

                def here(point, k):
                    return UNITS_AT[point, k] if gf is not None else ()

                if alone:
                    expert_weights(range(NE))
                    for n in range(UNITS):
                        unit(n)
                    return
                for n in here("start", 0):
                    unit(n)

                def layernorm(l):
                    pe.wait_ge(s["h_ready"], due(g, "h_ready", 2 * l + 2))
                    for c in range(C):
                        ins = mm(ps[0:R, 3, 0:N], full(ones_d), h[:, c, :], start=c == 0, stop=c == C - 1)
                    ins.then_inc(s["mean_done"], 1)
                    spread = l == 0 and gf is not None
                    if spread:
                        expert_weights((0, 1))
                    for n in here("norm_mean", l):
                        unit(n)
                    if spread:
                        expert_weights((2, 3))
                    pe.wait_ge(s["sq_done"], due(g, "sq_done", l + 1))
                    for i in range(NT):
                        for c in range(C):
                            ins = mm(ps[0:TR, 2, i:i + 1], sq[:, c, i * TR:(i + 1) * TR], ones_d[:, 0:1],
                                     start=c == 0, stop=c == C - 1)
                    ins.then_inc(s["var_done"], 1)
                    if spread:
                        expert_weights((4, 5))
                    for n in here("norm_var", l):
                        unit(n)
                    if spread:
                        expert_weights((6, 7))
                    pe.wait_ge(s["rsqrt_step"], due(g, "rsqrt_step", 11 * (l + 1)))
                    for i in range(NT):
                        ins = tr(ps[0:R, 2, R + i * TR:R + (i + 1) * TR], rs[:, i:i + 1].to_broadcast([TR, R]),
                                 ident[0:TR, 0:TR])
                    ins.then_inc(s["spread_done"], 1)
                    for n in here("norm_y", l):
                        unit(n)
                    pe.wait_ge(s["y_ready"], due(g, "y_ready", l + 1))

                def rows(c):
                    return R + 1 if c == 0 else R

                def logits(n):
                    for i in range(NT):
                        for c in range(C):
                            r = rows(c)
                            ins = mm(ps[0:TR, 3, i * NE:(i + 1) * NE], y[0:r, c, i * TR:(i + 1) * TR],
                                     w_gate[0:r, n, c, :], start=c == 0, stop=c == C - 1)
                    ins.then_inc(s["logits_done"], 1)

                def lora_down():
                    for c in range(C):
                        mm(ps[:, 2, 0:N], lora_a[:, c, :], y[0:R, c, :], start=c == 0, stop=c == C - 1)
                    for n in here("gate", 0):
                        unit(n)
                    pe.wait_ge(s["gate_ready"], due(g, "gate_ready", 1))
                    for i in range(NT):
                        ins = tr(ps[:, 3, 32 + i * TR:32 + (i + 1) * TR],
                                 disp_x[:, i, :, :].rearrange("p e r -> p (e r)"), ident[0:TR, 0:TR])
                    ins.then_inc(s["disp_done"], 1)
                    pe.wait_ge(s["ad_ready"], due(g, "ad_ready", 3))

                def projections(l):
                    lora = l == 1
                    for n in range(2):
                        for c in range(C):
                            cols = slice(n * D + c * R, n * D + (c + 1) * R)
                            for i in range(C):
                                r = rows(i)
                                ins = mm(ps[0:R, 2 * n + c, 0:N], w_qkv[l][0:r, i, cols], y[0:r, i, :], start=i == 0,
                                         stop=i == C - 1 and not lora)
                            if lora:
                                ins = mm(ps[0:R, 2 * n + c, 0:N], lora_b[:, cols], full(ad), start=False, stop=True)
                        ins.then_inc(s["qk_done"], 1)
                    for n in here("kv", l):
                        unit(n)
                    pe.wait_ge(s["yrep_ready"], due(g, "yrep_ready", 2 * l + 2))
                    pe.wait_ge(s["k_ready"], due(g, "k_ready", l + 1))
                    for b in range(G):
                        for m, lhs, lhs_ad, col in (
                                (128, lambda i, r: y[0:r, i, b * T:b * T + 128], ad[:, b * T:b * T + 128], 0),
                                (R, lambda i, r: yrep[0:r, i, b].rearrange("p n h -> p (n h)"),
                                 adrep[:, b].rearrange("p n h -> p (n h)"), D)):
                            dst = ps[0:m, 2 + b, col:col + D]
                            for i in range(C):
                                r = rows(i)
                                ins = mm(dst, lhs(i, r), w_qkv[l][0:r, i, 2 * D:3 * D], start=i == 0,
                                         stop=i == C - 1 and not lora)
                            if lora:
                                ins = mm(dst, lhs_ad, lora_b[:, 2 * D:3 * D], start=False, stop=True)
                        ins.then_inc(s["v_done"], 1)

                def scores_a(u, i):
                    l, b = PASSES[u]
                    before_ = 5 * u + ORDER[i - 2] if i >= 2 else 5 * (u - 1) + ORDER[i + 2]
                    if i >= 2 or u > FIRST_PASS[l]:
                        pe.wait_ge(s["exp_done"], due(g, "exp_done", before_))
                    c, j = i // 2, 3 * (i % 2)
                    dst = ps[:, i % 2, 0:3 * T]
                    ins = mm(dst, q[:, c, b * T:b * T + 128], kbd[:, c, j:j + 3, b * T:(b + 1) * T],
                             start=True, stop=l > 0)
                    if l == 0:
                        ins = mm(dst, full(ident_bf), mask_a[:, :].unsqueeze(1).to_broadcast([128, 3, T]),
                                 start=False, stop=True)
                    ins.then_inc(s["s_done"], 1)

                def scores_b(u):
                    l, b = PASSES[u]
                    pe.wait_ge(s["qbd_ready"], due(g, "qbd_ready", u + 1))
                    if u > FIRST_PASS[l]:
                        pe.wait_ge(s["o_ready"], due(g, "o_ready", u))
                    for c in range(C):
                        dst = ps[0:R, 3, c * T:(c + 1) * T]
                        ins = mm(dst, qbd[:, u % 2, c].rearrange("p h i -> p (h i)"), k[:, c, b * T:(b + 1) * T],
                                 start=True, stop=l > 0)
                        if l == 0:
                            ins = mm(dst, ident_bf[0:R, 0:R], full(mask_b), start=False, stop=True)
                    ins.then_inc(s["s_done"], 1)

                def transposes_a(u, i):
                    if i == 0:
                        if u:
                            pe.wait_ge(s["pt_act"], due(g, "pt_act", 4 * u))
                    elif i % 2:
                        pe.wait_ge(s["pt_dve"], due(g, "pt_dve", 4 * u + (i + 1) // 2))
                    else:
                        pe.wait_ge(s["pt_act"], due(g, "pt_act", 4 * u + 1))
                    pe.wait_ge(s["exp_done"], due(g, "exp_done", 5 * u + ORDER[i]))
                    for j in range(3):
                        hh = 3 * i + j
                        ins = tr(ps[:, 2, j * 128:(j + 1) * 128], pa[:, u % 2, hh // HC, 0:128, hh % HC], full(ident))
                    ins.then_inc(s["t_done"], 1)

                def transposes_b(u):
                    pe.wait_ge(s["pt_act"], due(g, "pt_act", 4 * u + 2))
                    pe.wait_ge(s["norm_step"], due(g, "norm_step", 4 * u + 3))
                    for c in range(C):
                        tr(ps[:, 2, c * R:(c + 1) * R], pb[:, u % 2, c, 0:128], ident[0:R, 0:R])
                    for c in range(C):
                        ins = tr(ps[0:R, 2, 192 + c * 128:320 + c * 128],
                                 pa[:, u % 2, c, 128:T, :].rearrange("p n h -> p (n h)"), full(ident))
                    ins.then_inc(s["t_done"], 1)

                def transposes_x(u):
                    pe.wait_ge(s["pt_dve"], due(g, "pt_dve", 4 * u + 4))
                    pe.wait_ge(s["norm_step"], due(g, "norm_step", 4 * u + 4))
                    for gg in range(3):
                        tr(ps[:, 2, gg * 128:(gg + 1) * 128],
                           inv_x[:, 4 * gg:4 * gg + 4, :].rearrange("p h r -> p (h r)"), full(ident))
                    pe.wait_ge(s["lb_ready"], due(g, "lb_ready", u + 1))
                    for c in range(C):
                        ins = mm(ps[0:R, 2, 384 + c * TB:384 + (c + 1) * TB], lb[:, c].rearrange("p n h -> p (n h)"),
                                 full(col_i), start=True, stop=True)
                    ins.then_inc(s["t_done"], 1)

                def values(u):
                    l, b = PASSES[u]
                    pe.wait_ge(s["exp_done"], due(g, "exp_done", 5 * u + 5))
                    pe.wait_ge(s["pt_act"], due(g, "pt_act", 4 * u + 3))
                    for gg in range(3):
                        cols = slice(gg * T, (gg + 1) * T)
                        for j in range(4):
                            mm(ps[SL * j:SL * (j + 1), 3, cols], va[:, b, 4 * gg + j, :], pt[:, 4 * gg + j, :],
                               start=True, stop=False)
                        chunks = [c for g_, c in GROUP_CHUNKS if g_ == gg]
                        for c in chunks:
                            first = 4 * gg - 4 * c
                            ins = mm(ps[:, 3, cols], vb[:, b, c, first:first + 4, :].rearrange("p h r -> p (h r)"),
                                     ptk[:, c, :], start=False, stop=c == chunks[-1])
                    ins.then_inc(s["pv_done"], 1)

                for l in range(2):
                    layernorm(l)
                    if l == 1:
                        logits(0)
                        lora_down()
                    projections(l)
                    for n in here("keys", l):
                        unit(n)
                    first, last = FIRST_PASS[l], FIRST_PASS[l + 1]
                    pe.wait_ge(s["q_ready"], due(g, "q_ready", l + 1))
                    pe.wait_ge(s["kbd"], due(g, "kbd", (l + 1) * HC * 16))
                    for u in range(first, last):
                        if u == first:
                            scores_a(u, 0)
                            scores_a(u, 1)
                            pe.wait_ge(s["v_ready"], due(g, "v_ready", 6 * (l + 1)))
                            scores_b(u)
                            for n in here("scores", l):
                                unit(n)
                        transposes_a(u, 0)
                        scores_a(u, 2)
                        for n in here("t0", u):
                            unit(n)
                        transposes_a(u, 1)
                        scores_a(u, 3)
                        for n in here("t1", u):
                            unit(n)
                        transposes_a(u, 2)
                        for n in here("t2", u):
                            unit(n)
                        transposes_a(u, 3)
                        if u + 1 < last:
                            scores_a(u + 1, 0)
                            scores_a(u + 1, 1)
                        for n in here("t3", u):
                            unit(n)
                        transposes_b(u)
                        for n in here("x0", u):
                            unit(n)
                        transposes_x(u)
                        for n in here("x1", u):
                            unit(n)
                        values(u)
                        for n in here("x2", u):
                            unit(n)
                        if u + 1 < last:
                            scores_b(u + 1)
                    pe.wait_ge(s["o_ready"], due(g, "o_ready", last))
                    for c in range(C):
                        for gg in range(3):
                            ins = mm(ps[0:R, c, 0:N], w_out[l][:, gg, c * R:(c + 1) * R], o[:, gg, :],
                                     start=gg == 0, stop=gg == 2)
                    ins.then_inc(s["proj_done"], 1)
                    for n in here("proj", l):
                        unit(n)

                layernorm(2)
                for i in range(NT):
                    if i == 2:
                        pe.wait_ge(s["mix_copied"], due(g, "mix_copied", 1))
                    b0 = 2 * (i % 2)
                    for bank, cols in ((b0, slice(0, 2 * D)), (b0 + 1, slice(2 * D, 3 * D))):
                        for c in range(C):
                            r = rows(c)
                            ins = mm(ps[0:TR, bank, 0:cols.stop - cols.start], y[0:r, c, i * TR:(i + 1) * TR],
                                     w_qkv[2][0:r, c, cols], start=c == 0, stop=c == C - 1)
                    ins.then_inc(s["mix_proj"], 1)

                def mix_transposes(i):
                    pe.wait_ge(s["mix_out"], due(g, "mix_out", i + 1))
                    if i == 2:
                        pe.wait_ge(s["mix_back"], due(g, "mix_back", 1))
                    for c in range(C):
                        ins = tr(ps[0:R, 2 + i % 2, c * TR:(c + 1) * TR], ot[:, i, c * R:(c + 1) * R],
                                 ident[0:TR, 0:TR])
                    ins.then_inc(s["mix_t"], 1)

                for m in range(0, 9):
                    for n in here("mix", m):
                        unit(n)
                mix_transposes(0)
                for m in range(9, 13):
                    for n in here("mix", m):
                        unit(n)
                mix_transposes(1)
                for n in here("mix", 13):
                    unit(n)
                mix_transposes(2)
                pe.wait_ge(s["mix_back"], due(g, "mix_back", NT))
                for c in range(C):
                    for i in range(C):
                        ins = mm(ps[0:R, c, 0:N], w_out[2][:, i, c * R:(c + 1) * R], o[0:R, i, :], start=i == 0,
                                 stop=i == C - 1)
                ins.then_inc(s["proj_done"], 1)
                for n in here("proj", 2):
                    unit(n)

                layernorm(3)
                for n in here("rest", 0):
                    unit(n)
                logits(1)

            turn(0, None)
            pe.wait_ge(ld_ffn, 32)
            with pe.Fori(1, NG) as g:
                turn(g, g - 1)
            turn(None, NG - 1)


SHIFTS = [(0, 0), (0, -1), (0, 1), (-1, 0), (1, 0)]


def chunked(w):
    return w.reshape(C, R, -1).transpose(1, 0, 2)


def with_bias(w, bias):
    out = np.zeros((R + 1, C, w.shape[1]), w.dtype)
    out[:R] = chunked(w)
    if bias is not None:
        out[R, 0] = bias
    return out


def padded_rows(w):
    out = np.zeros((4, SL, 3, D), w.dtype)
    out[:, :HD] = w.reshape(3, 4, HD, D).transpose(1, 2, 0, 3)
    return out.reshape(128, 3, D)


def layout(i):
    f = {}
    x = i["x"]
    xp = np.zeros((B, 66, 66, 3), x.dtype)
    xp[:, 1:65, 1:65] = x
    win = np.stack([xp[:, 16 * r:16 * r + 18, 16 * c:16 * c + 18] for r in range(4) for c in range(4)], 1)
    f["win"] = win.reshape(NI, NH, HP).transpose(2, 1, 0)
    per_feature = {"wtok": (i["L0_tok_W"], D), "g": (i["L0_tok_gamma"], 1), "be": (i["L0_tok_beta"], 1)}
    for name, (v, n) in per_feature.items():
        v = v.reshape(16, 16, 5, 3, n)
        placed = np.zeros((5, 18, 18, 3, n), v.dtype)
        for sh, (di, dj) in enumerate(SHIFTS):
            placed[sh, 1 + di:17 + di, 1 + dj:17 + dj] = v[:, :, sh]
        f[name] = placed.reshape(5, NH, HP, n).transpose(0, 2, 1, 3)
    f["gtok"] = np.stack([f.pop("g")[..., 0], f.pop("be")[..., 0]], 0).transpose(2, 0, 1, 3)
    occurs = np.zeros((18, 18, 3), np.float32)
    for di, dj in SHIFTS:
        occurs[1 + di:17 + di, 1 + dj:17 + dj] += np.float32(1.0 / (16 * 16 * 15))
    f["mult"] = occurs.reshape(NH, HP).T
    f["btok"] = i["L0_tok_b"].reshape(C, R).T
    txt = np.zeros((B + G, D, TT), i["txt"].dtype)
    txt[:B] = i["txt"].transpose(0, 2, 1)
    f["txt"] = txt.reshape(B + G, C, R, TT).transpose(0, 2, 1, 3)
    wa, ba = i["L0_attn_w_attn"].T, i["L0_attn_b_attn"]
    kqv = lambda v: np.concatenate([v[..., D:2 * D], v[..., 0:D], v[..., 2 * D:]], -1)
    f["w_qkv0"] = with_bias(kqv(wa), kqv(ba))
    f["w_qkv1"] = with_bias(i["L0_ffn_W_qkv"].T, i["L0_ffn_b_qkv"])
    f["w_qkv2"] = with_bias(i["L1_attn_W_attn"].T, None)
    f["w_out0"] = padded_rows(i["L0_attn_w_proj"].T)
    f["w_out1"] = padded_rows(i["L0_ffn_W_proj"].T)
    f["w_out2"] = chunked(i["L1_attn_W_out"].T)
    b_out = np.zeros((3, D), np.float32)
    b_out[0], b_out[1] = i["L0_attn_b_proj"], i["L0_ffn_b_proj"]
    f["b_out"] = b_out.reshape(3, C, R).transpose(2, 0, 1)
    f["lam"] = np.broadcast_to(np.stack([i[f"L1_attn_lambda_{n}"] for n in ("q1", "k1", "q2", "k2")]),
                               (TR, 4, HD // 2))
    f["w_gate"] = np.stack([with_bias(i["L0_ffn_W_gate"].T, i["L0_ffn_b_gate"]),
                            with_bias(i["L1_ffn_w_router"].T, None)], 1)
    f["lora_a"] = chunked(i["L0_ffn_A"].reshape(NE * RANK, D).T)
    f["lora_b"] = i["L0_ffn_B_lora"].transpose(0, 2, 1).reshape(NE * RANK, 3 * D)
    f["e_bias"] = np.broadcast_to(i["L1_ffn_expert_bias"], (TR, NT, NE))
    wide = lambda e, sh: chunked(np.concatenate([sh, e.reshape(NE * FE, D)], 0).T)
    f["wgu"] = np.stack([wide(i["L1_ffn_Wg"], i["L1_ffn_sg"]), wide(i["L1_ffn_Wu"], i["L1_ffn_su"])], 1)
    wd = np.concatenate([i["L1_ffn_sd"].T, i["L1_ffn_Wd"].transpose(0, 2, 1).reshape(NE * FE, D)], 0)
    f["wdn"] = wd.reshape(NJ, 128, D).transpose(1, 0, 2)
    f["ident"] = np.eye(128, dtype=np.float32)
    causal = np.where(np.arange(T)[None, :] > np.arange(T)[:, None], MASKED, 0.0).astype(np.float32)
    masks = np.zeros((128, 2, T), np.float32)
    masks[:, 0] = causal[:128]
    masks[:R, 1] = np.tile(causal[128:], (HC, 1))
    f["masks"] = masks.reshape(128, 2 * T)
    rows = np.arange(R)
    f["head_q"] = np.equal(rows[:, None] // HD, np.arange(HC)[None, :]).astype(np.float32)
    f["head_k"] = np.equal(rows[:, None] % HC, np.arange(HC)[None, :]).astype(np.float32)
    f["col_i"] = np.equal(rows[:, None] % TB, np.arange(TB)[None, :]).astype(np.float32)
    f["before"] = np.broadcast_to(np.tril(np.ones((NE, NE), np.float32), -1), (TR, NT, NE, NE))
    return {n: np.ascontiguousarray(v) for n, v in f.items()}


def kernel(**inputs):
    import concourse.bacc as bacc
    from concourse.bass_utils import run_bass_kernel_spmd

    nc = bacc.Bacc("TRN2", target_bir_lowering=False, num_devices=1)
    arrays, aps = {}, {}
    for name, v in layout({n: np.asarray(v) for n, v in inputs.items()}).items():
        arrays[f"in_{name}"] = v
        aps[name] = nc.dram_tensor(f"in_{name}", v.shape, mybir.dt.from_np(v.dtype), kind="ExternalInput").ap()
    out = nc.dram_tensor("out", (B, R, C, T), F32, kind="ExternalOutput").ap()
    program(nc, aps, out)
    got = run_bass_kernel_spmd(nc, [arrays], core_ids=[0]).results[0]["out"]
    return got.transpose(0, 3, 2, 1).reshape(B, T, D)
```
